# Optimizing a Trainium2 kernel written in Bass

```python
import numpy as np
import jax
import jax.numpy as jnp

def _softmax(x, axis=-1):
    return jax.nn.softmax(x, axis=axis)

def _gelu(x):
    return jax.nn.gelu(x, approximate=True)

def _silu(x):
    return jax.nn.silu(x)

def _sigmoid(x):
    return jax.nn.sigmoid(x)

def _layernorm(x, axis=-1, eps=1e-05):
    m = jnp.mean(x, axis=axis, keepdims=True)
    v = jnp.var(x, axis=axis, keepdims=True)
    return (x - m) / jnp.sqrt(v + eps)

def _scatter_add(tgt, idx, src, axis=0):
    return tgt.at[idx].add(src)

def _segment_sum(src, seg, n):
    return jax.ops.segment_sum(src, seg, n)
kernel_name = 'mk_flamingo_gated_d2_seqx_r2_5686af'

def setup_inputs(seed: int=0):
    np.random.seed(seed)
    _w = jnp.asarray

    def _rec_inputs():
        import jax
        import jax.numpy as jnp
        _rk = jax.random.key(seed)
        x = -0.0002928 + 1 * jax.random.normal(jax.random.fold_in(_rk, 1), (4, 1024, 512), jnp.float32)
        _lenS = 1024 - jax.random.randint(jax.random.fold_in(_rk, 7), (4,), 0, max(1, 1024 // 4) + 1, jnp.int32)
        _lenS2 = 64 - jax.random.randint(jax.random.fold_in(_rk, 8), (4,), 0, max(1, 64 // 4) + 1, jnp.int32)
        _ctx_1024P = jax.random.normal(jax.random.fold_in(_rk, 11), (4, 16, 512), jnp.float32)
        _ctx_1024c = jax.random.dirichlet(jax.random.fold_in(_rk, 511), 0.3 * jnp.ones((16,), jnp.float32), (4, 64))
        _ctx_1024t = jnp.einsum('bsk,bkd->bsd', _ctx_1024c, _ctx_1024P)
        _ctx_1024t = _ctx_1024t * jax.lax.rsqrt(jnp.mean(jnp.square(_ctx_1024t)) + 1e-12) * 0.953939
        ctx_1024 = -1.39393e-06 + 0.999914 * (_ctx_1024t + 0.3 * jax.random.normal(jax.random.fold_in(_rk, 611), (4, 64, 512), jnp.float32))
        _g = jax.random.normal(jax.random.fold_in(_rk, 9001), (2, 2), jnp.float32)
        _g = jnp.sign(_g) * jnp.maximum(jnp.abs(_g), 1.0) + (_g == 0) * 1.0
        g_xattn = _g[0]
        g_ffn = _g[1]
        return (x, ctx_1024, g_xattn, g_ffn)
    x, ctx_1024, g_xattn, g_ffn = _rec_inputs()

    def _L0_xattn_setup():
        import jax, jax.numpy as jnp
        import numpy as np
        B, S, D, H = (2, 1024, 512, 16)
        HD = D // H
        SCALE = HD ** (-0.5)
        NEG = -1000000000.0
        key = jax.random.key(seed)
        ks = jax.random.split(key, 7)
        w_std = 1.0 / np.sqrt(D)
        return {'query': jax.random.normal(ks[0], (B, S, D), dtype=jnp.float32), 'key': jax.random.normal(ks[1], (B, S, D), dtype=jnp.float32), 'value': jax.random.normal(ks[2], (B, S, D), dtype=jnp.float32), 'Wq': jax.random.normal(ks[3], (D, D), dtype=jnp.float32) * w_std, 'Wk': jax.random.normal(ks[4], (D, D), dtype=jnp.float32) * w_std, 'Wv': jax.random.normal(ks[5], (D, D), dtype=jnp.float32) * w_std, 'Wo': jax.random.normal(ks[6], (D, D), dtype=jnp.float32) * w_std}
    _L0_xattn_all = _L0_xattn_setup()
    _L0_xattn_in = {k: v for k, v in _L0_xattn_all.items() if k in ('Wq', 'Wk', 'Wv', 'Wo')}
    del _L0_xattn_all

    def _L0_ffn_setup():
        import jax, jax.numpy as jnp
        import numpy as np
        D_MODEL = 512
        HIDDEN = 2048
        N_ROUTING = 2
        key = jax.random.key(seed)
        ks = jax.random.split(key, 10)
        s = 0.02
        x = jax.random.normal(ks[0], (4, 2048, D_MODEL), dtype=jnp.float32)
        gate_w = jax.random.normal(ks[1], (N_ROUTING, D_MODEL), dtype=jnp.float32) * s
        w1 = jax.random.normal(ks[2], (N_ROUTING, D_MODEL, HIDDEN), dtype=jnp.float32) * s
        b1 = jax.random.normal(ks[3], (N_ROUTING, HIDDEN), dtype=jnp.float32) * s
        w2 = jax.random.normal(ks[4], (N_ROUTING, HIDDEN, D_MODEL), dtype=jnp.float32) * s
        b2 = jax.random.normal(ks[5], (N_ROUTING, D_MODEL), dtype=jnp.float32) * s
        sw1 = jax.random.normal(ks[6], (D_MODEL, HIDDEN), dtype=jnp.float32) * s
        sb1 = jax.random.normal(ks[7], (HIDDEN,), dtype=jnp.float32) * s
        sw2 = jax.random.normal(ks[8], (HIDDEN, D_MODEL), dtype=jnp.float32) * s
        sb2 = jax.random.normal(ks[9], (D_MODEL,), dtype=jnp.float32) * s
        return {'x': x, 'gate_w': gate_w, 'w1': w1, 'b1': b1, 'w2': w2, 'b2': b2, 'sw1': sw1, 'sb1': sb1, 'sw2': sw2, 'sb2': sb2}
    _L0_ffn_all = _L0_ffn_setup()
    _L0_ffn_in = {k: v for k, v in _L0_ffn_all.items() if k in ('gate_w', 'w1', 'b1', 'w2', 'b2', 'sw1', 'sb1', 'sw2', 'sb2')}
    del _L0_ffn_all

    def _L1_xattn_setup():
        import jax, jax.numpy as jnp
        import numpy as np
        HIDDEN = 512
        NUM_HEADS = 16
        HEAD_DIM = HIDDEN // NUM_HEADS
        key = jax.random.key(seed)
        ks = jax.random.split(key, 10)
        B, T, S = (2, 1024, 1024)
        sc = 1.0 / np.sqrt(HIDDEN)
        inp = {'tgt': jax.random.normal(ks[0], (B, T, HIDDEN), jnp.float32), 'src': jax.random.normal(ks[1], (B, S, HIDDEN), jnp.float32), 'Wq': jax.random.normal(ks[2], (NUM_HEADS, HIDDEN, HEAD_DIM), jnp.float32) * sc, 'bq': jnp.zeros((NUM_HEADS, HEAD_DIM), jnp.float32), 'Wk': jax.random.normal(ks[3], (NUM_HEADS, HIDDEN, HEAD_DIM), jnp.float32) * sc, 'bk': jnp.zeros((NUM_HEADS, HEAD_DIM), jnp.float32), 'Wv': jax.random.normal(ks[4], (NUM_HEADS, HIDDEN, HEAD_DIM), jnp.float32) * sc, 'bv': jnp.zeros((NUM_HEADS, HEAD_DIM), jnp.float32), 'Wo': jax.random.normal(ks[5], (HIDDEN, HIDDEN), jnp.float32) * sc, 'bo': jnp.zeros((HIDDEN,), jnp.float32)}
        return inp
    _L1_xattn_all = _L1_xattn_setup()
    _L1_xattn_in = {k: v for k, v in _L1_xattn_all.items() if k in ('Wq', 'bq', 'Wk', 'bk', 'Wv', 'bv', 'Wo', 'bo')}
    del _L1_xattn_all

    def _L1_ffn_setup():
        import jax, jax.numpy as jnp
        import numpy as np
        S, B, D, H, DH = (2048, 8, 512, 16, 64)

        def _forward(x, Wg, Wq, bq, Wkv, bkv, Wo, bo, ln_g, ln_b):
            s_len, bsz, d_model = x.shape
            n_head, _, d_head = Wq.shape
            cap = s_len // n_head
            scale = 1.0 / d_head ** 0.5
            h = jnp.transpose(x, (1, 0, 2))
            t = h
            probs = jax.nn.softmax(h @ Wg, axis=-1)
            scores = jnp.transpose(probs, (0, 2, 1))
            _, idx = jax.lax.top_k(scores, cap)
            idx = jnp.sort(idx, axis=-1)
            hg = jnp.take_along_axis(h[:, None, :, :], idx[..., None], axis=2)
            hg = jnp.transpose(hg, (1, 0, 2, 3))
            q = jnp.einsum('hbcd,hde->hbce', hg, Wq) + bq[:, None, None, :]
            kv = jnp.einsum('hbcd,hde->hbce', hg, Wkv) + bkv[:, None, None, :]
            k, v = jnp.split(kv, 2, axis=-1)
            att = jnp.einsum('hbid,hbjd->hbij', q, k) * scale
            p = jax.nn.softmax(att, axis=1)
            av = jnp.einsum('hbij,hbjd->hbid', p, v)
            ao = jnp.einsum('hbid,hde->hbie', av, Wo) + bo
            tok = jnp.transpose(idx, (1, 0, 2))
            b_ids = jnp.arange(bsz)[None, :, None]
            outs = jnp.zeros_like(t).at[b_ids, tok].add(ao)
            y = t + outs
            mu = jnp.mean(y, axis=-1, keepdims=True)
            var = jnp.var(y, axis=-1, keepdims=True)
            yn = (y - mu) * jax.lax.rsqrt(var + 1e-05) * ln_g + ln_b
            return jnp.transpose(yn, (1, 0, 2))
        key = jax.random.key(seed)
        ks = jax.random.split(key, 6)
        s = 0.02
        return {'x': jax.random.normal(ks[0], (S, B, D), jnp.float32), 'attn_mask': jnp.zeros((S, S), jnp.bool_), 'Wg': jax.random.normal(ks[1], (D, H), jnp.float32) * s, 'Wq': jax.random.normal(ks[2], (H, D, DH), jnp.float32) * s, 'bq': jnp.zeros((H, DH), jnp.float32), 'Wkv': jax.random.normal(ks[3], (H, D, 2 * DH), jnp.float32) * s, 'bkv': jnp.zeros((H, 2 * DH), jnp.float32), 'Wo': jax.random.normal(ks[4], (H, DH, D), jnp.float32) * s, 'bo': jnp.zeros((D,), jnp.float32), 'ln_g': jnp.ones((D,), jnp.float32), 'ln_b': jnp.zeros((D,), jnp.float32)}
    _L1_ffn_all = _L1_ffn_setup()
    _L1_ffn_in = {k: v for k, v in _L1_ffn_all.items() if k in ('attn_mask', 'Wg', 'Wq', 'bq', 'Wkv', 'bkv', 'Wo', 'bo', 'ln_g', 'ln_b')}
    del _L1_ffn_all
    return {'x': x, 'ctx_1024': ctx_1024, 'g_xattn': g_xattn, 'g_ffn': g_ffn, 'L0_xattn_Wq': _L0_xattn_in['Wq'], 'L0_xattn_Wk': _L0_xattn_in['Wk'], 'L0_xattn_Wv': _L0_xattn_in['Wv'], 'L0_xattn_Wo': _L0_xattn_in['Wo'], 'L0_ffn_gate_w': _L0_ffn_in['gate_w'], 'L0_ffn_w1': _L0_ffn_in['w1'], 'L0_ffn_b1': _L0_ffn_in['b1'], 'L0_ffn_w2': _L0_ffn_in['w2'], 'L0_ffn_b2': _L0_ffn_in['b2'], 'L0_ffn_sw1': _L0_ffn_in['sw1'], 'L0_ffn_sb1': _L0_ffn_in['sb1'], 'L0_ffn_sw2': _L0_ffn_in['sw2'], 'L0_ffn_sb2': _L0_ffn_in['sb2'], 'L1_xattn_Wq': _L1_xattn_in['Wq'], 'L1_xattn_bq': _L1_xattn_in['bq'], 'L1_xattn_Wk': _L1_xattn_in['Wk'], 'L1_xattn_bk': _L1_xattn_in['bk'], 'L1_xattn_Wv': _L1_xattn_in['Wv'], 'L1_xattn_bv': _L1_xattn_in['bv'], 'L1_xattn_Wo': _L1_xattn_in['Wo'], 'L1_xattn_bo': _L1_xattn_in['bo'], 'L1_ffn_attn_mask': _L1_ffn_in['attn_mask'], 'L1_ffn_Wg': _L1_ffn_in['Wg'], 'L1_ffn_Wq': _L1_ffn_in['Wq'], 'L1_ffn_bq': _L1_ffn_in['bq'], 'L1_ffn_Wkv': _L1_ffn_in['Wkv'], 'L1_ffn_bkv': _L1_ffn_in['bkv'], 'L1_ffn_Wo': _L1_ffn_in['Wo'], 'L1_ffn_bo': _L1_ffn_in['bo'], 'L1_ffn_ln_g': _L1_ffn_in['ln_g'], 'L1_ffn_ln_b': _L1_ffn_in['ln_b']}

def reference(x, ctx_1024, g_xattn, g_ffn, L0_xattn_Wq, L0_xattn_Wk, L0_xattn_Wv, L0_xattn_Wo, L0_ffn_gate_w, L0_ffn_w1, L0_ffn_b1, L0_ffn_w2, L0_ffn_b2, L0_ffn_sw1, L0_ffn_sb1, L0_ffn_sw2, L0_ffn_sb2, L1_xattn_Wq, L1_xattn_bq, L1_xattn_Wk, L1_xattn_bk, L1_xattn_Wv, L1_xattn_bv, L1_xattn_Wo, L1_xattn_bo, L1_ffn_attn_mask, L1_ffn_Wg, L1_ffn_Wq, L1_ffn_bq, L1_ffn_Wkv, L1_ffn_bkv, L1_ffn_Wo, L1_ffn_bo, L1_ffn_ln_g, L1_ffn_ln_b):
    import jax
    import jax.numpy as jnp

    def _L0_xattn_ref(query, key, value, Wq, Wk, Wv, Wo):
        import jax, jax.numpy as jnp
        import numpy as np
        B, S, D, H = (2, 1024, 512, 16)
        HD = D // H
        SCALE = HD ** (-0.5)
        NEG = -1000000000.0
        b, sq, d = query.shape
        sk = key.shape[1]
        q = (query @ Wq.T).reshape(b, sq, H, HD).transpose(0, 2, 1, 3)
        k = (key @ Wk.T).reshape(b, sk, H, HD).transpose(0, 2, 1, 3)
        v = (value @ Wv.T).reshape(b, sk, H, HD).transpose(0, 2, 1, 3)
        scores = jnp.einsum('bhqd,bhkd->bhqk', q, k) * SCALE
        causal = jnp.arange(sq)[:, None] >= jnp.arange(sk)[None, :]
        scores = jnp.where(causal[None, None], scores, NEG)
        attn = jax.nn.softmax(scores, axis=-1)
        out = jnp.einsum('bhqk,bhkd->bhqd', attn, v)
        out = out.transpose(0, 2, 1, 3).reshape(b, sq, d)
        return out @ Wo.T

    def _L0_ffn_ref(x, gate_w, w1, b1, w2, b2, sw1, sb1, sw2, sb2):
        import jax, jax.numpy as jnp
        import numpy as np
        D_MODEL = 512
        HIDDEN = 2048
        N_ROUTING = 2
        B, S, D = x.shape
        xf = x.reshape(-1, D)
        gate_scores = xf @ gate_w.T
        gate_probs = jax.nn.softmax(gate_scores, axis=-1)
        top1 = jnp.argmax(gate_probs, axis=-1)
        one_hot = jax.nn.one_hot(top1, N_ROUTING, dtype=xf.dtype)
        masked = xf[None, :, :] * one_hot.T[:, :, None]
        h = jax.nn.relu(jnp.einsum('end,edh->enh', masked, w1) + b1[:, None, :])
        expert_out = jnp.einsum('enh,ehd->end', h, w2) + b2[:, None, :]
        routing_output = expert_out.sum(axis=0)
        shared = jax.nn.relu(xf @ sw1 + sb1) @ sw2 + sb2
        return (routing_output + shared).reshape(B, S, D)

    def _L1_xattn_ref(tgt, src, Wq, bq, Wk, bk, Wv, bv, Wo, bo):
        import jax, jax.numpy as jnp
        import numpy as np
        HIDDEN = 512
        NUM_HEADS = 16
        HEAD_DIM = HIDDEN // NUM_HEADS
        q = jnp.einsum('btd,hdk->bhtk', tgt, Wq) + bq[None, :, None, :]
        k = jnp.einsum('bsd,hdk->bhsk', src, Wk) + bk[None, :, None, :]
        v = jnp.einsum('bsd,hdk->bhsk', src, Wv) + bv[None, :, None, :]
        scale = 1.0 / jnp.sqrt(jnp.asarray(HEAD_DIM, q.dtype))
        scores = jnp.einsum('bhtk,bhsk->bhts', q, k) * scale
        weights = jax.nn.softmax(scores, axis=-1)
        out = jnp.einsum('bhts,bhsk->bhtk', weights, v)
        B, H, T, Dh = out.shape
        h = out.transpose(0, 2, 1, 3).reshape(B, T, H * Dh)
        return h @ Wo + bo

    def _L1_ffn_ref(x, attn_mask, Wg, Wq, bq, Wkv, bkv, Wo, bo, ln_g, ln_b):
        import jax, jax.numpy as jnp
        import numpy as np
        S, B, D, H, DH = (2048, 8, 512, 16, 64)

        def _forward(x, Wg, Wq, bq, Wkv, bkv, Wo, bo, ln_g, ln_b):
            s_len, bsz, d_model = x.shape
            n_head, _, d_head = Wq.shape
            cap = s_len // n_head
            scale = 1.0 / d_head ** 0.5
            h = jnp.transpose(x, (1, 0, 2))
            t = h
            probs = jax.nn.softmax(h @ Wg, axis=-1)
            scores = jnp.transpose(probs, (0, 2, 1))
            _, idx = jax.lax.top_k(scores, cap)
            idx = jnp.sort(idx, axis=-1)
            hg = jnp.take_along_axis(h[:, None, :, :], idx[..., None], axis=2)
            hg = jnp.transpose(hg, (1, 0, 2, 3))
            q = jnp.einsum('hbcd,hde->hbce', hg, Wq) + bq[:, None, None, :]
            kv = jnp.einsum('hbcd,hde->hbce', hg, Wkv) + bkv[:, None, None, :]
            k, v = jnp.split(kv, 2, axis=-1)
            att = jnp.einsum('hbid,hbjd->hbij', q, k) * scale
            p = jax.nn.softmax(att, axis=1)
            av = jnp.einsum('hbij,hbjd->hbid', p, v)
            ao = jnp.einsum('hbid,hde->hbie', av, Wo) + bo
            tok = jnp.transpose(idx, (1, 0, 2))
            b_ids = jnp.arange(bsz)[None, :, None]
            outs = jnp.zeros_like(t).at[b_ids, tok].add(ao)
            y = t + outs
            mu = jnp.mean(y, axis=-1, keepdims=True)
            var = jnp.var(y, axis=-1, keepdims=True)
            yn = (y - mu) * jax.lax.rsqrt(var + 1e-05) * ln_g + ln_b
            return jnp.transpose(yn, (1, 0, 2))
        return _forward(x, Wg, Wq, bq, Wkv, bkv, Wo, bo, ln_g, ln_b)
    x = x + jnp.tanh(g_xattn[0]) * _L0_xattn_ref(_layernorm(x, axis=-1), ctx_1024, ctx_1024, L0_xattn_Wq, L0_xattn_Wk, L0_xattn_Wv, L0_xattn_Wo)
    x = x + jnp.tanh(g_ffn[0]) * _L0_ffn_ref(_layernorm(x, axis=-1), L0_ffn_gate_w, L0_ffn_w1, L0_ffn_b1, L0_ffn_w2, L0_ffn_b2, L0_ffn_sw1, L0_ffn_sb1, L0_ffn_sw2, L0_ffn_sb2)
    x = x + jnp.tanh(g_xattn[1]) * _L1_xattn_ref(_layernorm(x, axis=-1), ctx_1024, L1_xattn_Wq, L1_xattn_bq, L1_xattn_Wk, L1_xattn_bk, L1_xattn_Wv, L1_xattn_bv, L1_xattn_Wo, L1_xattn_bo)
    x = x + jnp.tanh(g_ffn[1]) * _L1_ffn_ref(_layernorm(x, axis=-1), L1_ffn_attn_mask, L1_ffn_Wg, L1_ffn_Wq, L1_ffn_bq, L1_ffn_Wkv, L1_ffn_bkv, L1_ffn_Wo, L1_ffn_bo, L1_ffn_ln_g, L1_ffn_ln_b)
    return x

_drawn_inputs = setup_inputs


def setup_inputs(seed=0):
    import zlib

    import numpy as np

    out = dict(_drawn_inputs(seed))
    spreads = {'g_ffn': (-1.0, 0.2),
     'L1_xattn_bq': (0.0, 0.516),
     'L1_xattn_bk': (0.0, 0.8),
     'L1_xattn_bv': (0.0, 0.1),
     'L1_xattn_bo': (0.0, 0.1),
     'L1_ffn_bq': (0.0, 0.1),
     'L1_ffn_bkv': (0.0, 0.1),
     'L1_ffn_bo': (0.0, 0.1),
     'L1_ffn_ln_g': (1.0, 0.2),
     'L1_ffn_ln_b': (0.0, 0.1)}
    factors = {'L0_ffn_b1': 5.523, 'L0_ffn_b2': 3.111, 'L0_ffn_sb1': 7.534, 'L0_ffn_sb2': 4.58}
    for name, (base, spread) in spreads.items():
        noise = np.random.default_rng([zlib.crc32(name.encode()), seed]).standard_normal(out[name].shape)
        drawn = base * np.exp(spread * noise) if base else spread * noise
        out[name] = jnp.asarray(drawn.astype(out[name].dtype))
    for name, factor in factors.items():
        out[name] = (out[name] * factor).astype(out[name].dtype)
    return out
```

```python
from contextlib import ExitStack

import concourse.bass as bass
from concourse import mybir

F32 = mybir.dt.float32
F32R = mybir.dt.float32r
I32 = mybir.dt.int32
ALU = mybir.AluOpType
ACT = mybir.ActivationFunctionType
AX = mybir.AxisListType

P = 128
BATCH, SEQ, D = 4, 1024, 512
KEYS = 64
HEADS, HD = 16, 32
HIDDEN = 2048
TOK = BATCH * SEQ
TILE = 512
SUB = TILE // P
KC = D // P
NT = TOK // TILE
TPB = SEQ // TILE
CH = HIDDEN // P
WCOL = 2 * D + 1
SLOTS = NT + 1
LIST = SLOTS * TILE
GROUPS = TOK // P
SCALE = HD ** -0.5
NEG = -1e9
EPS = 1e-5


def allocators(nc, ctx, prefix):
    sems = []

    def clear():
        nc.clear_and_free_semaphores(sems)
        nc.all_engine_barrier()
    ctx.callback(clear)

    def sb(name, shape, dt=F32):
        return ctx.enter_context(nc.sbuf_tensor(prefix + name, shape, dt))

    def ps(name, cols=512):
        return ctx.enter_context(nc.psum_tensor(prefix + name, [P, cols], F32))

    def sem(name):
        sems.append(nc.alloc_semaphore(prefix + name))
        return sems[-1]
    return sb, ps, sem


def product3(pe, out, w, x, start, stop):
    pe.matmul(out, w[0], x[1], start=start, stop=False)
    pe.matmul(out, w[0], x[0], start=False, stop=False)
    return pe.matmul(out, w[1], x[0], start=False, stop=stop)


def diagonal(pool, m, made):
    pool.memset(m[:, :], 0.0).then_inc(made, 1)
    pool.wait_ge(made, 1)
    pool.affine_select(out=m[:, :], in_=m[:, :], compare_op=ALU.not_equal, fill=1.0,
                       base=0, pattern=[[-1, P]], channel_multiplier=1).then_inc(made, 1)


def fallback_rows(nc, w_all, bias_rows, gates, rows_out):
    RING = 4
    with ExitStack() as ctx:
        sb, ps, sem = allocators(nc, ctx, "fr_")
        w2b1 = sb("w2b1", [P, RING, D + 1])
        b1_wide = sb("b1_wide", [P, RING, P])
        bias = sb("bias", [P, 3, D])
        gate_in = sb("gate_in", [P, 4])
        gate = sb("gate", [P, 4])
        total = sb("total", [P, 2, D])
        ones = sb("ones", [P, P])
        acc = [ps(f"acc{e}") for e in range(2)]
        small_in, ones_set, wide, used, tanh_done, summed, stored = (
            sem(n) for n in ("small_in", "ones_set", "wide", "used", "tanh_done", "summed", "stored"))
        w2_in = [sem(f"w2_in{r}") for r in range(RING)]
        pieces = [(e, j) for e in range(2) for j in range(CH)]
        block = ctx.enter_context(nc.Block())

        @block.sync
        def _(sp):
            for r in range(3):
                sp.dma_start(bias[:, r, :], bias_rows[r:r + 1, :].to_broadcast([P, D])).then_inc(small_in, 16)
            sp.dma_start(gate_in[:, :], gates.to_broadcast([P, 4])).then_inc(small_in, 16)
            for n, (e, j) in enumerate(pieces):
                if n >= RING:
                    sp.wait_ge(used, n - RING + 1)
                sp.dma_start(w2b1[:, n % RING, :], w_all[1 + e, j, :, D:WCOL]).then_inc(w2_in[n % RING], 16)
            for e in range(2):
                sp.wait_ge(summed, 4 * e + 4)
                sp.dma_start(rows_out[e], total[:, e, :]).then_inc(stored, 16)
            sp.wait_ge(stored, 32)

        @block.scalar
        def _(act):
            act.wait_ge(small_in, 64)
            act.activation(gate[:, :], gate_in[:, :], ACT.Tanh).then_inc(tanh_done, 1)

        @block.vector
        def _(dve):
            dve.memset(ones[:, :], 1.0).then_inc(ones_set, 1)
            dve.wait_ge(ones_set, 1)
            for n, (e, j) in enumerate(pieces):
                dve.wait_ge(w2_in[n % RING], 16 * (n // RING + 1))
                if n >= RING:
                    dve.wait_ge(used, n - RING + 1)
                dve.tensor_scalar(b1_wide[:, n % RING, :], ones[:, :], w2b1[:, n % RING, D:D + 1], 0.0,
                                  ALU.mult, ALU.max).then_inc(wide, 1)
            dve.wait_ge(tanh_done, 1)
            dve.wait_ge(used, len(pieces))
            for e in range(2):
                at = total[:, e, :]
                dve.tensor_tensor(at, acc[1 - e][:, :], bias[:, 0, :], ALU.add).then_inc(summed, 1)
                for r in (1, 2):
                    dve.wait_ge(summed, 4 * e + r)
                    dve.tensor_tensor(at, at, bias[:, r, :], ALU.add).then_inc(summed, 1)
                dve.wait_ge(summed, 4 * e + 3)
                dve.tensor_scalar(at, at, gate[:, 2:3], None, ALU.mult).then_inc(summed, 1)

        @block.tensor
        def _(pe):
            for n, (e, j) in enumerate(pieces):
                pe.wait_ge(w2_in[n % RING], 16 * (n // RING + 1))
                pe.wait_ge(wide, n + 1)
                pe.matmul(acc[e][:, :], b1_wide[:, n % RING, :], w2b1[:, n % RING, 0:D],
                          start=(j == 0), stop=(j == CH - 1)).then_inc(used, 1)


def context(nc, ctx_t, wk, wv, bk, bv, k_out, v_out):
    with ExitStack() as ctx:
        sb, ps, sem = allocators(nc, ctx, "cx_")
        raw = sb("raw", [P, KC, BATCH, 2, KEYS])
        c_hl = [sb("c_" + n, [P, KC, BATCH, 2, KEYS], F32R) for n in ("hi", "lo")]
        w_raw = sb("w_raw", [P, 2, KC, D])
        w_hl = [sb("w_" + n, [P, 2, KC, D], F32R) for n in ("hi", "lo")]
        bias_k = sb("bias_k", [P, 2, KC])
        bias_v = sb("bias_v", [P, 2, D])
        value = sb("value", [P, 2, D])
        k_all = sb("k_all", [P, BATCH, 2, KC, 4 * KEYS], F32R)
        v_all = sb("v_all", [P, BATCH, 2, KC, 2, P], F32R)
        bank = [ps(f"bank{n}") for n in range(4)]
        small_in, w_in, cleared, hi_done, lo_done, full, k_hi, biased, v_hi, built, stored = (
            sem(n) for n in ("small_in", "w_in", "cleared", "hi_done", "lo_done", "full",
                             "k_hi", "biased", "v_hi", "built", "stored"))
        USES = KC + BATCH
        block = ctx.enter_context(nc.Block())

        def v_parts():
            for half in range(2):
                for j in range(2):
                    yield slice(KEYS * half, KEYS * half + KEYS), j, half, j * 64 + half * HD

        @block.sync
        def _(sp):
            for k in range(KC):
                for twice in range(2):
                    sp.dma_start(raw[:, k, :, twice, :],
                                 ctx_t[k * P:(k + 1) * P, :].rearrange("p (b s) -> p b s", b=BATCH)
                                 ).then_inc(small_in, 16)
            for l in range(2):
                sp.dma_start(bias_k[:, l, :], bk[l]).then_inc(small_in, 16)
                sp.dma_start(bias_v[:, l, :], bv[l].to_broadcast([P, D])).then_inc(small_in, 16)
            for l in range(2):
                if l:
                    sp.wait_ge(lo_done, 2)
                for n, w in enumerate((wk, wv)):
                    sp.dma_start(w_raw[:, n], w[l].rearrange("(k p) n -> p k n", p=P)).then_inc(w_in, 16)
            for l in range(2):
                sp.wait_ge(built, USES * (l + 1))
                for b in range(BATCH):
                    sp.dma_start(k_out[l, b], k_all[:, b].bitcast(F32).rearrange("p h g n -> p (h g n)")).then_inc(stored, 16)
                    sp.dma_start(v_out[l, b], v_all[:, b].bitcast(F32).rearrange("p h g j n -> p (h g j n)")).then_inc(stored, 16)
            sp.wait_ge(stored, 2 * 2 * BATCH * 16)

        @block.gpsimd
        def _(pool):
            pool.memset(k_all[:].bitcast(F32), 0.0).then_inc(cleared, 1)
            pool.memset(v_all[:].bitcast(F32), 0.0).then_inc(cleared, 1)

        @block.scalar
        def _(act):
            act.wait_ge(small_in, 12 * 16)
            act.activation(c_hl[0][:], raw[:], ACT.Copy).then_inc(hi_done, 1)
            act.wait_ge(cleared, 2)
            for l in range(2):
                act.wait_ge(w_in, 32 * (l + 1))
                if l:
                    act.wait_ge(full, USES)
                act.activation(w_hl[0][:], w_raw[:], ACT.Copy).then_inc(hi_done, 1)
                if l:
                    act.wait_ge(stored, 2 * BATCH * 16)
                for g in range(KC):
                    act.wait_ge(full, USES * l + g + 1)
                    for h in range(4):
                        rows = slice(HD * h, HD * h + HD)
                        last = act.activation(
                            k_all[rows, :, 0, g, h * KEYS:(h + 1) * KEYS],
                            bank[g][rows, 0:BATCH * KEYS].rearrange("p (b s) -> p b s", b=BATCH),
                            ACT.Identity, bias=bias_k[rows, l, g:g + 1])
                    last.then_inc(k_hi, 1)
                for b in range(BATCH):
                    act.wait_ge(biased, BATCH * l + b + 1)
                    for rows, j, half, at in v_parts():
                        src = value[rows, b % 2].rearrange("p (g j h c) -> p g j h c", g=KC, j=2, h=2)
                        last = act.activation(v_all[rows, b, 0, :, j, at:at + HD], src[:, :, j, half, :], ACT.Copy)
                    last.then_inc(v_hi, 1)

        @block.vector
        def _(dve):
            dve.wait_ge(hi_done, 1)
            dve.tensor_tensor(c_hl[1][:].rearrange("p k b t s -> p (k b t s)"),
                              raw[:].rearrange("p k b t s -> p (k b t s)"),
                              c_hl[0][:].bitcast(F32).rearrange("p k b t s -> p (k b t s)"),
                              ALU.subtract).then_inc(lo_done, 1)
            for l in range(2):
                dve.wait_ge(hi_done, 2 + l)
                dve.tensor_tensor(w_hl[1][:].rearrange("p w k n -> p (w k n)"),
                                  w_raw[:].rearrange("p w k n -> p (w k n)"),
                                  w_hl[0][:].bitcast(F32).rearrange("p w k n -> p (w k n)"),
                                  ALU.subtract).then_inc(lo_done, 1)
                for g in range(KC):
                    dve.wait_ge(k_hi, KC * l + g + 1)
                    for h in range(4):
                        rows = slice(HD * h, HD * h + HD)
                        last = dve.scalar_tensor_tensor(
                            out=k_all[rows, :, 1, g, h * KEYS:(h + 1) * KEYS],
                            in0=bank[g][rows, 0:BATCH * KEYS].rearrange("p (b s) -> p b s", b=BATCH),
                            scalar=bias_k[rows, l, g:g + 1],
                            in1=k_all[rows, :, 0, g, h * KEYS:(h + 1) * KEYS].bitcast(F32),
                            op0=ALU.add, op1=ALU.subtract)
                    last.then_inc(built, 1)
                for b in range(BATCH):
                    dve.wait_ge(full, USES * l + KC + b + 1)
                    dve.tensor_tensor(value[:, b % 2, :], bank[b][:, :], bias_v[:, l, :],
                                      ALU.add).then_inc(biased, 1)
                    dve.wait_ge(v_hi, BATCH * l + b + 1)
                    for rows, j, half, at in v_parts():
                        src = value[rows, b % 2].rearrange("p (g j h c) -> p g j h c", g=KC, j=2, h=2)
                        last = dve.tensor_tensor(v_all[rows, b, 1, :, j, at:at + HD], src[:, :, j, half, :],
                                                 v_all[rows, b, 0, :, j, at:at + HD].bitcast(F32), ALU.subtract)
                    last.then_inc(built, 1)

        @block.tensor
        def _(pe):
            for l in range(2):
                pe.wait_ge(lo_done, 2 + l)
                for g in range(KC):
                    if l:
                        pe.wait_ge(built, USES * l - BATCH + g + 1)
                    cols = slice(g * P, (g + 1) * P)
                    for k in range(KC):
                        mm = product3(pe, bank[g][:, 0:BATCH * KEYS], [w[:, 0, k, cols] for w in w_hl],
                                      [c[:, k, :, 0, :] for c in c_hl], k == 0, k == KC - 1)
                    mm.then_inc(full, 1)
                for b in range(BATCH):
                    pe.wait_ge(built, USES * l + b + 1)
                    for k in range(KC):
                        mm = product3(pe, bank[b][:, :], [c[:, k, b].rearrange("p t s -> p (t s)") for c in c_hl],
                                      [w[:, 1, k, :] for w in w_hl], k == 0, k == KC - 1)
                    mm.then_inc(full, 1)


def attention(nc, layer, x_in, x_out, wq, wo, bq, gates, k_dram, v_dram, row_dram):
    final = row_dram is not None
    xv = x_in[0:TOK, :].rearrange("(t s p) d -> t p s d", s=SUB, p=P)
    ov = x_out[0:TOK, :].rearrange("(t s p) d -> t p s d", s=SUB, p=P)
    with ExitStack() as ctx:
        sb, ps, sem = allocators(nc, ctx, f"a{layer}_")
        wq_hl = sb("wq", [P, 2, KC, D], F32R)
        wo_hl = sb("wo", [P, 2, KC, D], F32R)
        x = sb("x", [P, 2, SUB, D])
        xt = sb("xt", [P, 2, KC, TILE], F32R)
        qt = sb("qt", [P, 2, KC, TILE], F32R)
        prob = sb("prob", [P, 2, SUB, HEADS, KEYS])
        prob_t = sb("prob_t", [P, 4, 2, TILE], F32R)
        heads_t = sb("heads_t", [P, 2, KC, TILE], F32R)
        res = sb("res", [P, 2, SUB, D])
        kbd = sb("kbd", [P, 2, KC, 4 * KEYS], F32R)
        vbd = sb("vbd", [P, 2, KC, 2, P], F32R)
        ident = sb("ident", [P, P])
        mask = sb("mask", [P, KEYS])
        gate_in = sb("gate_in", [P, 4])
        gate = sb("gate", [P, 4])
        bias_q = sb("bias_q", [P, KC])
        stats = sb("stats", [P, SUB, 6])
        waited = sb("waited", [P, 1])
        mean_var = sb("mean_var", [P, SUB, 2])
        rstd = sb("rstd", [P, SUB])
        minus_half, eps, zero = (sb(n, [P, SUB]) for n in ("minus_half", "eps", "zero"))
        shift = sb("shift", [P, SUB])
        top = sb("top", [P, SUB, HEADS])
        mass = sb("mass", [P, SUB, HEADS])
        inv = sb("inv", [P, SUB, HEADS])
        if final:
            rows = sb("rows", [P, 3, D])
            normed = sb("normed", [P, SUB, D])
            f_stats = sb("f_stats", [P, SUB, 6])
            f_waited = sb("f_waited", [P, 1])
            f_mv = sb("f_mv", [P, SUB, 2])
            f_rstd, f_var, f_rstd2, f_scale, f_shift = (
                sb(n, [P, SUB]) for n in ("f_rstd", "f_var", "f_rstd2", "f_scale", "f_shift"))
        score_bank = [ps(f"score{i}", HEADS * KEYS) for i in range(2)]
        bank = [ps(f"bank{i}") for i in range(4)]
        (small_in, w_hi, w_ready, made, gate_done, rows_done, k_loaded, v_loaded, stored, normed_x,
         norm_chain, rstd_done, norm_ready, full, free, hi_done, score_full, masked, maxed, score_free, exp_done,
         summed, inv_done, prob_ready, res_biased, f_chain, f_done, f_ready, f_normed, f_scaled, out_ready) = (
            sem(n) for n in (
                "small_in", "w_hi", "w_ready", "made", "gate_done", "rows_done", "k_loaded", "v_loaded",
                "stored", "normed_x", "norm_chain", "rstd_done", "norm_ready", "full", "free", "hi_done", "score_full",
                "masked", "maxed", "score_free", "exp_done", "summed", "inv_done", "prob_ready",
                "res_biased", "f_chain", "f_done", "f_ready", "f_normed", "f_scaled", "out_ready"))
        w_in = [sem(f"w_in{n}") for n in range(2)]
        x_loaded = [sem(f"x_loaded{n}") for n in range(2)]
        res_loaded = [sem(f"res_loaded{n}") for n in range(2)]

        TURN, PV, XT, OUT, QT = "turn", "pv", "xt", "out", "qt"
        HEAD = [(TURN, 0), (TURN, 1)]
        for i in range(1, SUB):
            HEAD += [(TURN, 2 * i), (TURN, 2 * i + 1), (PV, i - 1)]
        SCORES = {(TURN, 2): 0, (PV, 3): 1, (OUT, 1): 2, (OUT, 3): 3}
        EXPONENT = {(TURN, 4): 0, (OUT, 0): 1, (OUT, 3): 2}
        NORM = {(TURN, 6): 0, (TURN, 7): 1, (PV, 2): 2, (XT, 0): 3}
        LAST_NORM = {(TURN, 4): 0, (TURN, 5): 1, (PV, 1): 2, (TURN, 7): 3}
        SUM = {(TURN, 6): 0, (OUT, 0): 1, (OUT, 2): 2}
        FULL_STEP = (HEAD + [(XT, 0), (XT, 1), (PV, 3), (XT, 2), (XT, 3)]
                     + [(OUT, i) for i in range(4)] + [(QT, i) for i in range(4)])
        TAIL_STEP = HEAD + [(PV, 3)] + [(OUT, i) for i in range(4)]
        OPENING = [(XT, i) for i in range(4)] + [(QT, i) for i in range(4)]
        N_OPEN, N_STEP, N_TAIL = len(OPENING), len(FULL_STEP), len(TAIL_STEP)
        N_OUT = SUB
        PEELED = 2
        LOOP_END = NT - 2

        class Step:

            def __init__(self, u, par, pair, first_use, first_hi, plan, has_v, has_w, has_last):
                self.u, self.par, self.pair = u, par, pair
                self.use, self.hi, self.plan = first_use, first_hi, plan
                self.has_v, self.has_w, self.has_last = has_v, has_w, has_last
                self.had_w = has_w or has_v

            def after(self, what):
                return self.use + self.plan.index(what) + 1

        def steps(eng, opening, step):
            def in_order(u, par, pair):
                return Step(u, par, pair, 2 * N_OPEN + N_STEP * u, 2 * N_OPEN + (N_STEP - N_OUT) * u,
                            FULL_STEP, True, True, not (isinstance(u, int) and u == 0))
            opening()
            for u in range(PEELED):
                step(in_order(u, u % 2, u // 2))
            with eng.Fori(PEELED // 2, LOOP_END // 2) as pair:
                for par in range(2):
                    step(in_order(pair * 2 + par, par, pair))
            use = 2 * N_OPEN + N_STEP * LOOP_END
            hi = 2 * N_OPEN + (N_STEP - N_OUT) * LOOP_END
            step(Step(NT - 2, 0, NT // 2 - 1, use, hi, TAIL_STEP, True, False, True))
            step(Step(NT - 1, 1, NT // 2 - 1, use + N_TAIL, hi + N_TAIL - N_OUT, TAIL_STEP, False, False, True))

        block = ctx.enter_context(nc.Block())

        @block.sync
        def _(sp):
            sp.dma_start(res[:, 0], wq.rearrange("(k p) n -> p k n", p=P)).then_inc(w_in[0], 16)
            sp.dma_start(x[:, 0], xv[0]).then_inc(x_loaded[0], 16)
            sp.dma_start(x[:, 1], xv[1]).then_inc(x_loaded[1], 16)
            sp.dma_start(gate_in[:, :], gates.to_broadcast([P, 4])).then_inc(small_in, 16)
            sp.dma_start(bias_q[:, :], bq).then_inc(small_in, 16)
            if final:
                for r in range(3):
                    sp.dma_start(rows[:, r, :], row_dram[r:r + 1, :].to_broadcast([P, D])).then_inc(small_in, 16)
            sp.dma_start(res[:, 1], wo.rearrange("(k p) n -> p k n", p=P)).then_inc(w_in[1], 16)
            sp.dma_start(kbd[:].bitcast(F32).rearrange("p h g n -> p (h g n)"), k_dram[0]).then_inc(k_loaded, 16)
            sp.dma_start(vbd[:].bitcast(F32).rearrange("p h g j n -> p (h g j n)"), v_dram[0]).then_inc(v_loaded, 16)
            for t in range(2):
                sp.wait_ge(w_ready, t + 1)
                sp.dma_start(res[:, t], xv[t]).then_inc(res_loaded[t], 16)

            def step(s):
                if s.has_w:
                    sp.wait_ge(full, s.use - 8)
                    sp.dma_start(x[:, s.par], xv[s.u + 2]).then_inc(x_loaded[s.par], 16)
                if s.has_last:
                    if final:
                        sp.wait_ge(out_ready, SUB * s.u)
                    else:
                        sp.wait_ge(free, s.use - 4 * s.had_w)
                    sp.dma_start(ov[s.u - 1], res[:, 1 - s.par]).then_inc(stored, 16)
                if s.has_last and s.has_v:
                    sp.wait_ge(stored, 16 * s.u)
                    sp.dma_start(res[:, 1 - s.par], xv[s.u + 1]).then_inc(res_loaded[1 - s.par], 16)
                if s.has_v and s.par == 1:
                    sp.wait_ge(full, s.after((PV, 3)))
                    sp.dma_start(vbd[:].bitcast(F32).rearrange("p h g j n -> p (h g j n)"), v_dram[s.pair + 1]).then_inc(v_loaded, 16)

                if s.has_w and s.par == 0:
                    sp.wait_ge(score_full, SUB * (s.u + 2))
                    sp.dma_start(kbd[:].bitcast(F32).rearrange("p h g n -> p (h g n)"), k_dram[s.pair + 1]).then_inc(k_loaded, 16)

            steps(sp, lambda: None, step)
            if final:
                sp.wait_ge(out_ready, SUB * NT)
            else:
                sp.wait_ge(free, 2 * N_OPEN + N_STEP * LOOP_END + 2 * N_TAIL)
            sp.dma_start(ov[NT - 1], res[:, (NT - 1) % 2]).then_inc(stored, 16)
            sp.wait_ge(stored, 16 * NT)

        @block.gpsimd
        def _(pool):
            diagonal(pool, ident, made)
            pool.memset(mask[:, :], 0.0).then_inc(made, 1)
            pool.wait_ge(made, 3)
            pool.affine_select(out=mask[:, :], in_=mask[:, :], compare_op=ALU.is_ge, fill=NEG / SCALE,
                               base=0, pattern=[[-1, KEYS]], channel_multiplier=1).then_inc(made, 1)
            for m, value in ((minus_half, -0.5), (eps, EPS), (zero, 0.0)):
                pool.memset(m[:, :], value).then_inc(made, 1)
            pool.wait_ge(made, 7)

            def normalise(v, par, i):
                pool.wait_ge(inv_done, SUB * v + i + 1)
                pool.tensor_tensor(prob[:, par, i], prob[:, par, i],
                                   inv[:, i, :].unsqueeze(2).to_broadcast([P, HEADS, KEYS]),
                                   ALU.mult).then_inc(prob_ready, 1)

            def norm_rstd(t):
                pool.wait_ge(norm_chain, (SUB + 1) * (t + 1))
                pool.tensor_tensor(rstd[:, :], mean_var[:, :, 1], eps[:, :], ALU.add).then_inc(rstd_done, 1)
                pool.wait_ge(rstd_done, 2 * t + 1)
                pool.tensor_tensor(rstd[:, :], rstd[:, :], minus_half[:, :], ALU.pow).then_inc(rstd_done, 1)

            def last_norm_scale(t):
                pool.wait_ge(f_chain, (SUB + 1) * (t + 1))
                if not (isinstance(t, int) and t == 0):
                    pool.wait_ge(f_normed, SUB * t)

                def then(ins, k):
                    ins.then_inc(f_done, 1)
                    pool.wait_ge(f_done, 8 * t + k)
                then(pool.tensor_tensor(f_var[:, :], f_mv[:, :, 1], eps[:, :], ALU.add), 1)
                then(pool.tensor_tensor(f_rstd[:, :], f_var[:, :], minus_half[:, :], ALU.pow), 2)
                then(pool.tensor_tensor(f_var[:, :], f_mv[:, :, 1], f_rstd[:, :], ALU.mult), 3)
                then(pool.tensor_tensor(f_var[:, :], f_var[:, :], f_rstd[:, :], ALU.mult), 4)
                then(pool.tensor_tensor(f_var[:, :], f_var[:, :], eps[:, :], ALU.add), 5)
                then(pool.tensor_tensor(f_rstd2[:, :], f_var[:, :], minus_half[:, :], ALU.pow), 6)
                then(pool.tensor_tensor(f_scale[:, :], f_rstd2[:, :], f_rstd[:, :], ALU.mult), 7)
                then(pool.tensor_tensor(f_shift[:, :], f_mv[:, :, 0], f_scale[:, :], ALU.mult), 8)
                pool.tensor_tensor(f_shift[:, :], zero[:, :], f_shift[:, :], ALU.subtract).then_inc(f_ready, 1)

            def last_norm_affine(t):
                pool.wait_ge(f_normed, SUB * (t + 1))
                for r, op in ((1, ALU.mult), (2, ALU.add)):
                    if r == 2:
                        pool.wait_ge(f_scaled, 2 * t + 1)
                    pool.tensor_tensor(normed[:], normed[:],
                                       rows[:, r, :].unsqueeze(1).to_broadcast([P, SUB, D]),
                                       op).then_inc(f_scaled, 1)

            def opening():
                norm_rstd(0)
                norm_rstd(1)
                if final:
                    pool.wait_ge(rows_done, 3)
                for i in range(SUB):
                    normalise(0, 0, i)

            def step(s):
                if final and s.has_last:
                    last_norm_scale(s.u - 1)
                if s.has_w:
                    norm_rstd(s.u + 2)
                if final:
                    pool.wait_ge(res_loaded[s.par], 16 * (s.pair + 1))
                    pool.tensor_tensor(res[:, s.par], res[:, s.par],
                                       rows[:, 0, :].unsqueeze(1).to_broadcast([P, SUB, D]),
                                       ALU.add).then_inc(res_biased, 1)
                for i in range(SUB):
                    if s.has_v:
                        normalise(s.u + 1, 1 - s.par, i)
                    if final and s.has_last and i == 0:
                        last_norm_affine(s.u - 1)

            steps(pool, opening, step)
            if final:
                last_norm_scale(NT - 1)
                last_norm_affine(NT - 1)

        @block.scalar
        def _(act):
            for m, w in enumerate((wq_hl, wo_hl)):
                act.wait_ge(w_in[m], 16)
                act.activation(w[:, 0], res[:, m], ACT.Copy).then_inc(w_hi, 1)
            act.wait_ge(small_in, 32 + 48 * final)
            act.activation(gate[:, :], gate_in[:, :], ACT.Tanh).then_inc(gate_done, 1)

            def norm(t, par, groups=range(SUB)):
                for i in groups:
                    if i == 0:
                        act.wait_ge(norm_ready, t + 1)
                    act.activation(x[:, par, i], x[:, par, i], ACT.Identity, bias=shift[:, i:i + 1],
                                   scale=rstd[:, i:i + 1]).then_inc(normed_x, 1)

            def exponent(v, par, i):
                act.wait_ge(score_free, SUB * v + i + 1)
                act.activation(prob[:, par, i], prob[:, par, i], ACT.Exp, scale=SCALE).then_inc(exp_done, 1)

            def last_norm(t, par, i):
                if i == 0:
                    act.wait_ge(f_ready, t + 1)
                    if not (isinstance(t, int) and t == 0):
                        act.wait_ge(out_ready, SUB * t)
                act.activation(normed[:, i], res[:, par, i], ACT.Identity,
                               bias=f_shift[:, i:i + 1], scale=f_scale[:, i:i + 1]).then_inc(f_normed, 1)

            def hi_half(kind, a, use, k):
                act.wait_ge(full, use + k + 1)
                src = bank[k % 4][:, :]
                if kind == QT:
                    ins = act.activation(qt[:, 0, a], src, ACT.Identity, bias=bias_q[:, a:a + 1])
                else:
                    dst = {XT: xt[:, 0, a % KC], TURN: prob_t[:, a % 4, 0], PV: heads_t[:, 0, a % KC]}[kind]
                    ins = act.activation(dst, src, ACT.Copy)
                ins.then_inc(hi_done, 1)

            def opening():
                norm(0, 0)
                for k, (kind, a) in enumerate(OPENING):
                    hi_half(kind, a, 0, k)
                norm(1, 1)
                for i in range(SUB):
                    exponent(0, 0, i)
                for k, (kind, a) in enumerate(OPENING):
                    hi_half(kind, a, N_OPEN, k)

            def step(s):
                for k, (kind, a) in enumerate(s.plan):
                    if s.has_v and (kind, a) in EXPONENT:
                        exponent(s.u + 1, 1 - s.par, EXPONENT[kind, a])
                    if s.has_v and (kind, a) == (QT, 1):
                        exponent(s.u + 1, 1 - s.par, SUB - 1)
                    if final and s.has_last and (kind, a) in LAST_NORM:
                        last_norm(s.u - 1, 1 - s.par, LAST_NORM[kind, a])
                    if s.has_w and (kind, a) in NORM:
                        norm(s.u + 2, s.par, [NORM[kind, a]])
                    if kind != OUT:
                        hi_half(kind, a, s.use, k)
                if s.has_v and not s.has_w:
                    exponent(s.u + 1, 1 - s.par, SUB - 1)

            steps(act, opening, step)
            if final:
                for i in range(SUB):
                    last_norm(NT - 1, (NT - 1) % 2, i)

        @block.vector
        def _(dve):
            for m, w in enumerate((wq_hl, wo_hl)):
                dve.wait_ge(w_hi, m + 1)
                dve.tensor_tensor(w[:, 1], res[:, m], w[:, 0].bitcast(F32), ALU.subtract).then_inc(w_ready, 1)
            dve.wait_ge(gate_done, 1)
            dve.wait_ge(made, 4)
            if final:
                for r, by in enumerate((1, 3, 3)):
                    dve.tensor_scalar(rows[:, r, :], rows[:, r, :], gate[:, by:by + 1], None,
                                      ALU.mult).then_inc(rows_done, 1)

            def norm_stats(t, par, loads):
                for i in range(SUB):
                    group_stats(t, par, loads, i)
                norm_mean(t)

            def group_stats(t, par, loads, i):
                if i == 0:
                    dve.wait_ge(x_loaded[par], 16 * loads)
                    if not (isinstance(t, int) and t == 0):
                        dve.wait_ge(normed_x, SUB * t)
                dve.bn_stats(stats[:, i, :], x[:, par, i, :]).then_inc(norm_chain, 1)

            def norm_mean(t):
                dve.wait_ge(norm_chain, (SUB + 1) * t + SUB)
                dve.tensor_copy(waited[:, :], stats[:, 0, 0:1])
                for i in range(SUB):
                    last = dve.bn_aggr(mean_var[:, i, :], stats[:, i, :])
                last.then_inc(norm_chain, 1)

            def norm_shift(t):
                dve.wait_ge(rstd_done, 2 * t + 2)
                dve.scalar_tensor_tensor(out=shift[:, :], in0=mean_var[:, :, 0], scalar=-1.0,
                                         in1=rstd[:, :], op0=ALU.mult, op1=ALU.mult).then_inc(norm_ready, 1)

            def softmax_shift(v, par, pair, i):
                dve.wait_ge(score_full, SUB * v + i + 1)
                raw = score_bank[i % 2][:, :].rearrange("p (h s) -> p h s", h=HEADS)
                if layer == 0 and par == 0 and i == 0:
                    dve.tensor_tensor(prob[:, par, i], raw, mask[:, :].unsqueeze(1).to_broadcast([P, HEADS, KEYS]),
                                      ALU.add).then_inc(masked, 1)
                    dve.wait_ge(masked, pair + 1)
                    raw = prob[:, par, i]
                dve.tensor_reduce(top[:, i, :], raw, AX.X, ALU.max).then_inc(maxed, 1)
                dve.wait_ge(maxed, SUB * v + i + 1)
                dve.tensor_tensor(prob[:, par, i], raw, top[:, i, :].unsqueeze(2).to_broadcast([P, HEADS, KEYS]),
                                  ALU.subtract).then_inc(score_free, 1)

            def softmax_sum(v, par, i):
                dve.wait_ge(exp_done, SUB * v + i + 1)
                dve.tensor_reduce(mass[:, i, :], prob[:, par, i], AX.X, ALU.add).then_inc(summed, 1)
                dve.wait_ge(summed, SUB * v + i + 1)
                if not (isinstance(v, int) and v == 0):
                    dve.wait_ge(prob_ready, SUB * v + i - 3)
                dve.reciprocal(inv[:, i, :], mass[:, i, :]).then_inc(inv_done, 1)

            def lo_half(kind, a, k, hi_count):
                dve.wait_ge(hi_done, hi_count)
                src = bank[k % 4][:, :]
                if kind == QT:
                    ins = dve.scalar_tensor_tensor(out=qt[:, 1, a], in0=src, scalar=bias_q[:, a:a + 1],
                                                   in1=qt[:, 0, a].bitcast(F32), op0=ALU.add, op1=ALU.subtract)
                else:
                    hi, lo = {XT: (xt[:, 0, a % KC], xt[:, 1, a % KC]),
                              PV: (heads_t[:, 0, a % KC], heads_t[:, 1, a % KC]),
                              TURN: (prob_t[:, a % 4, 0], prob_t[:, a % 4, 1])}[kind]
                    ins = dve.tensor_tensor(lo, src, hi.bitcast(F32), ALU.subtract)
                ins.then_inc(free, 1)

            def residual(s, i, k):
                if i == 0:
                    dve.wait_ge(res_loaded[s.par], 16 * (s.pair + 1))
                    if final:
                        dve.wait_ge(res_biased, s.u + 1)
                dve.wait_ge(full, s.use + k + 1)
                dve.scalar_tensor_tensor(out=res[:, s.par, i], in0=bank[k % 4][:, :], scalar=gate[:, layer:layer + 1],
                                         in1=res[:, s.par, i], op0=ALU.mult, op1=ALU.add).then_inc(free, 1)

            def last_stats(s, i):
                if i == 0:
                    dve.wait_ge(free, s.after((OUT, 3)))
                    if s.has_last:
                        dve.wait_ge(f_ready, s.u)
                dve.bn_stats(f_stats[:, i, :], res[:, s.par, i, :]).then_inc(f_chain, 1)

            def last_mean(s):
                dve.wait_ge(f_chain, (SUB + 1) * s.u + SUB)
                dve.tensor_copy(f_waited[:, :], f_stats[:, 0, 0:1])
                for i in range(SUB):
                    last = dve.bn_aggr(f_mv[:, i, :], f_stats[:, i, :])
                last.then_inc(f_chain, 1)

            def output(tile, par):
                dve.wait_ge(f_scaled, 2 * tile + 2)
                for i in range(SUB):
                    dve.tensor_tensor(res[:, par, i], res[:, par, i], normed[:, i], ALU.add).then_inc(out_ready, 1)

            def opening():
                norm_stats(0, 0, 1)
                norm_shift(0)
                norm_stats(1, 1, 1)
                norm_shift(1)
                for k, (kind, a) in enumerate(OPENING):
                    lo_half(kind, a, k, k + 1)
                for i in range(SUB):
                    softmax_shift(0, 0, 0, i)
                    softmax_sum(0, 0, i)
                for k, (kind, a) in enumerate(OPENING):
                    lo_half(kind, a, k, N_OPEN + k + 1)

            def step(s):
                v_par, hi = 1 - s.par, s.hi
                for k, (kind, a) in enumerate(s.plan):
                    if s.has_v and (kind, a) in SCORES:
                        softmax_shift(s.u + 1, v_par, s.pair + s.par, SCORES[kind, a])
                    if kind == OUT:
                        residual(s, a, k)
                    else:
                        hi = hi + 1
                        lo_half(kind, a, k, hi)
                    if s.has_w and (kind, a) == (TURN, 5):
                        norm_shift(s.u + 2)
                    if s.has_v and (kind, a) in SUM:
                        softmax_sum(s.u + 1, v_par, SUM[kind, a])
                    if s.has_v and (kind, a) == (QT, 1):
                        softmax_sum(s.u + 1, v_par, SUB - 1)
                    if s.has_w and kind == TURN and a < SUB:
                        group_stats(s.u + 2, s.par, s.pair + 2, a)
                    if s.has_w and (kind, a) == (TURN, 3):
                        norm_mean(s.u + 2)
                    if final and kind == QT:
                        last_stats(s, a)
                    if final and s.has_last and (kind, a) == (OUT, 1):
                        output(s.u - 1, 1 - s.par)
                if s.has_v and not s.has_w:
                    softmax_sum(s.u + 1, v_par, SUB - 1)
                if final:
                    if not s.has_w:
                        for i in range(SUB):
                            last_stats(s, i)
                    last_mean(s)

            steps(dve, opening, step)
            if final:
                output(NT - 1, (NT - 1) % 2)

        @block.tensor
        def _(pe):
            pe.wait_ge(made, 2)
            pe.wait_ge(w_ready, 2)

            def turn_x(par, k, at):
                for i in range(SUB):
                    mm = pe.transpose(bank[at % 4][:, i * P:(i + 1) * P], x[:, par, i, k * P:(k + 1) * P], ident[:, :])
                return mm

            def query(m, at):
                for k in range(KC):
                    mm = product3(pe, bank[at % 4][:, :], [wq_hl[:, h, k, m * P:(m + 1) * P] for h in range(2)],
                                  [xt[:, h, k] for h in range(2)], k == 0, k == KC - 1)
                return mm

            def scores(v, par, i, after_first):
                if after_first:
                    pe.wait_ge(score_free, SUB * v + i - 1)
                if i == 0 and par == 0:
                    pe.wait_ge(k_loaded, 8 * v + 16)
                for g in range(KC):
                    mm = product3(pe, score_bank[i % 2][:, g * 4 * KEYS:(g + 1) * 4 * KEYS],
                                  [qt[:, h, g, i * P:(i + 1) * P] for h in range(2)],
                                  [kbd[:, h, g] for h in range(2)], True, True)
                mm.then_inc(score_full, 1)

            def opening():
                for t in range(2):
                    first = N_OPEN * t
                    pe.wait_ge(normed_x, SUB * (t + 1))
                    for k, (kind, a) in enumerate(OPENING):
                        if (kind, a) == (QT, 0):
                            pe.wait_ge(free, first + 4)
                        elif first + k >= 4:
                            pe.wait_ge(free, first + k - 3)
                        mm = turn_x(t, a, k) if kind == XT else query(a, k)
                        mm.then_inc(full, 1)
                    if t == 0:
                        pe.wait_ge(free, N_OPEN)
                        for i in range(SUB):
                            scores(0, 0, i, i >= 2)

            def step(s):
                for k, (kind, a) in enumerate(s.plan):
                    if s.has_v and (kind, a) in SCORES:
                        if SCORES[kind, a] == 0:
                            pe.wait_ge(free, s.use)
                        scores(s.u + 1, 1 - s.par, SCORES[kind, a], True)
                    if (kind, a) == (TURN, 0):
                        pe.wait_ge(prob_ready, SUB * (s.u + 1))
                        if s.par == 0:
                            pe.wait_ge(v_loaded, 8 * s.u + 16)
                    pe.wait_ge(free, s.use + k - 3)
                    if kind == TURN:
                        for i in range(SUB):
                            mm = pe.transpose(bank[k % 4][:, i * P:(i + 1) * P],
                                              prob[:, s.par, i, 2 * a:2 * a + 2, :].rearrange("p h s -> p (h s)"),
                                              ident[:, :])
                    elif kind == PV:
                        pe.wait_ge(free, s.after((TURN, 2 * a + 1)))
                        for j in range(2):
                            mm = product3(pe, bank[k % 4][:, :], [vbd[:, h, a, j] for h in range(2)],
                                          [prob_t[:, (2 * a + j) % 4, h] for h in range(2)], j == 0, j == 1)
                    elif kind == XT:
                        if a == 0:
                            pe.wait_ge(normed_x, SUB * (s.u + 3))
                        mm = turn_x(s.par, a, k)
                    elif kind == OUT:
                        if a == 0:
                            pe.wait_ge(free, s.after((PV, 3)))
                        for g in range(KC):
                            mm = product3(pe, bank[k % 4][:, :],
                                          [heads_t[:, h, g, a * P:(a + 1) * P] for h in range(2)],
                                          [wo_hl[:, h, g] for h in range(2)], g == 0, g == KC - 1)
                    else:
                        if a == 0:
                            pe.wait_ge(free, s.after((XT, 3)))
                        mm = query(a, k)
                    mm.then_inc(full, 1)

            steps(pe, opening, step)


def mlp(nc, routed, x_in, res_in, x_out, w_all, gates, gate_w, is_second, order, expert, fallback):
    tiles = SLOTS if routed else NT
    xv = x_in[0:TOK, :].rearrange("(t s p) d -> t p s d", s=SUB, p=P)
    rv = res_in[0:TOK, :].rearrange("(t s p) d -> t p s d", s=SUB, p=P)
    ov = x_out[0:TOK, :].rearrange("(t s p) d -> t p s d", s=SUB, p=P)
    with ExitStack() as ctx:
        sb, ps, sem = allocators(nc, ctx, "mr_" if routed else "ms_")
        RING = 4
        stage = sb("stage", [P, RING, WCOL])
        w_hl = sb("w", [P, 2, CH, 2 * D], F32R)
        b1 = sb("b1", [P, CH])
        x = sb("x", [P, SUB, D])
        xt = sb("xt", [P, 2, KC, TILE], F32R)
        hidden = sb("hidden", [P, 2, TILE])
        h_hl = sb("h", [P, 2, 2, TILE], F32R)
        res = sb("res", [P, SUB, D])
        ident = sb("ident", [P, P])
        minus_half, eps, zero = (sb(n, [P, SUB]) for n in ("minus_half", "eps", "zero"))
        gate_in = sb("gate_in", [P, 4])
        gate = sb("gate", [P, 4])
        stats = sb("stats", [P, SUB, 6])
        waited = sb("waited", [P, 1])
        mean_var = sb("mean_var", [P, SUB, 2])
        rstd = sb("rstd", [P, SUB])
        shift = sb("shift", [P, SUB])
        if routed:
            x_list = sb("x_list", [P, SUB], I32)
            res_list = sb("res_list", [P, SUB], I32)
            fall = sb("fall", [P, D])
            carrier = sb("carrier", [P, 4])
        else:
            gate_rows = sb("gate_rows", [P, 2, D])
            product = sb("product", [P, 2, D])
            score = sb("score", [P, SUB, 2])
        hid_bank = [ps(f"hid{i}") for i in range(2)]
        turn_bank = [ps(f"turn{i}") for i in range(2)]
        out_bank = [ps(f"out{i}") for i in range(SUB)]
        (small_in, made, gate_done, x_loaded, res_loaded, stored, norm_chain, rstd_done, norm_ready,
         normed_x, turn_full, turn_hi, turn_free, w_split, w_ready, hid_full, hid_hi, hid_ready, piece_done,
         out_ready, fall_in, fall_added, x_list_in, res_list_in, scored, chosen) = (
            sem(n) for n in (
                "small_in", "made", "gate_done", "x_loaded", "res_loaded", "stored", "norm_chain",
                "rstd_done", "norm_ready", "normed_x", "turn_full", "turn_hi", "turn_free", "w_split",
                "w_ready", "hid_full", "hid_hi", "hid_ready", "piece_done", "out_ready",
                "fall_in", "fall_added", "x_list_in", "res_list_in", "scored", "chosen"))
        w_in = [sem(f"w_in{r}") for r in range(RING)]
        AHEAD = 3
        LOADS = 64 if routed else 16
        block = ctx.enter_context(nc.Block())

        def tiles_loop(eng, first, body):
            for s in range(first):
                body(s, True)
            with eng.Fori(first, tiles - 1) as s:
                body(s, True)
            body(tiles - 1, False)

        def list_rows(s):
            return order[bass.ds(s * TILE, TILE), :].rearrange("(p g) o -> p (g o)", p=P)

        @block.sync
        def _(sp):
            sp.dma_start(gate_in[:, :], gates.to_broadcast([P, 4])).then_inc(small_in, 16)
            if not routed:
                for e in range(2):
                    sp.dma_start(gate_rows[:, e, :], gate_w[e:e + 1, :].to_broadcast([P, D])).then_inc(small_in, 16)
                sp.dma_start(x[:], xv[0]).then_inc(x_loaded, 16)
            else:
                sp.dma_start(x_list[:, :], list_rows(0)).then_inc(x_list_in, 16)

            def weights(s, which, lists=None):
                for j in range(CH):
                    if not (isinstance(s, int) and CH * s + j < RING):
                        sp.wait_ge(w_ready, CH * s + j - RING + 1)
                    sp.dma_start(stage[:, j % RING, :], which[j]).then_inc(w_in[j % RING], 16)
                    if lists and j == 2 * RING:
                        lists()

            if routed:
                def body(s, more):
                    e = sp.value_load(expert[0:1, bass.ds(s, 1)],
                                      min_val=0, max_val=1)

                    def lists():
                        if not (isinstance(s, int) and s == 0):
                            sp.wait_ge(stored, 64 * s)
                        sp.dma_start(res_list[:, :], list_rows(s)).then_inc(res_list_in, 16)
                        sp.dma_start(fall[:, :], fallback[e]).then_inc(fall_in, 16)
                        if more:
                            sp.wait_ge(x_loaded, 64 * (s + 1))
                            sp.dma_start(x_list[:, :], list_rows(s + 1)).then_inc(x_list_in, 16)
                    weights(s, w_all[e + 1], lists)
                tiles_loop(sp, 1, body)
            else:
                weights(0, w_all[0])

                def body(s, more):
                    if not (isinstance(s, int) and s == 0):
                        sp.wait_ge(stored, 16 * s)
                    sp.dma_start(res[:], rv[s]).then_inc(res_loaded, 16)
                    if more:
                        sp.wait_ge(turn_full, KC * (s + 1))
                        sp.wait_ge(scored, SUB * (s + 1))
                        sp.dma_start(x[:], xv[s + 1]).then_inc(x_loaded, 16)
                    sp.wait_ge(out_ready, SUB * (s + 1))
                    sp.dma_start(ov[s], res[:]).then_inc(stored, 16)
                tiles_loop(sp, 1, body)
                sp.wait_ge(stored, 16 * tiles)

        @block.gpsimd
        def _(pool):
            diagonal(pool, ident, made)
            for m, value in ((minus_half, -0.5), (eps, EPS), (zero, 0.0)):
                pool.memset(m[:, :], value).then_inc(made, 1)
            pool.wait_ge(made, 5)

            def gather(dst, lists, lists_in, table, loaded, s):
                pool.wait_ge(lists_in, 16 * (s + 1))
                at = 0 if dst is x else 1
                pool.tensor_tensor(carrier[:, at:at + 1], zero[:, 0:1], zero[:, 0:1], ALU.add)
                for g in range(SUB):
                    pool.indirect_dma_start(
                        out=dst[:, g, :], out_offset=None, in_=table,
                        in_offset=bass.IndirectOffsetOnAxis(ap=lists[:, g:g + 1], axis=0)).then_inc(loaded, 16)

            def scatter(s, at=2):
                pool.wait_ge(out_ready, SUB * (s + 1))
                pool.tensor_tensor(carrier[:, at:at + 1], zero[:, 0:1], zero[:, 0:1], ALU.add)
                for g in range(SUB):
                    pool.indirect_dma_start(
                        out=x_out, out_offset=bass.IndirectOffsetOnAxis(ap=res_list[:, g:g + 1], axis=0),
                        in_=res[:, g, :], in_offset=None).then_inc(stored, 16)

            def norm_rstd(t):
                pool.wait_ge(norm_chain, 2 * t + 2)
                pool.tensor_tensor(rstd[:, :], mean_var[:, :, 1], eps[:, :], ALU.add).then_inc(rstd_done, 1)
                pool.wait_ge(rstd_done, 2 * t + 1)
                pool.tensor_tensor(rstd[:, :], rstd[:, :], minus_half[:, :], ALU.pow).then_inc(rstd_done, 1)

            def split(s, j):
                pool.wait_ge(w_split, CH * s + j + 1)
                pool.tensor_tensor(b1[:, j:j + 1], stage[:, j % RING, 2 * D:WCOL], zero[:, 0:1], ALU.add)
                pool.tensor_tensor(w_hl[:, 1, j], stage[:, j % RING, 0:2 * D], w_hl[:, 0, j].bitcast(F32),
                                   ALU.subtract).then_inc(w_ready, 1)

            if routed:
                gather(x, x_list, x_list_in, x_in, x_loaded, 0)
            norm_rstd(0)
            for j in range(AHEAD):
                split(0, j)

            def body(s, more):
                first = isinstance(s, int) and s == 0
                for j in range(CH):
                    if j + AHEAD < CH:
                        if routed or first:
                            split(s, j + AHEAD)
                    elif routed and more:
                        split(s + 1, j + AHEAD - CH)
                    if routed and j == 0 and not first:
                        scatter(s - 1)
                    if routed and j == 1:
                        if not first:
                            pool.wait_ge(stored, 64 * s)
                        gather(res, res_list, res_list_in, res_in, res_loaded, s)
                    if routed and j == 3 and more:
                        pool.wait_ge(turn_full, KC * (s + 1))
                        gather(x, x_list, x_list_in, x_in, x_loaded, s + 1)
                    if more and j == 9:
                        norm_rstd(s + 1)
            tiles_loop(pool, 1, body)
            if routed:
                scatter(tiles - 1, 3)
                pool.wait_ge(stored, 64 * tiles)

        @block.scalar
        def _(act):
            act.wait_ge(small_in, 16 if routed else 48)
            act.activation(gate[:, :], gate_in[:, :], ACT.Tanh).then_inc(gate_done, 1)

            def norm(t):
                act.wait_ge(norm_ready, t + 1)
                for i in range(SUB):
                    act.activation(x[:, i], x[:, i], ACT.Identity, bias=shift[:, i:i + 1],
                                   scale=rstd[:, i:i + 1]).then_inc(normed_x, 1)

            def turn_halves(t):
                for k in range(KC):
                    act.wait_ge(turn_full, KC * t + k + 1)
                    act.activation(xt[:, 0, k], turn_bank[k % 2][:, :], ACT.Copy).then_inc(turn_hi, 1)

            def split(s, j):
                act.wait_ge(w_in[j % RING], 16 * (CH // RING * s + j // RING + 1))
                if not (isinstance(s, int) and s == 0):
                    act.wait_ge(piece_done, CH * s + j - CH + 1)
                act.activation(w_hl[:, 0, j], stage[:, j % RING, 0:2 * D], ACT.Copy).then_inc(w_split, 1)

            def split_ahead(s, j, more):
                if j + AHEAD < CH:
                    if routed or (isinstance(s, int) and s == 0):
                        split(s, j + AHEAD)
                elif routed and more:
                    split(s + 1, j + AHEAD - CH)

            for j in range(AHEAD):
                split(0, j)
            norm(0)
            turn_halves(0)

            def body(s, more):
                for j in range(CH):
                    split_ahead(s, j, more)
                    if j == 11 and more:
                        norm(s + 1)
                    act.wait_ge(hid_full, CH * s + j + 1)
                    if not (isinstance(s, int) and CH * s + j < 2):
                        act.wait_ge(piece_done, CH * s + j - 1)
                    for dst in (hidden[:, j % 2], h_hl[:, j % 2, 0]):
                        last = act.activation(dst, hid_bank[j % 2][:, :], ACT.Relu, bias=b1[:, j:j + 1])
                    last.then_inc(hid_hi, 1)
                if more:
                    turn_halves(s + 1)
            tiles_loop(act, 1, body)

        @block.vector
        def _(dve):
            dve.wait_ge(gate_done, 1)

            def norm_stats(t):
                dve.wait_ge(x_loaded, LOADS * (t + 1))
                if not (isinstance(t, int) and t == 0):
                    dve.wait_ge(normed_x, SUB * t)
                for i in range(SUB):
                    last = dve.bn_stats(stats[:, i, :], x[:, i, :])
                last.then_inc(norm_chain, 1)
                dve.wait_ge(norm_chain, 2 * t + 1)
                dve.tensor_copy(waited[:, :], stats[:, 0, 0:1])
                for i in range(SUB):
                    last = dve.bn_aggr(mean_var[:, i, :], stats[:, i, :])
                last.then_inc(norm_chain, 1)

            def norm_shift(t):
                dve.wait_ge(rstd_done, 2 * t + 2)
                dve.scalar_tensor_tensor(out=shift[:, :], in0=mean_var[:, :, 0], scalar=-1.0,
                                         in1=rstd[:, :], op0=ALU.mult, op1=ALU.mult).then_inc(norm_ready, 1)

            def gate_scores(t):
                dve.wait_ge(normed_x, SUB * (t + 1))
                for i in range(SUB):
                    for e in range(2):
                        last = dve.tensor_tensor_reduce(product[:, e, :], x[:, i, :], gate_rows[:, e, :], 1.0, 0.0,
                                                        ALU.mult, ALU.add, score[:, i, e:e + 1])
                    last.then_inc(scored, 1)
                    dve.wait_ge(scored, SUB * t + i + 1)
                dve.tensor_tensor(is_second[:, bass.ds(t * SUB, SUB)], score[:, :, 1], score[:, :, 0],
                                  ALU.is_gt).then_inc(chosen, 1)

            def turn_los(t):
                for k in range(KC):
                    dve.wait_ge(turn_hi, KC * t + k + 1)
                    dve.tensor_tensor(xt[:, 1, k], turn_bank[k % 2][:, :], xt[:, 0, k].bitcast(F32),
                                      ALU.subtract).then_inc(turn_free, 1)

            norm_stats(0)
            norm_shift(0)
            turn_los(0)
            if not routed:
                gate_scores(0)

            def body(s, more):
                for j in range(CH):
                    if more and j == 8:
                        norm_stats(s + 1)
                    if more and j == 10:
                        norm_shift(s + 1)
                    if more and j == 13 and not routed:
                        gate_scores(s + 1)
                    dve.wait_ge(hid_hi, CH * s + j + 1)
                    dve.tensor_tensor(h_hl[:, j % 2, 1], hidden[:, j % 2], h_hl[:, j % 2, 0].bitcast(F32),
                                      ALU.subtract).then_inc(hid_ready, 1)
                    if routed and j == 6:
                        dve.wait_ge(fall_in, 16 * (s + 1))
                        dve.wait_ge(res_loaded, LOADS * (s + 1))
                        dve.tensor_tensor(res[:], res[:], fall[:, :].unsqueeze(1).to_broadcast([P, SUB, D]),
                                          ALU.add).then_inc(fall_added, 1)
                if more:
                    turn_los(s + 1)
                if routed:
                    dve.wait_ge(fall_added, s + 1)
                else:
                    dve.wait_ge(res_loaded, LOADS * (s + 1))
                dve.wait_ge(piece_done, CH * (s + 1))
                for i in range(SUB):
                    dve.scalar_tensor_tensor(out=res[:, i], in0=out_bank[i][:, :], scalar=gate[:, 2:3],
                                             in1=res[:, i], op0=ALU.mult, op1=ALU.add).then_inc(out_ready, 1)
            tiles_loop(dve, 1, body)

        @block.tensor
        def _(pe):
            pe.wait_ge(made, 2)

            def turn(t):
                pe.wait_ge(normed_x, SUB * (t + 1))
                for k in range(KC):
                    if not (isinstance(t, int) and KC * t + k < 2):
                        pe.wait_ge(turn_free, KC * t + k - 1)
                    for i in range(SUB):
                        mm = pe.transpose(turn_bank[k % 2][:, i * P:(i + 1) * P], x[:, i, k * P:(k + 1) * P],
                                          ident[:, :])
                    mm.then_inc(turn_full, 1)

            def up(s, j):
                pe.wait_ge(w_ready, CH * s + j + 1 if routed else j + 1)
                if not (isinstance(s, int) and CH * s + j < 2):
                    pe.wait_ge(hid_ready, CH * s + j - 1)
                if j == 0:
                    pe.wait_ge(turn_free, KC * (s + 1))
                for k in range(KC):
                    mm = product3(pe, hid_bank[j % 2][:, :], [w_hl[:, h, j, k * P:(k + 1) * P] for h in range(2)],
                                  [xt[:, h, k] for h in range(2)], k == 0, k == KC - 1)
                mm.then_inc(hid_full, 1)

            def down(s, j):
                pe.wait_ge(hid_ready, CH * s + j + 1)
                if j == 0 and not (isinstance(s, int) and s == 0):
                    pe.wait_ge(out_ready, SUB * s)
                for i in range(SUB):
                    mm = product3(pe, out_bank[i][:, :], [h_hl[:, j % 2, h, i * P:(i + 1) * P] for h in range(2)],
                                  [w_hl[:, h, j, D:2 * D] for h in range(2)], j == 0, j == CH - 1)
                mm.then_inc(piece_done, 1)

            turn(0)

            def body(s, more):
                up(s, 0)
                for j in range(CH):
                    if j + 1 < CH:
                        up(s, j + 1)
                    if j == CH - 2 and more:
                        turn(s + 1)
                    down(s, j)
            tiles_loop(pe, 1, body)


def make_order(nc, is_second, order, expert_dram, x1, x1s):
    with ExitStack() as ctx:
        sb, ps, sem = allocators(nc, ctx, "or_")
        upto = sb("upto", [P, P])
        ones = sb("ones", [P, P])
        inside = sb("inside", [P, GROUPS])
        totals = sb("totals", [P, GROUPS])
        before = sb("before", [P, GROUPS])
        zero = sb("zero", [P, GROUPS])
        rank = sb("rank", [P, GROUPS])
        token = sb("token", [P, GROUPS], I32)
        token_f = sb("token_f", [P, GROUPS])
        spot = sb("spot", [P, GROUPS])
        place = sb("place", [P, GROUPS], I32)
        spare = sb("spare", [SLOTS, TILE], I32)
        start = sb("start", [1, SLOTS], I32)
        start_f = sb("start_f", [1, SLOTS])
        flag = sb("flag", [1, SLOTS])
        flag_i = sb("flag_i", [1, SLOTS], I32)
        blank = sb("blank", [P, SUB, D])
        rank_bank, total_bank = ps("rank_bank"), ps("total_bank")
        made, counted, chain, spare_out, scattered, stored = (
            sem(n) for n in ("made", "counted", "chain", "spare_out", "scattered", "stored"))
        PLACED, FLAGGED = 10, 13
        block = ctx.enter_context(nc.Block())

        @block.gpsimd
        def _(pool):
            pool.memset(upto[:, :], 1.0).then_inc(made, 1)
            pool.memset(ones[:, :], 1.0).then_inc(made, 1)
            pool.memset(blank[:], 0.0).then_inc(made, 1)
            pool.memset(zero[:, :], 0.0).then_inc(made, 1)
            pool.iota(token[:, :], pattern=[[P, GROUPS]], base=0, channel_multiplier=1).then_inc(made, 1)
            pool.iota(spare[:, :], pattern=[[1, TILE]], base=TOK, channel_multiplier=0).then_inc(made, 1)
            pool.iota(start[:, :], pattern=[[TILE, SLOTS]], base=0, channel_multiplier=0).then_inc(made, 1)
            pool.wait_ge(made, 7)
            pool.affine_select(out=upto[:, :], in_=upto[:, :], compare_op=ALU.is_ge, fill=0.0,
                               base=0, pattern=[[1, P]], channel_multiplier=-1).then_inc(made, 1)
            pool.wait_ge(spare_out, 16)
            pool.wait_ge(chain, PLACED)
            for g in range(GROUPS):
                pool.indirect_dma_start(
                    out=order, out_offset=bass.IndirectOffsetOnAxis(ap=place[:, g:g + 1], axis=0),
                    in_=token[:, g:g + 1], in_offset=None).then_inc(scattered, 16)
            pool.wait_ge(scattered, 16 * GROUPS)

        @block.tensor
        def _(pe):
            pe.wait_ge(made, 8)
            pe.matmul(rank_bank[:, 0:GROUPS], upto[:, :], is_second[:, :], start=True, stop=True).then_inc(counted, 1)
            pe.matmul(total_bank[:, 0:GROUPS], ones[:, :], is_second[:, :], start=True, stop=True).then_inc(counted, 1)

        @block.vector
        def _(dve):
            done = [0]

            def link(ins):
                done[0] += 1
                ins.then_inc(chain, 1)
                dve.wait_ge(chain, done[0])
            dve.wait_ge(made, 8)
            dve.wait_ge(counted, 2)
            link(dve.tensor_copy(totals[:, :], total_bank[:, 0:GROUPS]))
            link(dve.tensor_tensor_scan(before[:, :], totals[:, :], zero[:, :], 0.0, ALU.add, ALU.add))
            link(dve.tensor_tensor(rank[:, :], before[:, :], totals[:, :], ALU.subtract))
            link(dve.tensor_tensor(rank[:, :], rank_bank[:, 0:GROUPS], rank[:, :], ALU.add))
            link(dve.tensor_copy(token_f[:, :], token[:, :]))
            link(dve.tensor_scalar(spot[:, :], token_f[:, :], -1.0, float(LIST), ALU.mult, ALU.add))
            link(dve.tensor_tensor(spot[:, :], spot[:, :], is_second[:, :], ALU.mult))
            link(dve.tensor_tensor(spot[:, :], spot[:, :], token_f[:, :], ALU.add))
            link(dve.tensor_tensor(spot[:, :], spot[:, :], rank[:, :], ALU.subtract))
            link(dve.tensor_copy(place[:, :], spot[:, :]))
            link(dve.tensor_copy(start_f[:, :], start[:, :]))
            link(dve.tensor_scalar(flag[:, :], start_f[:, :], before[0:1, GROUPS - 1:GROUPS], float(TOK),
                                   ALU.add, ALU.is_ge))
            link(dve.tensor_copy(flag_i[:, :], flag[:, :]))

        @block.sync
        def _(sp):
            sp.wait_ge(made, 7)
            sp.dma_start(order.rearrange("(s r) o -> s (r o)", s=SLOTS), spare[:, :]).then_inc(spare_out, 16)
            for rows in (x1, x1s):
                sp.dma_start(rows[TOK:LIST, :].rearrange("(s p) d -> p s d", p=P), blank[:]).then_inc(stored, 16)
            sp.wait_ge(chain, FLAGGED)
            sp.dma_start(expert_dram, flag_i[:, :]).then_inc(stored, 16)
            sp.wait_ge(stored, 48)


def program(nc, x, ctx_t, gates, wq, wk, wv, wo, bq, bk, bv, rows1, gate_w, w_all, mlp_rows, out):
    def dram(name, shape, dt=F32):
        return nc.dram_tensor(name, shape, dt, kind="Internal").ap()
    k_dram = dram("k_dram", (2, BATCH, P, 2048))
    v_dram = dram("v_dram", (2, BATCH, P, 2048))
    x1 = dram("x1", (LIST, D))
    x1s = dram("x1s", (LIST, D))
    x2 = dram("x2", (LIST, D))
    order = dram("order", (LIST, 1), I32)
    expert = dram("expert", (1, SLOTS), I32)
    fallback = dram("fallback", (2, P, D))
    fallback_rows(nc, w_all, mlp_rows, gates, fallback)
    context(nc, ctx_t, wk, wv, bk, bv, k_dram, v_dram)
    attention(nc, 0, x, x1, wq[0], wo[0], bq[0], gates, k_dram[0], v_dram[0], None)
    with nc.sbuf_tensor("is_second", [P, GROUPS], F32) as is_second:
        mlp(nc, False, x1, x1, x1s, w_all, gates, gate_w, is_second, None, None, None)
        make_order(nc, is_second, order, expert, x1, x1s)
    mlp(nc, True, x1, x1s, x2, w_all, gates, None, None, order, expert, fallback)
    attention(nc, 1, x2, out, wq[1], wo[1], bq[1], gates, k_dram[1], v_dram[1], rows1)


def kernel(**inputs):
    import numpy as np
    import concourse.bacc as bacc
    from concourse.bass_utils import run_bass_kernel_spmd

    def merged(w):
        return w.transpose(1, 0, 2).reshape(D, D)

    def columns(b):
        return b.reshape(KC, P).T
    i = {k: np.asarray(v) for k, v in inputs.items()}
    none = np.zeros(D, np.float32)
    w1 = np.stack([i["L0_ffn_sw1"], *i["L0_ffn_w1"]])
    w2 = np.stack([i["L0_ffn_sw2"], *i["L0_ffn_w2"]])
    b1 = np.stack([i["L0_ffn_sb1"], *i["L0_ffn_b1"]])
    w_all = np.concatenate([
        w1.reshape(3, KC, P, CH, P).transpose(0, 3, 2, 1, 4).reshape(3, CH, P, D),
        w2.reshape(3, CH, P, D), b1.reshape(3, CH, P, 1)], axis=3)
    arrays = {
        "x": i["x"].reshape(TOK, D),
        "ctx_t": i["ctx_1024"].transpose(2, 0, 1).reshape(D, BATCH * KEYS),
        "gates": np.concatenate([i["g_xattn"], i["g_ffn"]]).reshape(1, 4),
        "wq": np.stack([i["L0_xattn_Wq"].T, merged(i["L1_xattn_Wq"])]),
        "wk": np.stack([i["L0_xattn_Wk"].T, merged(i["L1_xattn_Wk"])]),
        "wv": np.stack([i["L0_xattn_Wv"].T, merged(i["L1_xattn_Wv"])]),
        "wo": np.stack([i["L0_xattn_Wo"].T, i["L1_xattn_Wo"]]),
        "bq": np.stack([columns(none), columns(i["L1_xattn_bq"].reshape(D))]),
        "bk": np.stack([columns(none), columns(i["L1_xattn_bk"].reshape(D))]),
        "bv": np.stack([none, i["L1_xattn_bv"].reshape(D)]).reshape(2, 1, D),
        "rows1": np.stack([i["L1_xattn_bo"], i["L1_ffn_ln_g"], i["L1_ffn_ln_b"]]),
        "gate_w": i["L0_ffn_gate_w"],
        "w_all": w_all,
        "mlp_rows": np.stack([i["L0_ffn_sb2"], *i["L0_ffn_b2"]]),
    }
    arrays = {k: np.ascontiguousarray(v) for k, v in arrays.items()}
    nc = bacc.Bacc("TRN2", target_bir_lowering=False, num_devices=1)
    args = {k: nc.dram_tensor(k, v.shape, mybir.dt.from_np(v.dtype), kind="ExternalInput").ap()
            for k, v in arrays.items()}
    out = nc.dram_tensor("out", (TOK, D), F32, kind="ExternalOutput").ap()
    program(nc, **args, out=out)
    r = run_bass_kernel_spmd(nc, [arrays], core_ids=[0])
    return r.results[0]["out"].reshape(BATCH, SEQ, D)
```

```python
from contextlib import ExitStack

import concourse.bass as bass
from concourse import mybir

F32 = mybir.dt.float32
F32R = mybir.dt.float32r
I32 = mybir.dt.int32
ALU = mybir.AluOpType
ACT = mybir.ActivationFunctionType
AX = mybir.AxisListType

P = 128
BATCH, SEQ, D = 4, 1024, 512
KEYS = 64
HEADS, HD = 16, 32
HIDDEN = 2048
TOK = BATCH * SEQ
TILE = 512
SUB = TILE // P
KC = D // P
NT = TOK // TILE
TPB = SEQ // TILE
CH = HIDDEN // P
WCOL = 2 * D + 1
SLOTS = NT + 1
LIST = SLOTS * TILE
GROUPS = TOK // P
SCALE = HD ** -0.5
NEG = -1e9
EPS = 1e-5


def allocators(nc, ctx, prefix):
    sems = []

    def clear():
        nc.clear_and_free_semaphores(sems)
        nc.all_engine_barrier()
    ctx.callback(clear)

    def sb(name, shape, dt=F32):
        return ctx.enter_context(nc.sbuf_tensor(prefix + name, shape, dt))

    def ps(name, cols=512):
        return ctx.enter_context(nc.psum_tensor(prefix + name, [P, cols], F32))

    def sem(name):
        sems.append(nc.alloc_semaphore(prefix + name))
        return sems[-1]
    return sb, ps, sem


def product3(pe, out, w, x, start, stop):
    pe.matmul(out, w[0], x[1], start=start, stop=False)
    pe.matmul(out, w[0], x[0], start=False, stop=False)
    return pe.matmul(out, w[1], x[0], start=False, stop=stop)


def diagonal(pool, m, made):
    pool.memset(m[:, :], 0.0).then_inc(made, 1)
    pool.wait_ge(made, 1)
    pool.affine_select(out=m[:, :], in_=m[:, :], compare_op=ALU.not_equal, fill=1.0,
                       base=0, pattern=[[-1, P]], channel_multiplier=1).then_inc(made, 1)


def context(nc, ctx_t, wk, wv, bk, bv, k_out, v_out, order, spare_rows):
    with ExitStack() as ctx:
        sb, ps, sem = allocators(nc, ctx, "cx_")
        raw = sb("raw", [P, KC, BATCH, KEYS])
        c_hl = [sb("c_" + n, [P, KC, BATCH, 2, KEYS], F32R) for n in ("hi", "lo")]
        w_raw = sb("w_raw", [P, 2, KC, D])
        w_hl = [sb("w_" + n, [P, 2, KC, D], F32R) for n in ("hi", "lo")]
        bias_k = sb("bias_k", [P, 2, KC])
        bias_v = sb("bias_v", [P, 2, D])
        value = sb("value", [P, 2, D])
        k_all = sb("k_all", [P, 2, BATCH, 2, KC, 4 * KEYS], F32R)
        v_all = sb("v_all", [P, BATCH, 2, KC, 2, P], F32R)
        spare = sb("spare", [SLOTS, TILE], I32)
        blank = sb("blank", [P, D])
        bank = [ps(f"bank{n}") for n in range(4)]
        filled, ctx_in, small_in, cleared, hi_done, lo_done, full, k_hi, biased, v_hi, built, k_stored = (
            sem(n) for n in ("filled", "ctx_in", "small_in", "cleared", "hi_done", "lo_done", "full",
                             "k_hi", "biased", "v_hi", "built", "k_stored"))
        w_in = [sem(f"w_in{n}") for n in range(2)]
        v_stored = [sem(f"v_stored{b}") for b in range(BATCH)]
        USES = KC + BATCH
        block = ctx.enter_context(nc.Block())

        def v_parts():
            for half in range(2):
                for j in range(2):
                    yield slice(KEYS * half, KEYS * half + KEYS), j, half, j * 64 + half * HD

        @block.sync
        def _(sp):
            def weights(l):
                for n, w in enumerate((wk, wv)):
                    sp.dma_start(w_raw[:, n], w[l].rearrange("(k p) n -> p k n", p=P)).then_inc(w_in[n], 16)

            sp.dma_start(raw[:], ctx_t.rearrange("(k p) (b s) -> p k b s", p=P, b=BATCH)).then_inc(ctx_in, 16)
            for l in range(2):
                if l == 1:
                    weights(0)
                sp.dma_start(bias_k[:, l, :], bk[l]).then_inc(small_in, 16)
                sp.dma_start(bias_v[:, l, :], bv[l].to_broadcast([P, D])).then_inc(small_in, 16)
            sp.wait_ge(lo_done, 3)
            weights(1)
            sp.wait_ge(cleared, 4)
            sp.dma_start(order.rearrange("(s r) o -> s (r o)", s=SLOTS), spare[:, :]).then_inc(filled, 16)
            for rows in spare_rows:
                sp.dma_start(rows.rearrange("(s p) d -> p s d", p=P), blank[:, :].unsqueeze(1).to_broadcast([P, SUB, D])).then_inc(filled, 16)
            for l in range(2):
                for b in range(BATCH):
                    sp.wait_ge(built, USES * l + KC)
                    sp.dma_start(k_out[l, b], k_all[:, l, b].bitcast(F32).rearrange("p h g n -> p (h g n)")).then_inc(k_stored, 16)
                for b in range(BATCH):
                    sp.wait_ge(built, USES * l + KC + b + 1)
                    sp.dma_start(v_out[l, b], v_all[:, b].bitcast(F32).rearrange("p h g j n -> p (h g j n)")).then_inc(v_stored[b], 16)
            sp.wait_ge(k_stored, 2 * BATCH * 16)
            for b in range(BATCH):
                sp.wait_ge(v_stored[b], 32)
            sp.wait_ge(filled, 16 + 16 * len(spare_rows))

        @block.gpsimd
        def _(pool):
            pool.memset(k_all[:].bitcast(F32), 0.0).then_inc(cleared, 1)
            pool.memset(v_all[:].bitcast(F32), 0.0).then_inc(cleared, 1)
            pool.memset(blank[:], 0.0).then_inc(cleared, 1)
            pool.iota(spare[:, :], pattern=[[1, TILE]], base=TOK, channel_multiplier=0).then_inc(cleared, 1)

        @block.scalar
        def _(act):
            def split(l, n):
                act.wait_ge(w_in[n], 16 * (l + 1))
                if l:
                    act.wait_ge(full, KC if n == 0 else USES)
                act.activation(w_hl[0][:, n], w_raw[:, n], ACT.Copy).then_inc(hi_done, 1)

            act.wait_ge(ctx_in, 16)
            for twice in range(2):
                last = act.activation(c_hl[0][:, :, :, twice, :], raw[:], ACT.Copy)
            last.then_inc(hi_done, 1)
            split(0, 0)
            split(0, 1)
            act.wait_ge(small_in, 64)
            act.wait_ge(cleared, 3)
            for l in range(2):
                for g in range(KC):
                    act.wait_ge(full, USES * l + g + 1)
                    for h in range(4):
                        rows = slice(HD * h, HD * h + HD)
                        last = act.activation(
                            k_all[rows, l, :, 0, g, h * KEYS:(h + 1) * KEYS],
                            bank[g][rows, 0:BATCH * KEYS].rearrange("p (b s) -> p b s", b=BATCH),
                            ACT.Identity, bias=bias_k[rows, l, g:g + 1])
                    last.then_inc(k_hi, 1)
                if l == 0:
                    split(1, 0)
                for b in range(BATCH):
                    act.wait_ge(biased, BATCH * l + b + 1)
                    if l:
                        act.wait_ge(v_stored[b], 16)
                    for rows, j, half, at in v_parts():
                        src = value[rows, b % 2].rearrange("p (g j h c) -> p g j h c", g=KC, j=2, h=2)
                        last = act.activation(v_all[rows, b, 0, :, j, at:at + HD], src[:, :, j, half, :], ACT.Copy)
                    last.then_inc(v_hi, 1)
                if l == 0:
                    split(1, 1)

        @block.vector
        def _(dve):
            def split(l, n):
                dve.wait_ge(hi_done, 2 + 2 * l + n)
                dve.tensor_tensor(w_hl[1][:, n].rearrange("p k n -> p (k n)"), w_raw[:, n].rearrange("p k n -> p (k n)"),
                                  w_hl[0][:, n].bitcast(F32).rearrange("p k n -> p (k n)"),
                                  ALU.subtract).then_inc(lo_done, 1)

            dve.wait_ge(hi_done, 1)
            for twice in range(2):
                last = dve.tensor_tensor(c_hl[1][:, :, :, twice, :], raw[:], c_hl[0][:, :, :, twice, :].bitcast(F32),
                                         ALU.subtract)
            last.then_inc(lo_done, 1)
            split(0, 0)
            split(0, 1)
            dve.wait_ge(small_in, 64)
            for l in range(2):
                for g in range(KC):
                    dve.wait_ge(k_hi, KC * l + g + 1)
                    for h in range(4):
                        rows = slice(HD * h, HD * h + HD)
                        last = dve.scalar_tensor_tensor(
                            out=k_all[rows, l, :, 1, g, h * KEYS:(h + 1) * KEYS],
                            in0=bank[g][rows, 0:BATCH * KEYS].rearrange("p (b s) -> p b s", b=BATCH),
                            scalar=bias_k[rows, l, g:g + 1],
                            in1=k_all[rows, l, :, 0, g, h * KEYS:(h + 1) * KEYS].bitcast(F32),
                            op0=ALU.add, op1=ALU.subtract)
                    last.then_inc(built, 1)
                if l == 0:
                    split(1, 0)
                for b in range(BATCH):
                    dve.wait_ge(full, USES * l + KC + b + 1)
                    dve.tensor_tensor(value[:, b % 2, :], bank[b][:, :], bias_v[:, l, :],
                                      ALU.add).then_inc(biased, 1)
                    dve.wait_ge(v_hi, BATCH * l + b + 1)
                    for rows, j, half, at in v_parts():
                        src = value[rows, b % 2].rearrange("p (g j h c) -> p g j h c", g=KC, j=2, h=2)
                        last = dve.tensor_tensor(v_all[rows, b, 1, :, j, at:at + HD], src[:, :, j, half, :],
                                                 v_all[rows, b, 0, :, j, at:at + HD].bitcast(F32), ALU.subtract)
                    last.then_inc(built, 1)
                if l == 0:
                    split(1, 1)

        @block.tensor
        def _(pe):
            for l in range(2):
                pe.wait_ge(lo_done, 2 + 2 * l)
                for g in range(KC):
                    if l:
                        pe.wait_ge(built, USES * l - BATCH + g + 1)
                    cols = slice(g * P, (g + 1) * P)
                    for k in range(KC):
                        mm = product3(pe, bank[g][:, 0:BATCH * KEYS], [w[:, 0, k, cols] for w in w_hl],
                                      [c[:, k, :, 0, :] for c in c_hl], k == 0, k == KC - 1)
                    mm.then_inc(full, 1)
                pe.wait_ge(lo_done, 3 + 2 * l)
                for b in range(BATCH):
                    pe.wait_ge(built, USES * l + b + 1)
                    for k in range(KC):
                        mm = product3(pe, bank[b][:, :], [c[:, k, b].rearrange("p t s -> p (t s)") for c in c_hl],
                                      [w[:, 1, k, :] for w in w_hl], k == 0, k == KC - 1)
                    mm.then_inc(full, 1)


def attention(nc, layer, x_in, x_out, wq, wo, bq, gates, k_dram, v_dram, row_dram):
    final = row_dram is not None
    xv = x_in[0:TOK, :].rearrange("(t s p) d -> t p s d", s=SUB, p=P)
    ov = x_out[0:TOK, :].rearrange("(t s p) d -> t p s d", s=SUB, p=P)
    with ExitStack() as ctx:
        sb, ps, sem = allocators(nc, ctx, f"a{layer}_")
        wq_hl = sb("wq", [P, 2, KC, D], F32R)
        wo_hl = sb("wo", [P, 2, KC, D], F32R)
        x = sb("x", [P, 2, SUB, D])
        xt = sb("xt", [P, 2, KC, TILE], F32R)
        qt = sb("qt", [P, 2, KC, TILE], F32R)
        prob = sb("prob", [P, 2, SUB, HEADS, KEYS])
        prob_t = sb("prob_t", [P, 4, 2, TILE], F32R)
        heads_t = sb("heads_t", [P, 2, KC, TILE], F32R)
        res = sb("res", [P, 2, SUB, D])
        kbd = sb("kbd", [P, 2, KC, 4 * KEYS], F32R)
        vbd = sb("vbd", [P, 2, KC, 2, P], F32R)
        ident = sb("ident", [P, P])
        mask = sb("mask", [P, KEYS])
        gate_in = sb("gate_in", [P, 4])
        gate = sb("gate", [P, 4])
        bias_q = sb("bias_q", [P, KC])
        stats = sb("stats", [P, SUB, 6])
        waited = sb("waited", [P, 1])
        mean_var = sb("mean_var", [P, SUB, 2])
        rstd = sb("rstd", [P, SUB])
        minus_half, eps, zero = (sb(n, [P, SUB]) for n in ("minus_half", "eps", "zero"))
        shift = sb("shift", [P, SUB])
        top = sb("top", [P, SUB, HEADS])
        mass = sb("mass", [P, SUB, HEADS])
        inv = sb("inv", [P, SUB, HEADS])
        if final:
            rows = sb("rows", [P, 3, D])
            normed = sb("normed", [P, SUB, D])
            f_stats = sb("f_stats", [P, SUB, 6])
            f_waited = sb("f_waited", [P, 1])
            f_mv = sb("f_mv", [P, SUB, 2])
            f_rstd, f_var, f_rstd2, f_scale, f_shift = (
                sb(n, [P, SUB]) for n in ("f_rstd", "f_var", "f_rstd2", "f_scale", "f_shift"))
        score_bank = [ps(f"score{i}", HEADS * KEYS) for i in range(2)]
        bank = [ps(f"bank{i}") for i in range(4)]
        (small_in, w_hi, w_ready, made, gate_done, rows_done, k_loaded, v_loaded, stored, normed_x,
         norm_chain, rstd_done, norm_ready, full, free, hi_done, score_full, masked, maxed, score_free, exp_done,
         summed, inv_done, prob_ready, res_biased, f_chain, f_done, f_ready, f_normed, f_scaled, out_ready) = (
            sem(n) for n in (
                "small_in", "w_hi", "w_ready", "made", "gate_done", "rows_done", "k_loaded", "v_loaded",
                "stored", "normed_x", "norm_chain", "rstd_done", "norm_ready", "full", "free", "hi_done", "score_full",
                "masked", "maxed", "score_free", "exp_done", "summed", "inv_done", "prob_ready",
                "res_biased", "f_chain", "f_done", "f_ready", "f_normed", "f_scaled", "out_ready"))
        w_in = [sem(f"w_in{n}") for n in range(2)]
        x_loaded = [sem(f"x_loaded{n}") for n in range(2)]
        res_loaded = [sem(f"res_loaded{n}") for n in range(2)]

        TURN, PV, XT, OUT, QT = "turn", "pv", "xt", "out", "qt"
        HEAD = [(TURN, 0), (TURN, 1)]
        for i in range(1, SUB):
            HEAD += [(TURN, 2 * i), (TURN, 2 * i + 1), (PV, i - 1)]
        SCORES = {(TURN, 2): 0, (PV, 3): 1, (OUT, 1): 2, (OUT, 3): 3}
        EXPONENT = {(TURN, 4): 0, (OUT, 0): 1, (OUT, 3): 2}
        NORM = {(TURN, 6): 0, (TURN, 7): 1, (PV, 2): 2, (XT, 0): 3}
        LAST_NORM = {(TURN, 4): 0, (TURN, 5): 1, (PV, 1): 2, (TURN, 7): 3}
        SUM = {(TURN, 6): 0, (OUT, 0): 1, (OUT, 2): 2}
        FULL_STEP = (HEAD + [(XT, 0), (XT, 1), (PV, 3), (XT, 2), (XT, 3)]
                     + [(OUT, i) for i in range(4)] + [(QT, i) for i in range(4)])
        TAIL_STEP = HEAD + [(PV, 3)] + [(OUT, i) for i in range(4)]
        OPENING = [(XT, i) for i in range(4)] + [(QT, i) for i in range(4)]
        N_OPEN, N_STEP, N_TAIL = len(OPENING), len(FULL_STEP), len(TAIL_STEP)
        N_OUT = SUB
        PEELED = 2
        LOOP_END = NT - 2

        class Step:

            def __init__(self, u, par, pair, first_use, first_hi, plan, has_v, has_w, has_last):
                self.u, self.par, self.pair = u, par, pair
                self.use, self.hi, self.plan = first_use, first_hi, plan
                self.has_v, self.has_w, self.has_last = has_v, has_w, has_last
                self.had_w = has_w or has_v

            def after(self, what):
                return self.use + self.plan.index(what) + 1

        def steps(eng, opening, step):
            def in_order(u, par, pair):
                return Step(u, par, pair, 2 * N_OPEN + N_STEP * u, 2 * N_OPEN + (N_STEP - N_OUT) * u,
                            FULL_STEP, True, True, not (isinstance(u, int) and u == 0))
            opening()
            for u in range(PEELED):
                step(in_order(u, u % 2, u // 2))
            with eng.Fori(PEELED // 2, LOOP_END // 2) as pair:
                for par in range(2):
                    step(in_order(pair * 2 + par, par, pair))
            use = 2 * N_OPEN + N_STEP * LOOP_END
            hi = 2 * N_OPEN + (N_STEP - N_OUT) * LOOP_END
            step(Step(NT - 2, 0, NT // 2 - 1, use, hi, TAIL_STEP, True, False, True))
            step(Step(NT - 1, 1, NT // 2 - 1, use + N_TAIL, hi + N_TAIL - N_OUT, TAIL_STEP, False, False, True))

        block = ctx.enter_context(nc.Block())

        @block.sync
        def _(sp):
            sp.dma_start(res[:, 0], wq.rearrange("(k p) n -> p k n", p=P)).then_inc(w_in[0], 16)
            sp.dma_start(x[:, 0], xv[0]).then_inc(x_loaded[0], 16)
            sp.dma_start(x[:, 1], xv[1]).then_inc(x_loaded[1], 16)
            sp.dma_start(gate_in[:, :], gates.to_broadcast([P, 4])).then_inc(small_in, 16)
            sp.dma_start(bias_q[:, :], bq).then_inc(small_in, 16)
            if final:
                for r in range(3):
                    sp.dma_start(rows[:, r, :], row_dram[r:r + 1, :].to_broadcast([P, D])).then_inc(small_in, 16)
            sp.dma_start(res[:, 1], wo.rearrange("(k p) n -> p k n", p=P)).then_inc(w_in[1], 16)
            sp.dma_start(kbd[:].bitcast(F32).rearrange("p h g n -> p (h g n)"), k_dram[0]).then_inc(k_loaded, 16)
            sp.dma_start(vbd[:].bitcast(F32).rearrange("p h g j n -> p (h g j n)"), v_dram[0]).then_inc(v_loaded, 16)
            for t in range(2):
                sp.wait_ge(w_ready, t + 1)
                sp.dma_start(res[:, t], xv[t]).then_inc(res_loaded[t], 16)

            def step(s):
                if s.has_w:
                    sp.wait_ge(full, s.use - 8)
                    sp.dma_start(x[:, s.par], xv[s.u + 2]).then_inc(x_loaded[s.par], 16)
                if s.has_last:
                    if final:
                        sp.wait_ge(out_ready, SUB * s.u)
                    else:
                        sp.wait_ge(free, s.use - 4 * s.had_w)
                    sp.dma_start(ov[s.u - 1], res[:, 1 - s.par]).then_inc(stored, 16)
                if s.has_last and s.has_v:
                    sp.wait_ge(stored, 16 * s.u)
                    sp.dma_start(res[:, 1 - s.par], xv[s.u + 1]).then_inc(res_loaded[1 - s.par], 16)
                if s.has_v and s.par == 1:
                    sp.wait_ge(full, s.after((PV, 3)))
                    sp.dma_start(vbd[:].bitcast(F32).rearrange("p h g j n -> p (h g j n)"), v_dram[s.pair + 1]).then_inc(v_loaded, 16)

                if s.has_w and s.par == 0:
                    sp.wait_ge(score_full, SUB * (s.u + 2))
                    sp.dma_start(kbd[:].bitcast(F32).rearrange("p h g n -> p (h g n)"), k_dram[s.pair + 1]).then_inc(k_loaded, 16)

            steps(sp, lambda: None, step)
            if final:
                sp.wait_ge(out_ready, SUB * NT)
            else:
                sp.wait_ge(free, 2 * N_OPEN + N_STEP * LOOP_END + 2 * N_TAIL)
            sp.dma_start(ov[NT - 1], res[:, (NT - 1) % 2]).then_inc(stored, 16)
            sp.wait_ge(stored, 16 * NT)

        @block.gpsimd
        def _(pool):
            diagonal(pool, ident, made)
            pool.memset(mask[:, :], 0.0).then_inc(made, 1)
            pool.wait_ge(made, 3)
            pool.affine_select(out=mask[:, :], in_=mask[:, :], compare_op=ALU.is_ge, fill=NEG / SCALE,
                               base=0, pattern=[[-1, KEYS]], channel_multiplier=1).then_inc(made, 1)
            for m, value in ((minus_half, -0.5), (eps, EPS), (zero, 0.0)):
                pool.memset(m[:, :], value).then_inc(made, 1)
            pool.wait_ge(made, 7)

            def normalise(v, par, i):
                pool.wait_ge(inv_done, SUB * v + i + 1)
                pool.tensor_tensor(prob[:, par, i], prob[:, par, i],
                                   inv[:, i, :].unsqueeze(2).to_broadcast([P, HEADS, KEYS]),
                                   ALU.mult).then_inc(prob_ready, 1)

            def norm_rstd(t):
                pool.wait_ge(norm_chain, (SUB + 1) * (t + 1))
                pool.tensor_tensor(rstd[:, :], mean_var[:, :, 1], eps[:, :], ALU.add).then_inc(rstd_done, 1)
                pool.wait_ge(rstd_done, 2 * t + 1)
                pool.tensor_tensor(rstd[:, :], rstd[:, :], minus_half[:, :], ALU.pow).then_inc(rstd_done, 1)

            def last_norm_scale(t):
                pool.wait_ge(f_chain, (SUB + 1) * (t + 1))
                if not (isinstance(t, int) and t == 0):
                    pool.wait_ge(f_normed, SUB * t)

                def then(ins, k):
                    ins.then_inc(f_done, 1)
                    pool.wait_ge(f_done, 8 * t + k)
                then(pool.tensor_tensor(f_var[:, :], f_mv[:, :, 1], eps[:, :], ALU.add), 1)
                then(pool.tensor_tensor(f_rstd[:, :], f_var[:, :], minus_half[:, :], ALU.pow), 2)
                then(pool.tensor_tensor(f_var[:, :], f_mv[:, :, 1], f_rstd[:, :], ALU.mult), 3)
                then(pool.tensor_tensor(f_var[:, :], f_var[:, :], f_rstd[:, :], ALU.mult), 4)
                then(pool.tensor_tensor(f_var[:, :], f_var[:, :], eps[:, :], ALU.add), 5)
                then(pool.tensor_tensor(f_rstd2[:, :], f_var[:, :], minus_half[:, :], ALU.pow), 6)
                then(pool.tensor_tensor(f_scale[:, :], f_rstd2[:, :], f_rstd[:, :], ALU.mult), 7)
                then(pool.tensor_tensor(f_shift[:, :], f_mv[:, :, 0], f_scale[:, :], ALU.mult), 8)
                pool.tensor_tensor(f_shift[:, :], zero[:, :], f_shift[:, :], ALU.subtract).then_inc(f_ready, 1)

            def last_norm_affine(t):
                pool.wait_ge(f_normed, SUB * (t + 1))
                for r, op in ((1, ALU.mult), (2, ALU.add)):
                    if r == 2:
                        pool.wait_ge(f_scaled, 2 * t + 1)
                    pool.tensor_tensor(normed[:], normed[:],
                                       rows[:, r, :].unsqueeze(1).to_broadcast([P, SUB, D]),
                                       op).then_inc(f_scaled, 1)

            def opening():
                norm_rstd(0)
                norm_rstd(1)
                if final:
                    pool.wait_ge(rows_done, 3)
                for i in range(SUB):
                    normalise(0, 0, i)

            def step(s):
                if final and s.has_last:
                    last_norm_scale(s.u - 1)
                if s.has_w:
                    norm_rstd(s.u + 2)
                if final:
                    pool.wait_ge(res_loaded[s.par], 16 * (s.pair + 1))
                    pool.tensor_tensor(res[:, s.par], res[:, s.par],
                                       rows[:, 0, :].unsqueeze(1).to_broadcast([P, SUB, D]),
                                       ALU.add).then_inc(res_biased, 1)
                for i in range(SUB):
                    if s.has_v:
                        normalise(s.u + 1, 1 - s.par, i)
                    if final and s.has_last and i == 0:
                        last_norm_affine(s.u - 1)

            steps(pool, opening, step)
            if final:
                last_norm_scale(NT - 1)
                last_norm_affine(NT - 1)

        @block.scalar
        def _(act):
            for m, w in enumerate((wq_hl, wo_hl)):
                act.wait_ge(w_in[m], 16)
                act.activation(w[:, 0], res[:, m], ACT.Copy).then_inc(w_hi, 1)
            act.wait_ge(small_in, 32 + 48 * final)
            act.activation(gate[:, :], gate_in[:, :], ACT.Tanh).then_inc(gate_done, 1)

            def norm(t, par, groups=range(SUB)):
                for i in groups:
                    if i == 0:
                        act.wait_ge(norm_ready, t + 1)
                    act.activation(x[:, par, i], x[:, par, i], ACT.Identity, bias=shift[:, i:i + 1],
                                   scale=rstd[:, i:i + 1]).then_inc(normed_x, 1)

            def exponent(v, par, i):
                act.wait_ge(score_free, SUB * v + i + 1)
                act.activation(prob[:, par, i], prob[:, par, i], ACT.Exp, scale=SCALE).then_inc(exp_done, 1)

            def last_norm(t, par, i):
                if i == 0:
                    act.wait_ge(f_ready, t + 1)
                    if not (isinstance(t, int) and t == 0):
                        act.wait_ge(out_ready, SUB * t)
                act.activation(normed[:, i], res[:, par, i], ACT.Identity,
                               bias=f_shift[:, i:i + 1], scale=f_scale[:, i:i + 1]).then_inc(f_normed, 1)

            def hi_half(kind, a, use, k):
                act.wait_ge(full, use + k + 1)
                src = bank[k % 4][:, :]
                if kind == QT:
                    ins = act.activation(qt[:, 0, a], src, ACT.Identity, bias=bias_q[:, a:a + 1])
                else:
                    dst = {XT: xt[:, 0, a % KC], TURN: prob_t[:, a % 4, 0], PV: heads_t[:, 0, a % KC]}[kind]
                    ins = act.activation(dst, src, ACT.Copy)
                ins.then_inc(hi_done, 1)

            def opening():
                norm(0, 0)
                for k, (kind, a) in enumerate(OPENING):
                    hi_half(kind, a, 0, k)
                norm(1, 1)
                for i in range(SUB):
                    exponent(0, 0, i)
                for k, (kind, a) in enumerate(OPENING):
                    hi_half(kind, a, N_OPEN, k)

            def step(s):
                for k, (kind, a) in enumerate(s.plan):
                    if s.has_v and (kind, a) in EXPONENT:
                        exponent(s.u + 1, 1 - s.par, EXPONENT[kind, a])
                    if s.has_v and (kind, a) == (QT, 1):
                        exponent(s.u + 1, 1 - s.par, SUB - 1)
                    if final and s.has_last and (kind, a) in LAST_NORM:
                        last_norm(s.u - 1, 1 - s.par, LAST_NORM[kind, a])
                    if s.has_w and (kind, a) in NORM:
                        norm(s.u + 2, s.par, [NORM[kind, a]])
                    if kind != OUT:
                        hi_half(kind, a, s.use, k)
                if s.has_v and not s.has_w:
                    exponent(s.u + 1, 1 - s.par, SUB - 1)

            steps(act, opening, step)
            if final:
                for i in range(SUB):
                    last_norm(NT - 1, (NT - 1) % 2, i)

        @block.vector
        def _(dve):
            for m, w in enumerate((wq_hl, wo_hl)):
                dve.wait_ge(w_hi, m + 1)
                dve.tensor_tensor(w[:, 1], res[:, m], w[:, 0].bitcast(F32), ALU.subtract).then_inc(w_ready, 1)
            dve.wait_ge(gate_done, 1)
            dve.wait_ge(made, 4)
            if final:
                for r, by in enumerate((1, 3, 3)):
                    dve.tensor_scalar(rows[:, r, :], rows[:, r, :], gate[:, by:by + 1], None,
                                      ALU.mult).then_inc(rows_done, 1)

            def norm_stats(t, par, loads):
                for i in range(SUB):
                    group_stats(t, par, loads, i)
                norm_mean(t)

            def group_stats(t, par, loads, i):
                if i == 0:
                    dve.wait_ge(x_loaded[par], 16 * loads)
                    if not (isinstance(t, int) and t == 0):
                        dve.wait_ge(normed_x, SUB * t)
                dve.bn_stats(stats[:, i, :], x[:, par, i, :]).then_inc(norm_chain, 1)

            def norm_mean(t):
                dve.wait_ge(norm_chain, (SUB + 1) * t + SUB)
                dve.tensor_copy(waited[:, :], stats[:, 0, 0:1])
                for i in range(SUB):
                    last = dve.bn_aggr(mean_var[:, i, :], stats[:, i, :])
                last.then_inc(norm_chain, 1)

            def norm_shift(t):
                dve.wait_ge(rstd_done, 2 * t + 2)
                dve.scalar_tensor_tensor(out=shift[:, :], in0=mean_var[:, :, 0], scalar=-1.0,
                                         in1=rstd[:, :], op0=ALU.mult, op1=ALU.mult).then_inc(norm_ready, 1)

            def softmax_shift(v, par, pair, i):
                dve.wait_ge(score_full, SUB * v + i + 1)
                raw = score_bank[i % 2][:, :].rearrange("p (h s) -> p h s", h=HEADS)
                if layer == 0 and par == 0 and i == 0:
                    dve.tensor_tensor(prob[:, par, i], raw, mask[:, :].unsqueeze(1).to_broadcast([P, HEADS, KEYS]),
                                      ALU.add).then_inc(masked, 1)
                    dve.wait_ge(masked, pair + 1)
                    raw = prob[:, par, i]
                dve.tensor_reduce(top[:, i, :], raw, AX.X, ALU.max).then_inc(maxed, 1)
                dve.wait_ge(maxed, SUB * v + i + 1)
                dve.tensor_tensor(prob[:, par, i], raw, top[:, i, :].unsqueeze(2).to_broadcast([P, HEADS, KEYS]),
                                  ALU.subtract).then_inc(score_free, 1)

            def softmax_sum(v, par, i):
                dve.wait_ge(exp_done, SUB * v + i + 1)
                dve.tensor_reduce(mass[:, i, :], prob[:, par, i], AX.X, ALU.add).then_inc(summed, 1)
                dve.wait_ge(summed, SUB * v + i + 1)
                if not (isinstance(v, int) and v == 0):
                    dve.wait_ge(prob_ready, SUB * v + i - 3)
                dve.reciprocal(inv[:, i, :], mass[:, i, :]).then_inc(inv_done, 1)

            def lo_half(kind, a, k, hi_count):
                dve.wait_ge(hi_done, hi_count)
                src = bank[k % 4][:, :]
                if kind == QT:
                    ins = dve.scalar_tensor_tensor(out=qt[:, 1, a], in0=src, scalar=bias_q[:, a:a + 1],
                                                   in1=qt[:, 0, a].bitcast(F32), op0=ALU.add, op1=ALU.subtract)
                else:
                    hi, lo = {XT: (xt[:, 0, a % KC], xt[:, 1, a % KC]),
                              PV: (heads_t[:, 0, a % KC], heads_t[:, 1, a % KC]),
                              TURN: (prob_t[:, a % 4, 0], prob_t[:, a % 4, 1])}[kind]
                    ins = dve.tensor_tensor(lo, src, hi.bitcast(F32), ALU.subtract)
                ins.then_inc(free, 1)

            def residual(s, i, k):
                if i == 0:
                    dve.wait_ge(res_loaded[s.par], 16 * (s.pair + 1))
                    if final:
                        dve.wait_ge(res_biased, s.u + 1)
                dve.wait_ge(full, s.use + k + 1)
                dve.scalar_tensor_tensor(out=res[:, s.par, i], in0=bank[k % 4][:, :], scalar=gate[:, layer:layer + 1],
                                         in1=res[:, s.par, i], op0=ALU.mult, op1=ALU.add).then_inc(free, 1)

            def last_stats(s, i):
                if i == 0:
                    dve.wait_ge(free, s.after((OUT, 3)))
                    if s.has_last:
                        dve.wait_ge(f_ready, s.u)
                dve.bn_stats(f_stats[:, i, :], res[:, s.par, i, :]).then_inc(f_chain, 1)

            def last_mean(s):
                dve.wait_ge(f_chain, (SUB + 1) * s.u + SUB)
                dve.tensor_copy(f_waited[:, :], f_stats[:, 0, 0:1])
                for i in range(SUB):
                    last = dve.bn_aggr(f_mv[:, i, :], f_stats[:, i, :])
                last.then_inc(f_chain, 1)

            def output(tile, par):
                dve.wait_ge(f_scaled, 2 * tile + 2)
                for i in range(SUB):
                    dve.tensor_tensor(res[:, par, i], res[:, par, i], normed[:, i], ALU.add).then_inc(out_ready, 1)

            def opening():
                norm_stats(0, 0, 1)
                norm_shift(0)
                norm_stats(1, 1, 1)
                norm_shift(1)
                for k, (kind, a) in enumerate(OPENING):
                    lo_half(kind, a, k, k + 1)
                for i in range(SUB):
                    softmax_shift(0, 0, 0, i)
                    softmax_sum(0, 0, i)
                for k, (kind, a) in enumerate(OPENING):
                    lo_half(kind, a, k, N_OPEN + k + 1)

            def step(s):
                v_par, hi = 1 - s.par, s.hi
                for k, (kind, a) in enumerate(s.plan):
                    if s.has_v and (kind, a) in SCORES:
                        softmax_shift(s.u + 1, v_par, s.pair + s.par, SCORES[kind, a])
                    if kind == OUT:
                        residual(s, a, k)
                    else:
                        hi = hi + 1
                        lo_half(kind, a, k, hi)
                    if s.has_w and (kind, a) == (TURN, 5):
                        norm_shift(s.u + 2)
                    if s.has_v and (kind, a) in SUM:
                        softmax_sum(s.u + 1, v_par, SUM[kind, a])
                    if s.has_v and (kind, a) == (QT, 1):
                        softmax_sum(s.u + 1, v_par, SUB - 1)
                    if s.has_w and kind == TURN and a < SUB:
                        group_stats(s.u + 2, s.par, s.pair + 2, a)
                    if s.has_w and (kind, a) == (TURN, 3):
                        norm_mean(s.u + 2)
                    if final and kind == QT:
                        last_stats(s, a)
                    if final and s.has_last and (kind, a) == (OUT, 1):
                        output(s.u - 1, 1 - s.par)
                if s.has_v and not s.has_w:
                    softmax_sum(s.u + 1, v_par, SUB - 1)
                if final:
                    if not s.has_w:
                        for i in range(SUB):
                            last_stats(s, i)
                    last_mean(s)

            steps(dve, opening, step)
            if final:
                output(NT - 1, (NT - 1) % 2)

        @block.tensor
        def _(pe):
            pe.wait_ge(made, 2)
            pe.wait_ge(w_ready, 2)

            def turn_x(par, k, at):
                for i in range(SUB):
                    mm = pe.transpose(bank[at % 4][:, i * P:(i + 1) * P], x[:, par, i, k * P:(k + 1) * P], ident[:, :])
                return mm

            def query(m, at):
                for k in range(KC):
                    mm = product3(pe, bank[at % 4][:, :], [wq_hl[:, h, k, m * P:(m + 1) * P] for h in range(2)],
                                  [xt[:, h, k] for h in range(2)], k == 0, k == KC - 1)
                return mm

            def scores(v, par, i, after_first):
                if after_first:
                    pe.wait_ge(score_free, SUB * v + i - 1)
                if i == 0 and par == 0:
                    pe.wait_ge(k_loaded, 8 * v + 16)
                for g in range(KC):
                    mm = product3(pe, score_bank[i % 2][:, g * 4 * KEYS:(g + 1) * 4 * KEYS],
                                  [qt[:, h, g, i * P:(i + 1) * P] for h in range(2)],
                                  [kbd[:, h, g] for h in range(2)], True, True)
                mm.then_inc(score_full, 1)

            def opening():
                for t in range(2):
                    first = N_OPEN * t
                    pe.wait_ge(normed_x, SUB * (t + 1))
                    for k, (kind, a) in enumerate(OPENING):
                        if (kind, a) == (QT, 0):
                            pe.wait_ge(free, first + 4)
                        elif first + k >= 4:
                            pe.wait_ge(free, first + k - 3)
                        mm = turn_x(t, a, k) if kind == XT else query(a, k)
                        mm.then_inc(full, 1)
                    if t == 0:
                        pe.wait_ge(free, N_OPEN)
                        for i in range(SUB):
                            scores(0, 0, i, i >= 2)

            def step(s):
                for k, (kind, a) in enumerate(s.plan):
                    if s.has_v and (kind, a) in SCORES:
                        if SCORES[kind, a] == 0:
                            pe.wait_ge(free, s.use)
                        scores(s.u + 1, 1 - s.par, SCORES[kind, a], True)
                    if (kind, a) == (TURN, 0):
                        pe.wait_ge(prob_ready, SUB * (s.u + 1))
                        if s.par == 0:
                            pe.wait_ge(v_loaded, 8 * s.u + 16)
                    pe.wait_ge(free, s.use + k - 3)
                    if kind == TURN:
                        for i in range(SUB):
                            mm = pe.transpose(bank[k % 4][:, i * P:(i + 1) * P],
                                              prob[:, s.par, i, 2 * a:2 * a + 2, :].rearrange("p h s -> p (h s)"),
                                              ident[:, :])
                    elif kind == PV:
                        pe.wait_ge(free, s.after((TURN, 2 * a + 1)))
                        for j in range(2):
                            mm = product3(pe, bank[k % 4][:, :], [vbd[:, h, a, j] for h in range(2)],
                                          [prob_t[:, (2 * a + j) % 4, h] for h in range(2)], j == 0, j == 1)
                    elif kind == XT:
                        if a == 0:
                            pe.wait_ge(normed_x, SUB * (s.u + 3))
                        mm = turn_x(s.par, a, k)
                    elif kind == OUT:
                        if a == 0:
                            pe.wait_ge(free, s.after((PV, 3)))
                        for g in range(KC):
                            mm = product3(pe, bank[k % 4][:, :],
                                          [heads_t[:, h, g, a * P:(a + 1) * P] for h in range(2)],
                                          [wo_hl[:, h, g] for h in range(2)], g == 0, g == KC - 1)
                    else:
                        if a == 0:
                            pe.wait_ge(free, s.after((XT, 3)))
                        mm = query(a, k)
                    mm.then_inc(full, 1)

            steps(pe, opening, step)


def mlp(nc, routed, x_in, res_in, x_out, w_all, gates, gate_w, bias_rows, order, expert, fallback):
    tiles = SLOTS if routed else NT
    xv = x_in[0:TOK, :].rearrange("(t s p) d -> t p s d", s=SUB, p=P)
    rv = res_in[0:TOK, :].rearrange("(t s p) d -> t p s d", s=SUB, p=P)
    ov = x_out[0:TOK, :].rearrange("(t s p) d -> t p s d", s=SUB, p=P)
    with ExitStack() as ctx:
        sb, ps, sem = allocators(nc, ctx, "mr_" if routed else "ms_")
        RING = 4 if routed else 2
        stage = sb("stage", [P, RING, WCOL])
        w_hl = sb("w", [P, 2, CH, 2 * D], F32R)
        b1 = sb("b1", [P, CH])
        x = sb("x", [P, SUB, D])
        xt = sb("xt", [P, 2, KC, TILE], F32R)
        hidden = sb("hidden", [P, 2, TILE])
        h_hl = sb("h", [P, 2, 2, TILE], F32R)
        res = sb("res", [P, SUB, D])
        ident = sb("ident", [P, P])
        minus_half, eps, zero = (sb(n, [P, SUB]) for n in ("minus_half", "eps", "zero"))
        gate_in = sb("gate_in", [P, 4])
        gate = sb("gate", [P, 4])
        stats = sb("stats", [P, SUB, 6])
        waited = sb("waited", [P, 1])
        mean_var = sb("mean_var", [P, SUB, 2])
        rstd = sb("rstd", [P, SUB])
        shift = sb("shift", [P, SUB])
        if routed:
            x_list = sb("x_list", [P, SUB], I32)
            res_list = sb("res_list", [P, SUB], I32)
            fall = sb("fall", [P, D])
            carrier = sb("carrier", [P, 4])
        else:
            gate_rows = sb("gate_rows", [P, 2, D])
            product = sb("product", [P, D])
            score = sb("score", [P, SUB, 2])
            is_second = sb("is_second", [P, GROUPS])
            other = sb("other", [P, 4, D + 1])
            relu_b1 = sb("relu_b1", [P, 4])
            fall_sum = sb("fall_sum", [P, 2, D])
            bias3 = sb("bias3", [3, D])
            upto = sb("upto", [P, P])
            ones = sb("ones", [P, P])
            totals, before, rank, token_f, spot, zeros = (
                sb(n, [P, GROUPS]) for n in ("totals", "before", "rank", "token_f", "spot", "zeros"))
            token, place = sb("token", [P, GROUPS], I32), sb("place", [P, GROUPS], I32)
            start, flag_i = sb("start", [1, SLOTS], I32), sb("flag_i", [1, SLOTS], I32)
            start_f, flag = sb("start_f", [1, SLOTS]), sb("flag", [1, SLOTS])
            order_made, counted, chain, scattered, facts_out, first_scored, fall_w_in, fall_relu, fall_terms, fall_full, fall_row = (
                sem(n) for n in ("order_made", "counted", "chain", "scattered", "facts_out", "first_scored", "fall_w_in", "fall_relu",
                                 "fall_terms", "fall_full", "fall_row"))
            PLACED, FLAGGED = 10, 13
        hid_bank = [ps(f"hid{i}") for i in range(2)]
        turn_bank = [ps(f"turn{i}") for i in range(2)]
        out_bank = [ps(f"out{i}") for i in range(SUB)]
        (small_in, made, gate_done, x_loaded, res_loaded, stored, norm_chain, rstd_done, norm_ready,
         normed_x, turn_full, turn_hi, turn_free, w_split, w_ready, hid_full, hid_hi, hid_ready, piece_done,
         out_ready, fall_in, fall_added, x_list_in, res_list_in, scored, chosen) = (
            sem(n) for n in (
                "small_in", "made", "gate_done", "x_loaded", "res_loaded", "stored", "norm_chain",
                "rstd_done", "norm_ready", "normed_x", "turn_full", "turn_hi", "turn_free", "w_split",
                "w_ready", "hid_full", "hid_hi", "hid_ready", "piece_done", "out_ready",
                "fall_in", "fall_added", "x_list_in", "res_list_in", "scored", "chosen"))
        w_in = [sem(f"w_in{r}") for r in range(RING)]
        AHEAD = 3
        LOADS = 64 if routed else 16
        block = ctx.enter_context(nc.Block())

        def tiles_loop(eng, first, body):
            for s in range(first):
                body(s, True)
            with eng.Fori(first, tiles - 1) as s:
                body(s, True)
            body(tiles - 1, False)

        def list_rows(s):
            return order[bass.ds(s * TILE, TILE), :].rearrange("(p g) o -> p (g o)", p=P)

        @block.sync
        def _(sp):
            sp.dma_start(gate_in[:, :], gates.to_broadcast([P, 4])).then_inc(small_in, 16)
            if not routed:
                for e in range(2):
                    sp.dma_start(gate_rows[:, e, :], gate_w[e:e + 1, :].to_broadcast([P, D])).then_inc(small_in, 16)
                sp.dma_start(x[:], xv[0]).then_inc(x_loaded, 16)
            else:
                sp.dma_start(x_list[:, :], list_rows(0)).then_inc(x_list_in, 16)

            def weights(s, which, lists=None):
                for j in range(CH):
                    if not (isinstance(s, int) and CH * s + j < RING):
                        sp.wait_ge(w_ready, CH * s + j - RING + 1)
                    sp.dma_start(stage[:, j % RING, :], which[j]).then_inc(w_in[j % RING], 16)
                    if lists and j == 2 * RING:
                        lists()

            if routed:
                def body(s, more):
                    e = sp.value_load(expert[0:1, bass.ds(s, 1)],
                                      min_val=0, max_val=1)

                    def lists():
                        if not (isinstance(s, int) and s == 0):
                            sp.wait_ge(stored, 64 * s)
                        sp.dma_start(res_list[:, :], list_rows(s)).then_inc(res_list_in, 16)
                        sp.dma_start(fall[:, :], fallback[e]).then_inc(fall_in, 16)
                        if more:
                            sp.wait_ge(x_loaded, 64 * (s + 1))
                            sp.dma_start(x_list[:, :], list_rows(s + 1)).then_inc(x_list_in, 16)
                    weights(s, w_all[e + 1], lists)
                tiles_loop(sp, 1, body)
            else:
                sp.dma_start(bias3[:, :], bias_rows).then_inc(small_in, 16)

                def loads(s, more):
                    if not (isinstance(s, int) and s == 0):
                        sp.wait_ge(stored, 16 * s)
                    sp.dma_start(res[:], rv[s]).then_inc(res_loaded, 16)
                    if not (isinstance(s, int) and s == 0):
                        sp.wait_ge(fall_terms, 4 * s)
                    for n in range(4):
                        sp.dma_start(other[:, n, :], w_pieces[n % 2][s, n // 2]).then_inc(fall_w_in, 16)
                    if more:
                        sp.wait_ge(turn_full, KC * (s + 1))
                        sp.wait_ge(scored, SUB * (s + 1))
                        sp.dma_start(x[:], xv[s + 1]).then_inc(x_loaded, 16)
                w_pieces = [w_all[1 + e].rearrange("(s n) p c -> s n p c", n=2)[:, :, :, D:WCOL] for e in range(2)]

                def body(s, more):
                    if isinstance(s, int) and s == 0:
                        weights(0, w_all[0], lambda: loads(0, True))
                    else:
                        loads(s, more)
                    if not more:
                        sp.wait_ge(chain, FLAGGED)
                        sp.dma_start(expert, flag_i[:, :]).then_inc(facts_out, 16)
                        for e in range(2):
                            sp.wait_ge(fall_row, e + 1)
                            sp.dma_start(fallback[e], fall_sum[:, e, :]).then_inc(facts_out, 16)
                    sp.wait_ge(out_ready, SUB * (s + 1))
                    sp.dma_start(ov[s], res[:]).then_inc(stored, 16)
                tiles_loop(sp, 1, body)
                sp.wait_ge(stored, 16 * tiles)
                sp.wait_ge(scattered, 16 * GROUPS)
                sp.wait_ge(facts_out, 48)

        @block.gpsimd
        def _(pool):
            diagonal(pool, ident, made)
            for m, value in ((minus_half, -0.5), (eps, EPS), (zero, 0.0)):
                pool.memset(m[:, :], value).then_inc(made, 1)
            pool.wait_ge(made, 5)

            def gather(dst, lists, lists_in, table, loaded, s):
                pool.wait_ge(lists_in, 16 * (s + 1))
                at = 0 if dst is x else 1
                pool.tensor_tensor(carrier[:, at:at + 1], zero[:, 0:1], zero[:, 0:1], ALU.add)
                for g in range(SUB):
                    pool.indirect_dma_start(
                        out=dst[:, g, :], out_offset=None, in_=table,
                        in_offset=bass.IndirectOffsetOnAxis(ap=lists[:, g:g + 1], axis=0)).then_inc(loaded, 16)

            def scatter(s, at=2):
                pool.wait_ge(out_ready, SUB * (s + 1))
                pool.tensor_tensor(carrier[:, at:at + 1], zero[:, 0:1], zero[:, 0:1], ALU.add)
                for g in range(SUB):
                    pool.indirect_dma_start(
                        out=x_out, out_offset=bass.IndirectOffsetOnAxis(ap=res_list[:, g:g + 1], axis=0),
                        in_=res[:, g, :], in_offset=None).then_inc(stored, 16)

            def norm_rstd(t):
                pool.wait_ge(norm_chain, 2 * t + 2)
                pool.tensor_tensor(rstd[:, :], mean_var[:, :, 1], eps[:, :], ALU.add).then_inc(rstd_done, 1)
                pool.wait_ge(rstd_done, 2 * t + 1)
                pool.tensor_tensor(rstd[:, :], rstd[:, :], minus_half[:, :], ALU.pow).then_inc(rstd_done, 1)

            def split(s, j):
                pool.wait_ge(w_split, CH * s + j + 1)
                pool.tensor_tensor(b1[:, j:j + 1], stage[:, j % RING, 2 * D:WCOL], zero[:, 0:1], ALU.add)
                pool.tensor_tensor(w_hl[:, 1, j], stage[:, j % RING, 0:2 * D], w_hl[:, 0, j].bitcast(F32),
                                   ALU.subtract).then_inc(w_ready, 1)

            if routed:
                gather(x, x_list, x_list_in, x_in, x_loaded, 0)
            else:
                pool.memset(fall_sum[:], 0.0).then_inc(order_made, 1)
                pool.memset(upto[:, :], 1.0).then_inc(order_made, 1)
                pool.memset(ones[:, :], 1.0).then_inc(order_made, 1)
                pool.memset(zeros[:, :], 0.0).then_inc(order_made, 1)
                pool.iota(token[:, :], pattern=[[P, GROUPS]], base=0, channel_multiplier=1).then_inc(order_made, 1)
                pool.iota(start[:, :], pattern=[[TILE, SLOTS]], base=0, channel_multiplier=0).then_inc(order_made, 1)
                pool.wait_ge(order_made, 2)
                pool.affine_select(out=upto[:, :], in_=upto[:, :], compare_op=ALU.is_ge, fill=0.0,
                                   base=0, pattern=[[1, P]], channel_multiplier=-1).then_inc(order_made, 1)
            norm_rstd(0)
            for j in range(AHEAD):
                split(0, j)

            def body(s, more):
                first = isinstance(s, int) and s == 0
                for j in range(CH):
                    if j + AHEAD < CH:
                        if routed or first:
                            split(s, j + AHEAD)
                    elif routed and more:
                        split(s + 1, j + AHEAD - CH)
                    if routed and j == 0 and not first:
                        scatter(s - 1)
                    if routed and j == 1:
                        if not first:
                            pool.wait_ge(stored, 64 * s)
                        gather(res, res_list, res_list_in, res_in, res_loaded, s)
                    if routed and j == 3 and more:
                        pool.wait_ge(turn_full, KC * (s + 1))
                        gather(x, x_list, x_list_in, x_in, x_loaded, s + 1)
                    if more and j == 9:
                        norm_rstd(s + 1)
                if not routed and not more:
                    pool.wait_ge(chain, PLACED)
                    for g in range(GROUPS):
                        pool.indirect_dma_start(
                            out=order, out_offset=bass.IndirectOffsetOnAxis(ap=place[:, g:g + 1], axis=0),
                            in_=token[:, g:g + 1], in_offset=None).then_inc(scattered, 16)
            tiles_loop(pool, 1, body)
            if routed:
                scatter(tiles - 1, 3)
                pool.wait_ge(stored, 64 * tiles)

        @block.scalar
        def _(act):
            act.wait_ge(small_in, 16 if routed else 64)
            act.activation(gate[:, :], gate_in[:, :], ACT.Tanh).then_inc(gate_done, 1)

            def norm(t):
                act.wait_ge(norm_ready, t + 1)
                for i in range(SUB):
                    act.activation(x[:, i], x[:, i], ACT.Identity, bias=shift[:, i:i + 1],
                                   scale=rstd[:, i:i + 1]).then_inc(normed_x, 1)

            def turn_halves(t):
                for k in range(KC):
                    act.wait_ge(turn_full, KC * t + k + 1)
                    act.activation(xt[:, 0, k], turn_bank[k % 2][:, :], ACT.Copy).then_inc(turn_hi, 1)

            def split(s, j):
                act.wait_ge(w_in[j % RING], 16 * (CH // RING * s + j // RING + 1))
                if not (isinstance(s, int) and s == 0):
                    act.wait_ge(piece_done, CH * s + j - CH + 1)
                act.activation(w_hl[:, 0, j], stage[:, j % RING, 0:2 * D], ACT.Copy).then_inc(w_split, 1)

            def split_ahead(s, j, more):
                if j + AHEAD < CH:
                    if routed or (isinstance(s, int) and s == 0):
                        split(s, j + AHEAD)
                elif routed and more:
                    split(s + 1, j + AHEAD - CH)

            for j in range(AHEAD):
                split(0, j)
            norm(0)
            turn_halves(0)

            def body(s, more):
                for j in range(CH):
                    split_ahead(s, j, more)
                    if j == 11 and more:
                        norm(s + 1)
                    act.wait_ge(hid_full, CH * s + j + 1)
                    if not (isinstance(s, int) and CH * s + j < 2):
                        act.wait_ge(piece_done, CH * s + j - 1)
                    for dst in (hidden[:, j % 2], h_hl[:, j % 2, 0]):
                        last = act.activation(dst, hid_bank[j % 2][:, :], ACT.Relu, bias=b1[:, j:j + 1])
                    last.then_inc(hid_hi, 1)
                if more:
                    turn_halves(s + 1)
            tiles_loop(act, 1, body)

        @block.vector
        def _(dve):
            dve.wait_ge(gate_done, 1)

            def norm_stats(t):
                dve.wait_ge(x_loaded, LOADS * (t + 1))
                if not (isinstance(t, int) and t == 0):
                    dve.wait_ge(normed_x, SUB * t)
                for i in range(SUB):
                    last = dve.bn_stats(stats[:, i, :], x[:, i, :])
                last.then_inc(norm_chain, 1)
                dve.wait_ge(norm_chain, 2 * t + 1)
                dve.tensor_copy(waited[:, :], stats[:, 0, 0:1])
                for i in range(SUB):
                    last = dve.bn_aggr(mean_var[:, i, :], stats[:, i, :])
                last.then_inc(norm_chain, 1)

            def norm_shift(t):
                dve.wait_ge(rstd_done, 2 * t + 2)
                dve.scalar_tensor_tensor(out=shift[:, :], in0=mean_var[:, :, 0], scalar=-1.0,
                                         in1=rstd[:, :], op0=ALU.mult, op1=ALU.mult).then_inc(norm_ready, 1)

            def gate_scores(t):
                dve.wait_ge(normed_x, SUB * (t + 1))
                for i in range(SUB):
                    for e in range(2):
                        done = (first_scored, scored)[e]
                        dve.tensor_tensor_reduce(product[:, :], x[:, i, :], gate_rows[:, e, :], 1.0, 0.0,
                                                 ALU.mult, ALU.add, score[:, i, e:e + 1]).then_inc(done, 1)
                        dve.wait_ge(done, SUB * t + i + 1)
                dve.tensor_tensor(is_second[:, bass.ds(t * SUB, SUB)], score[:, :, 1], score[:, :, 0],
                                  ALU.is_gt).then_inc(chosen, 1)

            def turn_los(t):
                for k in range(KC):
                    dve.wait_ge(turn_hi, KC * t + k + 1)
                    dve.tensor_tensor(xt[:, 1, k], turn_bank[k % 2][:, :], xt[:, 0, k].bitcast(F32),
                                      ALU.subtract).then_inc(turn_free, 1)

            def fall_term(s, n):
                if n == 0:
                    dve.wait_ge(fall_w_in, 64 * (s + 1))
                    if not (isinstance(s, int) and s == 0):
                        dve.wait_ge(fall_terms, 4 * s)
                    dve.tensor_scalar(relu_b1[:, :], other[:, :, D], 0.0, None, ALU.max).then_inc(fall_relu, 1)
                    dve.wait_ge(fall_relu, s + 1)
                if not (isinstance(s, int) and s == 0 and n < 2):
                    dve.wait_ge(fall_terms, 4 * s + n - 1)
                at = fall_sum[:, n % 2, :]
                dve.scalar_tensor_tensor(out=at, in0=other[:, n, 0:D], scalar=relu_b1[:, n:n + 1], in1=at,
                                         op0=ALU.mult, op1=ALU.add).then_inc(fall_terms, 1)

            def fall_rows():
                for e in range(2):
                    dve.wait_ge(fall_full, e + 1)
                    dve.tensor_scalar(fall_sum[:, e, :], turn_bank[e][:, :], gate[:, 2:3], None,
                                      ALU.mult).then_inc(fall_row, 1)

            def places():
                done = [0]

                def link(ins):
                    done[0] += 1
                    ins.then_inc(chain, 1)
                    dve.wait_ge(chain, done[0])
                dve.wait_ge(counted, 2)
                link(dve.tensor_copy(totals[:, :], turn_bank[1][:, 0:GROUPS]))
                link(dve.tensor_tensor_scan(before[:, :], totals[:, :], zeros[:, :], 0.0, ALU.add, ALU.add))
                link(dve.tensor_tensor(rank[:, :], before[:, :], totals[:, :], ALU.subtract))
                link(dve.tensor_tensor(rank[:, :], turn_bank[0][:, 0:GROUPS], rank[:, :], ALU.add))
                link(dve.tensor_copy(token_f[:, :], token[:, :]))
                link(dve.tensor_scalar(spot[:, :], token_f[:, :], -1.0, float(LIST), ALU.mult, ALU.add))
                link(dve.tensor_tensor(spot[:, :], spot[:, :], is_second[:, :], ALU.mult))
                link(dve.tensor_tensor(spot[:, :], spot[:, :], token_f[:, :], ALU.add))
                link(dve.tensor_tensor(spot[:, :], spot[:, :], rank[:, :], ALU.subtract))
                link(dve.tensor_copy(place[:, :], spot[:, :]))
                link(dve.tensor_copy(start_f[:, :], start[:, :]))
                link(dve.tensor_scalar(flag[:, :], start_f[:, :], before[0:1, GROUPS - 1:GROUPS], float(TOK),
                                       ALU.add, ALU.is_ge))
                link(dve.tensor_copy(flag_i[:, :], flag[:, :]))

            norm_stats(0)
            norm_shift(0)
            turn_los(0)
            if not routed:
                gate_scores(0)
                dve.wait_ge(order_made, 7)

            def body(s, more):
                for j in range(CH):
                    if more and j == 8:
                        norm_stats(s + 1)
                    if more and j == 10:
                        norm_shift(s + 1)
                    if more and j == 13 and not routed:
                        gate_scores(s + 1)
                    dve.wait_ge(hid_hi, CH * s + j + 1)
                    dve.tensor_tensor(h_hl[:, j % 2, 1], hidden[:, j % 2], h_hl[:, j % 2, 0].bitcast(F32),
                                      ALU.subtract).then_inc(hid_ready, 1)
                    if not routed and j in (4, 5, 6, 7):
                        fall_term(s, j - 4)
                    if not routed and not more and j == 2:
                        places()
                    if not routed and not more and j == 10:
                        fall_rows()
                    if routed and j == 6:
                        dve.wait_ge(fall_in, 16 * (s + 1))
                        dve.wait_ge(res_loaded, LOADS * (s + 1))
                        dve.tensor_tensor(res[:], res[:], fall[:, :].unsqueeze(1).to_broadcast([P, SUB, D]),
                                          ALU.add).then_inc(fall_added, 1)
                if more:
                    turn_los(s + 1)
                if routed:
                    dve.wait_ge(fall_added, s + 1)
                else:
                    dve.wait_ge(res_loaded, LOADS * (s + 1))
                dve.wait_ge(piece_done, CH * (s + 1))
                for i in range(SUB):
                    dve.scalar_tensor_tensor(out=res[:, i], in0=out_bank[i][:, :], scalar=gate[:, 2:3],
                                             in1=res[:, i], op0=ALU.mult, op1=ALU.add).then_inc(out_ready, 1)
            tiles_loop(dve, 1, body)

        @block.tensor
        def _(pe):
            pe.wait_ge(made, 2)
            if not routed:
                pe.wait_ge(order_made, 7)

            def turn(t):
                pe.wait_ge(normed_x, SUB * (t + 1))
                for k in range(KC):
                    if not (isinstance(t, int) and KC * t + k < 2):
                        pe.wait_ge(turn_free, KC * t + k - 1)
                    for i in range(SUB):
                        mm = pe.transpose(turn_bank[k % 2][:, i * P:(i + 1) * P], x[:, i, k * P:(k + 1) * P],
                                          ident[:, :])
                    mm.then_inc(turn_full, 1)

            def up(s, j):
                pe.wait_ge(w_ready, CH * s + j + 1 if routed else j + 1)
                if not (isinstance(s, int) and CH * s + j < 2):
                    pe.wait_ge(hid_ready, CH * s + j - 1)
                if j == 0:
                    pe.wait_ge(turn_free, KC * (s + 1))
                for k in range(KC):
                    mm = product3(pe, hid_bank[j % 2][:, :], [w_hl[:, h, j, k * P:(k + 1) * P] for h in range(2)],
                                  [xt[:, h, k] for h in range(2)], k == 0, k == KC - 1)
                mm.then_inc(hid_full, 1)

            def down(s, j):
                pe.wait_ge(hid_ready, CH * s + j + 1)
                if j == 0 and not (isinstance(s, int) and s == 0):
                    pe.wait_ge(out_ready, SUB * s)
                for i in range(SUB):
                    mm = product3(pe, out_bank[i][:, :], [h_hl[:, j % 2, h, i * P:(i + 1) * P] for h in range(2)],
                                  [w_hl[:, h, j, D:2 * D] for h in range(2)], j == 0, j == CH - 1)
                mm.then_inc(piece_done, 1)

            turn(0)

            def body(s, more):
                up(s, 0)
                for j in range(CH):
                    if j + 1 < CH:
                        up(s, j + 1)
                    if j == CH - 2 and more:
                        turn(s + 1)
                    if not routed and not more and j == 1:
                        pe.wait_ge(chosen, NT)
                        pe.wait_ge(turn_free, KC * NT)
                        for b, m in enumerate((upto, ones)):
                            pe.matmul(turn_bank[b][:, 0:GROUPS], m[:, :], is_second[:, :],
                                      start=True, stop=True).then_inc(counted, 1)
                    if not routed and not more and j == 9:
                        pe.wait_ge(fall_terms, 4 * NT)
                        pe.wait_ge(chain, PLACED)
                        for e in range(2):
                            pe.matmul(turn_bank[e][:, :], ones[:, :], fall_sum[:, 1 - e, :], start=True, stop=False)
                            mm = pe.matmul(turn_bank[e][:, :], ones[0:3, :], bias3[:, :], start=False, stop=True)
                        mm.then_inc(fall_full, 2)
                    down(s, j)
            tiles_loop(pe, 1, body)


def program(nc, x, ctx_t, gates, wq, wk, wv, wo, bq, bk, bv, rows1, gate_w, w_all, mlp_rows, out):
    def dram(name, shape, dt=F32):
        return nc.dram_tensor(name, shape, dt, kind="Internal").ap()
    k_dram = dram("k_dram", (2, BATCH, P, 2048))
    v_dram = dram("v_dram", (2, BATCH, P, 2048))
    x1 = dram("x1", (LIST, D))
    x1s = dram("x1s", (LIST, D))
    x2 = dram("x2", (LIST, D))
    order = dram("order", (LIST, 1), I32)
    expert = dram("expert", (1, SLOTS), I32)
    fallback = dram("fallback", (2, P, D))
    context(nc, ctx_t, wk, wv, bk, bv, k_dram, v_dram, order, [x1[TOK:LIST, :], x1s[TOK:LIST, :]])
    attention(nc, 0, x, x1, wq[0], wo[0], bq[0], gates, k_dram[0], v_dram[0], None)
    mlp(nc, False, x1, x1, x1s, w_all, gates, gate_w, mlp_rows, order, expert, fallback)
    mlp(nc, True, x1, x1s, x2, w_all, gates, None, None, order, expert, fallback)
    attention(nc, 1, x2, out, wq[1], wo[1], bq[1], gates, k_dram[1], v_dram[1], rows1)


def kernel(**inputs):
    import numpy as np
    import concourse.bacc as bacc
    from concourse.bass_utils import run_bass_kernel_spmd

    def merged(w):
        return w.transpose(1, 0, 2).reshape(D, D)

    def columns(b):
        return b.reshape(KC, P).T
    i = {k: np.asarray(v) for k, v in inputs.items()}
    none = np.zeros(D, np.float32)
    w1 = np.stack([i["L0_ffn_sw1"], *i["L0_ffn_w1"]])
    w2 = np.stack([i["L0_ffn_sw2"], *i["L0_ffn_w2"]])
    b1 = np.stack([i["L0_ffn_sb1"], *i["L0_ffn_b1"]])
    w_all = np.concatenate([
        w1.reshape(3, KC, P, CH, P).transpose(0, 3, 2, 1, 4).reshape(3, CH, P, D),
        w2.reshape(3, CH, P, D), b1.reshape(3, CH, P, 1)], axis=3)
    arrays = {
        "x": i["x"].reshape(TOK, D),
        "ctx_t": i["ctx_1024"].transpose(2, 0, 1).reshape(D, BATCH * KEYS),
        "gates": np.concatenate([i["g_xattn"], i["g_ffn"]]).reshape(1, 4),
        "wq": np.stack([i["L0_xattn_Wq"].T, merged(i["L1_xattn_Wq"])]),
        "wk": np.stack([i["L0_xattn_Wk"].T, merged(i["L1_xattn_Wk"])]),
        "wv": np.stack([i["L0_xattn_Wv"].T, merged(i["L1_xattn_Wv"])]),
        "wo": np.stack([i["L0_xattn_Wo"].T, i["L1_xattn_Wo"]]),
        "bq": np.stack([columns(none), columns(i["L1_xattn_bq"].reshape(D))]),
        "bk": np.stack([columns(none), columns(i["L1_xattn_bk"].reshape(D))]),
        "bv": np.stack([none, i["L1_xattn_bv"].reshape(D)]).reshape(2, 1, D),
        "rows1": np.stack([i["L1_xattn_bo"], i["L1_ffn_ln_g"], i["L1_ffn_ln_b"]]),
        "gate_w": i["L0_ffn_gate_w"],
        "w_all": w_all,
        "mlp_rows": np.stack([i["L0_ffn_sb2"], *i["L0_ffn_b2"]]),
    }
    arrays = {k: np.ascontiguousarray(v) for k, v in arrays.items()}
    nc = bacc.Bacc("TRN2", target_bir_lowering=False, num_devices=1)
    args = {k: nc.dram_tensor(k, v.shape, mybir.dt.from_np(v.dtype), kind="ExternalInput").ap()
            for k, v in arrays.items()}
    out = nc.dram_tensor("out", (TOK, D), F32, kind="ExternalOutput").ap()
    program(nc, **args, out=out)
    r = run_bass_kernel_spmd(nc, [arrays], core_ids=[0])
    return r.results[0]["out"].reshape(BATCH, SEQ, D)
```

```python
from contextlib import ExitStack

import concourse.bass as bass
from concourse import mybir

F32 = mybir.dt.float32
F32R = mybir.dt.float32r
I32 = mybir.dt.int32
ALU = mybir.AluOpType
ACT = mybir.ActivationFunctionType
AX = mybir.AxisListType

P = 128
BATCH, SEQ, D = 4, 1024, 512
KEYS = 64
HEADS, HD = 16, 32
HIDDEN = 2048
TOK = BATCH * SEQ
TILE = 512
SUB = TILE // P
KC = D // P
NT = TOK // TILE
TPB = SEQ // TILE
CH = HIDDEN // P
WCOL = 2 * D + 1
HALF = TILE // 2
LIST = TOK + HALF
GROUPS = TOK // P
SCALE = HD ** -0.5
NEG = -1e9
EPS = 1e-5


def allocators(nc, ctx, prefix):
    sems = []

    def clear():
        nc.clear_and_free_semaphores(sems)
        nc.all_engine_barrier()
    ctx.callback(clear)

    def sb(name, shape, dt=F32):
        return ctx.enter_context(nc.sbuf_tensor(prefix + name, shape, dt))

    def ps(name, cols=512):
        return ctx.enter_context(nc.psum_tensor(prefix + name, [P, cols], F32))

    def sem(name):
        sems.append(nc.alloc_semaphore(prefix + name))
        return sems[-1]
    return sb, ps, sem


def product3(pe, out, w, x, start, stop):
    pe.matmul(out, w[0], x[1], start=start, stop=False)
    pe.matmul(out, w[0], x[0], start=False, stop=False)
    return pe.matmul(out, w[1], x[0], start=False, stop=stop)


def diagonal(pool, m, made):
    pool.memset(m[:, :], 0.0).then_inc(made, 1)
    pool.wait_ge(made, 1)
    pool.affine_select(out=m[:, :], in_=m[:, :], compare_op=ALU.not_equal, fill=1.0,
                       base=0, pattern=[[-1, P]], channel_multiplier=1).then_inc(made, 1)


def context(nc, ctx_t, wk, wv, bk, bv, k_out, v_out, order, spare_rows):
    with ExitStack() as ctx:
        sb, ps, sem = allocators(nc, ctx, "cx_")
        raw = sb("raw", [P, KC, BATCH * KEYS])
        c_hl = [sb("c_" + n, [P, KC, BATCH * KEYS], F32R) for n in ("hi", "lo")]
        w_raw = sb("w_raw", [P, 2, 2, KC, D])
        w_hl = [sb("w_" + n, [P, 2, 2, KC, D], F32R) for n in ("hi", "lo")]
        bias_k = sb("bias_k", [P, 2, KC])
        bias_v = sb("bias_v", [P, 2, D])
        value = sb("value", [P, 2, 2, D])
        k_all = sb("k_all", [P, 2, 2, KC, BATCH * KEYS], F32R)
        v_all = sb("v_all", [P, 2, 2, 2, D], F32R)
        spare = sb("spare", [LIST // HALF, HALF], I32)
        blank = sb("blank", [P, D])
        bank = [ps(f"bank{n}") for n in range(KC + 2)]
        filled, made, ctx_in, small_in, hi_done, lo_done, full, k_hi, biased, v_hi, k_built, v_built, stored = (
            sem(n) for n in ("filled", "made", "ctx_in", "small_in", "hi_done", "lo_done", "full",
                             "k_hi", "biased", "v_hi", "k_built", "v_built", "stored"))
        w_in = [sem(f"w_in{n}") for n in range(4)]
        WEIGHTS = [(l, n) for l in range(2) for n in range(2)]
        USES = KC + 2
        block = ctx.enter_context(nc.Block())

        @block.sync
        def _(sp):
            sp.dma_start(raw[:], ctx_t.rearrange("(k p) n -> p k n", p=P)).then_inc(ctx_in, 16)
            for n, (l, kv) in enumerate(WEIGHTS):
                sp.dma_start(w_raw[:, l, kv], (wk, wv)[kv][l].rearrange("(k p) n -> p k n", p=P)).then_inc(w_in[n], 16)
                if n == 0:
                    for m in range(2):
                        sp.dma_start(bias_k[:, m, :], bk[m]).then_inc(small_in, 16)
                        sp.dma_start(bias_v[:, m, :], bv[m].to_broadcast([P, D])).then_inc(small_in, 16)
            sp.wait_ge(made, 2)
            sp.dma_start(order.rearrange("(s r) o -> s (r o)", r=HALF), spare[:, :]).then_inc(filled, 16)
            for rows in spare_rows:
                sp.dma_start(rows.rearrange("(s p) d -> p s d", p=P),
                             blank[:, :].unsqueeze(1).to_broadcast([P, HALF // P, D])).then_inc(filled, 16)
            for l in range(2):
                sp.wait_ge(k_built, KC * (l + 1))
                sp.dma_start(k_out[l].rearrange("p h g n -> p (h g n)"),
                             k_all[:, l].bitcast(F32).rearrange("p h g n -> p (h g n)")).then_inc(stored, 16)
                for b in range(2):
                    sp.wait_ge(v_built, 2 * l + b + 1)
                    sp.dma_start(v_out[l, b].rearrange("p h n -> p (h n)"),
                                 v_all[:, l, b].bitcast(F32).rearrange("p h n -> p (h n)")).then_inc(stored, 16)
            sp.wait_ge(stored, 96)
            sp.wait_ge(filled, 16 + 16 * len(spare_rows))

        @block.gpsimd
        def _(pool):
            pool.memset(blank[:, :], 0.0).then_inc(made, 1)
            pool.iota(spare[:, :], pattern=[[1, HALF]], base=TOK, channel_multiplier=0).then_inc(made, 1)

        @block.scalar
        def _(act):
            def split(n):
                l, kv = WEIGHTS[n]
                act.wait_ge(w_in[n], 16)
                act.activation(w_hl[0][:, l, kv], w_raw[:, l, kv], ACT.Copy).then_inc(hi_done, 1)

            act.wait_ge(ctx_in, 16)
            act.activation(c_hl[0][:], raw[:], ACT.Copy).then_inc(hi_done, 1)
            split(0)
            split(1)
            act.wait_ge(small_in, 64)
            for l in range(2):
                for g in range(KC):
                    act.wait_ge(full, USES * l + g + 1)
                    act.activation(k_all[:, l, 0, g], bank[g][:, 0:BATCH * KEYS], ACT.Identity,
                                   bias=bias_k[:, l, g:g + 1]).then_inc(k_hi, 1)
                if l == 0:
                    split(2)
                    split(3)
                for b in range(2):
                    act.wait_ge(biased, 2 * l + b + 1)
                    act.activation(v_all[:, l, b, 0], value[:, l, b], ACT.Copy).then_inc(v_hi, 1)

        @block.vector
        def _(dve):
            def split(n):
                l, kv = WEIGHTS[n]
                dve.wait_ge(hi_done, 2 + n)
                dve.tensor_tensor(w_hl[1][:, l, kv], w_raw[:, l, kv], w_hl[0][:, l, kv].bitcast(F32),
                                  ALU.subtract).then_inc(lo_done, 1)

            dve.wait_ge(hi_done, 1)
            dve.tensor_tensor(c_hl[1][:], raw[:], c_hl[0][:].bitcast(F32), ALU.subtract).then_inc(lo_done, 1)
            split(0)
            split(1)
            dve.wait_ge(small_in, 64)
            for l in range(2):
                for g in range(KC):
                    dve.wait_ge(k_hi, KC * l + g + 1)
                    dve.scalar_tensor_tensor(
                        out=k_all[:, l, 1, g], in0=bank[g][:, 0:BATCH * KEYS], scalar=bias_k[:, l, g:g + 1],
                        in1=k_all[:, l, 0, g].bitcast(F32), op0=ALU.add, op1=ALU.subtract).then_inc(k_built, 1)
                if l == 0:
                    split(2)
                for b in range(2):
                    dve.wait_ge(full, USES * l + KC + b + 1)
                    dve.tensor_tensor(value[:, l, b], bank[KC + b][:, :], bias_v[:, l, :], ALU.add).then_inc(biased, 1)
                if l == 0:
                    split(3)
                for b in range(2):
                    dve.wait_ge(v_hi, 2 * l + b + 1)
                    dve.tensor_tensor(v_all[:, l, b, 1], value[:, l, b], v_all[:, l, b, 0].bitcast(F32),
                                      ALU.subtract).then_inc(v_built, 1)

        @block.tensor
        def _(pe):
            for l in range(2):
                pe.wait_ge(lo_done, 2 + 2 * l)
                if l:
                    pe.wait_ge(k_built, KC)
                for g in range(KC):
                    cols = slice(g * P, (g + 1) * P)
                    for k in range(KC):
                        mm = product3(pe, bank[g][:, 0:BATCH * KEYS], [w[:, l, 0, k, cols] for w in w_hl],
                                      [c[:, k, :] for c in c_hl], k == 0, k == KC - 1)
                    mm.then_inc(full, 1)
                pe.wait_ge(lo_done, 3 + 2 * l)
                if l:
                    pe.wait_ge(biased, 2)
                for b in range(2):
                    for k in range(KC):
                        mm = product3(pe, bank[KC + b][:, :], [c[:, k, b * P:(b + 1) * P] for c in c_hl],
                                      [w[:, l, 1, k, :] for w in w_hl], k == 0, k == KC - 1)
                    mm.then_inc(full, 1)


def attention(nc, layer, x_in, x_out, wq, wo, bq, gates, k_dram, v_dram, row_dram):
    final = row_dram is not None
    xv = x_in[0:TOK, :].rearrange("(t s p) d -> t p s d", s=SUB, p=P)
    ov = x_out[0:TOK, :].rearrange("(t s p) d -> t p s d", s=SUB, p=P)
    with ExitStack() as ctx:
        sb, ps, sem = allocators(nc, ctx, f"a{layer}_")
        wq_hl = sb("wq", [P, 2, KC, D], F32R)
        wo_hl = sb("wo", [P, 2, KC, D], F32R)
        x = sb("x", [P, 2, SUB, D])
        xt = sb("xt", [P, 2, KC, TILE], F32R)
        qt = sb("qt", [P, 2, KC, TILE], F32R)
        prob = sb("prob", [P, 2, SUB, HEADS, KEYS])
        prob_t = sb("prob_t", [P, 4, 2, TILE], F32R)
        heads_t = sb("heads_t", [P, 2, KC, TILE], F32R)
        res = sb("res", [P, 2, SUB, D])
        kbd = sb("kbd", [P, 2, KC, 4 * KEYS], F32R)
        vbd = sb("vbd", [P, 2, KC, 2, P], F32R)
        ident = sb("ident", [P, P])
        mask = sb("mask", [P, KEYS])
        gate_in = sb("gate_in", [P, 4])
        gate = sb("gate", [P, 4])
        bias_q = sb("bias_q", [P, KC])
        stats = sb("stats", [P, SUB, 6])
        waited = sb("waited", [P, 1])
        mean_var = sb("mean_var", [P, SUB, 2])
        rstd = sb("rstd", [P, SUB])
        minus_half, eps, zero = (sb(n, [P, SUB]) for n in ("minus_half", "eps", "zero"))
        shift = sb("shift", [P, SUB])
        top = sb("top", [P, SUB, HEADS])
        mass = sb("mass", [P, SUB, HEADS])
        inv = sb("inv", [P, SUB, HEADS])
        if final:
            rows = sb("rows", [P, 3, D])
            normed = sb("normed", [P, SUB, D])
            f_stats = sb("f_stats", [P, SUB, 6])
            f_waited = sb("f_waited", [P, 1])
            f_mv = sb("f_mv", [P, SUB, 2])
            f_rstd, f_var, f_rstd2, f_scale, f_shift = (
                sb(n, [P, SUB]) for n in ("f_rstd", "f_var", "f_rstd2", "f_scale", "f_shift"))
        score_bank = [ps(f"score{i}", HEADS * KEYS) for i in range(2)]
        bank = [ps(f"bank{i}") for i in range(4)]
        (cleared, small_in, w_hi, w_ready, made, gate_done, rows_done, k_loaded, v_loaded, stored, normed_x,
         norm_chain, rstd_done, norm_ready, full, free, hi_done, score_full, masked, maxed, score_free, exp_done,
         summed, inv_done, prob_ready, res_biased, f_chain, f_done, f_ready, f_normed, f_scaled, out_ready) = (
            sem(n) for n in (
                "cleared", "small_in", "w_hi", "w_ready", "made", "gate_done", "rows_done", "k_loaded", "v_loaded",
                "stored", "normed_x", "norm_chain", "rstd_done", "norm_ready", "full", "free", "hi_done", "score_full",
                "masked", "maxed", "score_free", "exp_done", "summed", "inv_done", "prob_ready",
                "res_biased", "f_chain", "f_done", "f_ready", "f_normed", "f_scaled", "out_ready"))
        w_in = [sem(f"w_in{n}") for n in range(2)]
        x_loaded = [sem(f"x_loaded{n}") for n in range(2)]
        res_loaded = [sem(f"res_loaded{n}") for n in range(2)]

        QT, TURN, PV, XT, OUT = "qt", "turn", "pv", "xt", "out"
        FULL_STEP = [(QT, 0), (QT, 1), (TURN, 0), (TURN, 1), (QT, 2), (TURN, 2), (TURN, 3), (PV, 0),
                     (QT, 3), (TURN, 4), (TURN, 5), (PV, 1), (TURN, 6), (TURN, 7), (PV, 2),
                     (XT, 0), (XT, 1), (PV, 3), (XT, 2), (XT, 3), (OUT, 0), (OUT, 1), (OUT, 2), (OUT, 3)]
        NO_XT_STEP = [use for use in FULL_STEP if use[0] != XT]
        LAST_STEP = [use for use in NO_XT_STEP if use[0] != QT]
        OPENING = [(XT, i) for i in range(4)] + [(QT, i) for i in range(4)] + [(XT, i) for i in range(4)]
        N_OPEN, N_STEP = len(OPENING), len(FULL_STEP)
        N_OUT = SUB
        PRODUCED = {(TURN, 6): 0, (XT, 0): 1, (OUT, 0): 2, (OUT, 1): 3}
        SCORES = {(PV, 2): 0, (PV, 3): 1, (OUT, 0): 2, (OUT, 2): 3}
        EXPONENT = {(PV, 3): 0, (OUT, 0): 1, (OUT, 2): 2}
        SUM = {(PV, 3): 0, (OUT, 0): 1, (OUT, 2): 2}
        STATS = {(QT, 0): 0, (QT, 1): 1, (TURN, 1): 2, (QT, 2): 3}
        NORM = {(TURN, 6): 0, (TURN, 7): 1, (PV, 2): 2, (XT, 0): 3}
        LAST_NORM = {(TURN, 2): 0, (TURN, 3): 1, (PV, 0): 2, (TURN, 4): 3}
        PEELED = 2
        LOOP_END = NT - 2

        class Step:

            def __init__(self, u, par, pair, first_use, first_hi, plan, has_v, has_w, has_last):
                self.u, self.par, self.pair = u, par, pair
                self.use, self.hi, self.plan = first_use, first_hi, plan
                self.has_v, self.has_w, self.has_last = has_v, has_w, has_last

            def after(self, what):
                return self.use + self.plan.index(what) + 1

        def steps(eng, opening, step):
            def in_order(u, par, pair):
                return Step(u, par, pair, N_OPEN + N_STEP * u, N_OPEN + (N_STEP - N_OUT) * u,
                            FULL_STEP, True, True, not (isinstance(u, int) and u == 0))
            opening()
            for u in range(PEELED):
                step(in_order(u, u % 2, u // 2))
            with eng.Fori(PEELED // 2, LOOP_END // 2) as pair:
                for par in range(2):
                    step(in_order(pair * 2 + par, par, pair))
            use = N_OPEN + N_STEP * LOOP_END
            hi = N_OPEN + (N_STEP - N_OUT) * LOOP_END
            step(Step(NT - 2, 0, NT // 2 - 1, use, hi, NO_XT_STEP, True, False, True))
            step(Step(NT - 1, 1, NT // 2 - 1, use + len(NO_XT_STEP), hi + len(NO_XT_STEP) - N_OUT,
                      LAST_STEP, False, False, True))
        ALL_USES = N_OPEN + N_STEP * LOOP_END + len(NO_XT_STEP) + len(LAST_STEP)

        block = ctx.enter_context(nc.Block())

        def load_k(sp, b):
            for h in range(4):
                r = slice(HD * h, HD * h + HD)
                sp.dma_start(kbd[r, :, :, KEYS * h:KEYS * (h + 1)].rearrange("p s g n -> p (s g) n").bitcast(F32),
                             k_dram[r, :, :, bass.ds(b * KEYS, KEYS)].rearrange("p s g n -> p (s g) n")
                             ).then_inc(k_loaded, 16)

        def load_v(sp, b):
            src = v_dram.rearrange("b p s n -> (b p) s n")[bass.ds(b * KEYS, KEYS)].rearrange(
                "p s (g j h c) -> p (s g) j h c", g=KC, j=2, h=2)
            for h in range(2):
                for j in range(2):
                    at = j * 2 * HD + h * HD
                    sp.dma_start(vbd[KEYS * h:KEYS * (h + 1), :, :, j, at:at + HD].rearrange(
                        "p s g c -> p (s g) c").bitcast(F32), src[:, :, j, h, :]).then_inc(v_loaded, 16)

        @block.sync
        def _(sp):
            sp.dma_start(x[:, 0], xv[0]).then_inc(x_loaded[0], 16)
            sp.dma_start(res[:, 0], wq.rearrange("(k p) n -> p k n", p=P)).then_inc(w_in[0], 16)
            sp.dma_start(x[:, 1], xv[1]).then_inc(x_loaded[1], 16)
            sp.dma_start(gate_in[:, :], gates.to_broadcast([P, 4])).then_inc(small_in, 16)
            sp.dma_start(bias_q[:, :], bq).then_inc(small_in, 16)
            if final:
                for r in range(3):
                    sp.dma_start(rows[:, r, :], row_dram[r:r + 1, :].to_broadcast([P, D])).then_inc(small_in, 16)
            sp.dma_start(res[:, 1], wo.rearrange("(k p) n -> p k n", p=P)).then_inc(w_in[1], 16)
            sp.wait_ge(cleared, 2)
            load_k(sp, 0)
            load_v(sp, 0)
            for t in range(2):
                sp.wait_ge(w_ready, t + 1)
                sp.dma_start(res[:, t], xv[t]).then_inc(res_loaded[t], 16)

            def step(s):
                if s.has_w:
                    sp.wait_ge(full, s.use - 8)
                    sp.dma_start(x[:, s.par], xv[s.u + 2]).then_inc(x_loaded[s.par], 16)
                if not (isinstance(s.u, int) and s.u < 2):
                    sp.wait_ge(stored, 16 * (s.u - 1))
                    sp.dma_start(res[:, s.par], xv[s.u]).then_inc(res_loaded[s.par], 16)
                if s.has_last:
                    if final:
                        sp.wait_ge(out_ready, SUB * s.u)
                    else:
                        sp.wait_ge(free, s.use)
                    sp.dma_start(ov[s.u - 1], res[:, 1 - s.par]).then_inc(stored, 16)
                if s.has_v and s.par == 1:
                    sp.wait_ge(full, s.after((PV, 3)))
                    load_v(sp, s.pair + 1)

                if s.has_w and s.par == 0:
                    sp.wait_ge(score_full, SUB * (s.u + 2))
                    load_k(sp, s.pair + 1)

            steps(sp, lambda: None, step)
            for i in range(SUB):
                if final:
                    sp.wait_ge(out_ready, SUB * (NT - 1) + i + 1)
                else:
                    sp.wait_ge(free, ALL_USES - SUB + i + 1)
                sp.dma_start(ov[NT - 1, :, i], res[:, (NT - 1) % 2, i]).then_inc(stored, 16)
            sp.wait_ge(stored, 16 * (NT - 1 + SUB))

        @block.gpsimd
        def _(pool):
            pool.memset(kbd[:].bitcast(F32), 0.0).then_inc(cleared, 1)
            pool.memset(vbd[:].bitcast(F32), 0.0).then_inc(cleared, 1)
            diagonal(pool, ident, made)
            pool.memset(mask[:, :], 0.0).then_inc(made, 1)
            pool.wait_ge(made, 3)
            pool.affine_select(out=mask[:, :], in_=mask[:, :], compare_op=ALU.is_ge, fill=NEG / SCALE,
                               base=0, pattern=[[-1, KEYS]], channel_multiplier=1).then_inc(made, 1)
            for m, value in ((minus_half, -0.5), (eps, EPS), (zero, 0.0)):
                pool.memset(m[:, :], value).then_inc(made, 1)
            pool.wait_ge(made, 7)

            def normalise(v, par, i):
                pool.wait_ge(inv_done, SUB * v + i + 1)
                pool.tensor_tensor(prob[:, par, i], prob[:, par, i],
                                   inv[:, i, :].unsqueeze(2).to_broadcast([P, HEADS, KEYS]),
                                   ALU.mult).then_inc(prob_ready, 1)

            def norm_rstd(t):
                pool.wait_ge(norm_chain, (SUB + 1) * (t + 1))
                pool.tensor_tensor(rstd[:, :], mean_var[:, :, 1], eps[:, :], ALU.add).then_inc(rstd_done, 1)
                pool.wait_ge(rstd_done, 2 * t + 1)
                pool.tensor_tensor(rstd[:, :], rstd[:, :], minus_half[:, :], ALU.pow).then_inc(rstd_done, 1)

            def last_norm_scale(t):
                pool.wait_ge(f_chain, (SUB + 1) * (t + 1))
                if not (isinstance(t, int) and t == 0):
                    pool.wait_ge(f_normed, SUB * t)

                def then(ins, k):
                    ins.then_inc(f_done, 1)
                    pool.wait_ge(f_done, 8 * t + k)
                then(pool.tensor_tensor(f_var[:, :], f_mv[:, :, 1], eps[:, :], ALU.add), 1)
                then(pool.tensor_tensor(f_rstd[:, :], f_var[:, :], minus_half[:, :], ALU.pow), 2)
                then(pool.tensor_tensor(f_var[:, :], f_mv[:, :, 1], f_rstd[:, :], ALU.mult), 3)
                then(pool.tensor_tensor(f_var[:, :], f_var[:, :], f_rstd[:, :], ALU.mult), 4)
                then(pool.tensor_tensor(f_var[:, :], f_var[:, :], eps[:, :], ALU.add), 5)
                then(pool.tensor_tensor(f_rstd2[:, :], f_var[:, :], minus_half[:, :], ALU.pow), 6)
                then(pool.tensor_tensor(f_scale[:, :], f_rstd2[:, :], f_rstd[:, :], ALU.mult), 7)
                then(pool.tensor_tensor(f_shift[:, :], f_mv[:, :, 0], f_scale[:, :], ALU.mult), 8)
                pool.tensor_tensor(f_shift[:, :], zero[:, :], f_shift[:, :], ALU.subtract).then_inc(f_ready, 1)

            def last_norm_affine(t):
                pool.wait_ge(f_normed, SUB * (t + 1))
                for r, op in ((1, ALU.mult), (2, ALU.add)):
                    if r == 2:
                        pool.wait_ge(f_scaled, 2 * t + 1)
                    pool.tensor_tensor(normed[:], normed[:],
                                       rows[:, r, :].unsqueeze(1).to_broadcast([P, SUB, D]),
                                       op).then_inc(f_scaled, 1)

            def opening():
                norm_rstd(0)
                norm_rstd(1)
                for i in range(SUB):
                    normalise(0, 0, i)
                if final:
                    pool.wait_ge(rows_done, 3)

            def step(s):
                if final and s.has_last:
                    last_norm_scale(s.u - 1)
                if s.has_w:
                    norm_rstd(s.u + 2)
                if final:
                    pool.wait_ge(res_loaded[s.par], 16 * (s.pair + 1))
                    pool.tensor_tensor(res[:, s.par], res[:, s.par],
                                       rows[:, 0, :].unsqueeze(1).to_broadcast([P, SUB, D]),
                                       ALU.add).then_inc(res_biased, 1)
                    if s.has_last:
                        last_norm_affine(s.u - 1)
                        pool.wait_ge(f_scaled, 2 * s.u)
                        pool.tensor_tensor(res[:, 1 - s.par], res[:, 1 - s.par], normed[:],
                                           ALU.add).then_inc(out_ready, SUB)
                for i in range(SUB):
                    if s.has_v:
                        normalise(s.u + 1, 1 - s.par, i)

            steps(pool, opening, step)
            if final:
                last_norm_scale(NT - 1)

        @block.scalar
        def _(act):
            def weights_hi(m, w):
                act.wait_ge(w_in[m], 16)
                act.activation(w[:, 0], res[:, m], ACT.Copy).then_inc(w_hi, 1)

            def norm(t, par, groups=range(SUB)):
                for i in groups:
                    if i == 0:
                        act.wait_ge(norm_ready, t + 1)
                    act.activation(x[:, par, i], x[:, par, i], ACT.Identity, bias=shift[:, i:i + 1],
                                   scale=rstd[:, i:i + 1]).then_inc(normed_x, 1)

            def exponent(v, par, i):
                act.wait_ge(score_free, SUB * v + i + 1)
                act.activation(prob[:, par, i], prob[:, par, i], ACT.Exp, scale=SCALE).then_inc(exp_done, 1)

            def last_norm(t, par, i):
                if i == 0:
                    act.wait_ge(f_ready, t + 1)
                    if not (isinstance(t, int) and t == 0):
                        act.wait_ge(out_ready, SUB * t)
                act.activation(normed[:, i], res[:, par, i], ACT.Identity,
                               bias=f_shift[:, i:i + 1], scale=f_scale[:, i:i + 1]).then_inc(f_normed, 1)

            def hi_half(kind, a, use, k):
                act.wait_ge(full, use + k + 1)
                src = bank[k % 4][:, :]
                if kind == QT:
                    ins = act.activation(qt[:, 0, a], src, ACT.Identity, bias=bias_q[:, a:a + 1])
                else:
                    dst = {XT: xt[:, 0, a % KC], TURN: prob_t[:, a % 4, 0], PV: heads_t[:, 0, a % KC]}[kind]
                    ins = act.activation(dst, src, ACT.Copy)
                ins.then_inc(hi_done, 1)

            def opening():
                weights_hi(0, wq_hl)
                norm(0, 0)
                for k, (kind, a) in enumerate(OPENING):
                    if k == 4:
                        norm(1, 1)
                        act.wait_ge(small_in, 32 + 48 * final)
                    hi_half(kind, a, 0, k)
                act.activation(gate[:, :], gate_in[:, :], ACT.Tanh).then_inc(gate_done, 1)
                weights_hi(1, wo_hl)
                for i in range(SUB):
                    exponent(0, 0, i)

            def step(s):
                for k, (kind, a) in enumerate(s.plan):
                    if s.has_v and (kind, a) in EXPONENT:
                        exponent(s.u + 1, 1 - s.par, EXPONENT[kind, a])
                    if final and s.has_last and (kind, a) in LAST_NORM:
                        last_norm(s.u - 1, 1 - s.par, LAST_NORM[kind, a])
                    if s.has_w and (kind, a) in NORM:
                        norm(s.u + 2, s.par, [NORM[kind, a]])
                    if kind != OUT:
                        hi_half(kind, a, s.use, k)
                if s.has_v:
                    exponent(s.u + 1, 1 - s.par, SUB - 1)

            steps(act, opening, step)
            if final:
                for i in range(SUB):
                    last_norm(NT - 1, (NT - 1) % 2, i)

        @block.vector
        def _(dve):
            def weights_lo(m, w):
                dve.wait_ge(w_hi, m + 1)
                dve.tensor_tensor(w[:, 1], res[:, m], w[:, 0].bitcast(F32), ALU.subtract).then_inc(w_ready, 1)

            def norm_stats(t, par, loads):
                for i in range(SUB):
                    group_stats(t, par, loads, i)
                norm_mean(t)

            def group_stats(t, par, loads, i):
                if i == 0:
                    dve.wait_ge(x_loaded[par], 16 * loads)
                    if not (isinstance(t, int) and t == 0):
                        dve.wait_ge(normed_x, SUB * t)
                dve.bn_stats(stats[:, i, :], x[:, par, i, :]).then_inc(norm_chain, 1)

            def norm_mean(t):
                dve.wait_ge(norm_chain, (SUB + 1) * t + SUB)
                dve.tensor_copy(waited[:, :], stats[:, 0, 0:1])
                for i in range(SUB):
                    last = dve.bn_aggr(mean_var[:, i, :], stats[:, i, :])
                last.then_inc(norm_chain, 1)

            def norm_shift(t):
                dve.wait_ge(rstd_done, 2 * t + 2)
                dve.scalar_tensor_tensor(out=shift[:, :], in0=mean_var[:, :, 0], scalar=-1.0,
                                         in1=rstd[:, :], op0=ALU.mult, op1=ALU.mult).then_inc(norm_ready, 1)

            def softmax_shift(v, par, pair, i):
                dve.wait_ge(score_full, SUB * v + i + 1)
                raw = score_bank[i % 2][:, :].rearrange("p (h s) -> p h s", h=HEADS)
                if layer == 0 and par == 0 and i == 0:
                    dve.tensor_tensor(prob[:, par, i], raw, mask[:, :].unsqueeze(1).to_broadcast([P, HEADS, KEYS]),
                                      ALU.add).then_inc(masked, 1)
                    dve.wait_ge(masked, pair + 1)
                    raw = prob[:, par, i]
                dve.tensor_reduce(top[:, i, :], raw, AX.X, ALU.max).then_inc(maxed, 1)
                dve.wait_ge(maxed, SUB * v + i + 1)
                dve.tensor_tensor(prob[:, par, i], raw, top[:, i, :].unsqueeze(2).to_broadcast([P, HEADS, KEYS]),
                                  ALU.subtract).then_inc(score_free, 1)

            def softmax_sum(v, par, i):
                dve.wait_ge(exp_done, SUB * v + i + 1)
                dve.tensor_reduce(mass[:, i, :], prob[:, par, i], AX.X, ALU.add).then_inc(summed, 1)
                dve.wait_ge(summed, SUB * v + i + 1)
                if not (isinstance(v, int) and v == 0):
                    dve.wait_ge(prob_ready, SUB * v + i - 3)
                dve.reciprocal(inv[:, i, :], mass[:, i, :]).then_inc(inv_done, 1)

            def lo_half(kind, a, k, hi_count):
                dve.wait_ge(hi_done, hi_count)
                src = bank[k % 4][:, :]
                if kind == QT:
                    ins = dve.scalar_tensor_tensor(out=qt[:, 1, a], in0=src, scalar=bias_q[:, a:a + 1],
                                                   in1=qt[:, 0, a].bitcast(F32), op0=ALU.add, op1=ALU.subtract)
                else:
                    hi, lo = {XT: (xt[:, 0, a % KC], xt[:, 1, a % KC]),
                              PV: (heads_t[:, 0, a % KC], heads_t[:, 1, a % KC]),
                              TURN: (prob_t[:, a % 4, 0], prob_t[:, a % 4, 1])}[kind]
                    ins = dve.tensor_tensor(lo, src, hi.bitcast(F32), ALU.subtract)
                ins.then_inc(free, 1)

            def residual(s, i, k):
                if i == 0:
                    dve.wait_ge(res_loaded[s.par], 16 * (s.pair + 1))
                    if final:
                        dve.wait_ge(res_biased, s.u + 1)
                dve.wait_ge(full, s.use + k + 1)
                dve.scalar_tensor_tensor(out=res[:, s.par, i], in0=bank[k % 4][:, :], scalar=gate[:, layer:layer + 1],
                                         in1=res[:, s.par, i], op0=ALU.mult, op1=ALU.add).then_inc(free, 1)

            def last_stats(s, i):
                if i == 0 and s.has_last:
                    dve.wait_ge(f_ready, s.u)
                dve.wait_ge(free, s.after((OUT, i)))
                dve.bn_stats(f_stats[:, i, :], res[:, s.par, i, :]).then_inc(f_chain, 1)

            def last_mean(s):
                dve.wait_ge(f_chain, (SUB + 1) * s.u + SUB)
                dve.tensor_copy(f_waited[:, :], f_stats[:, 0, 0:1])
                for i in range(SUB):
                    last = dve.bn_aggr(f_mv[:, i, :], f_stats[:, i, :])
                last.then_inc(f_chain, 1)

            def last_output(i):
                at, before = normed[:, i], 2 * (NT - 1) + 2 * i
                dve.wait_ge(f_normed, SUB * (NT - 1) + i + 1)
                dve.tensor_tensor(at, at, rows[:, 1, :], ALU.mult).then_inc(f_scaled, 1)
                dve.wait_ge(f_scaled, before + 1)
                dve.tensor_tensor(at, at, rows[:, 2, :], ALU.add).then_inc(f_scaled, 1)
                dve.wait_ge(f_scaled, before + 2)
                dve.tensor_tensor(res[:, (NT - 1) % 2, i], res[:, (NT - 1) % 2, i], at, ALU.add).then_inc(out_ready, 1)

            def opening():
                norm_stats(0, 0, 1)
                weights_lo(0, wq_hl)
                norm_shift(0)
                norm_stats(1, 1, 1)
                for k, (kind, a) in enumerate(OPENING):
                    if k == 4:
                        norm_shift(1)
                        dve.wait_ge(small_in, 32 + 48 * final)
                    lo_half(kind, a, k, k + 1)
                dve.wait_ge(made, 4)
                softmax_shift(0, 0, 0, 0)
                for i in range(1, SUB):
                    softmax_shift(0, 0, 0, i)
                    softmax_sum(0, 0, i - 1)
                softmax_sum(0, 0, SUB - 1)
                weights_lo(1, wo_hl)
                dve.wait_ge(gate_done, 1)
                if final:
                    for r, by in enumerate((1, 3, 3)):
                        dve.tensor_scalar(rows[:, r, :], rows[:, r, :], gate[:, by:by + 1], None,
                                          ALU.mult).then_inc(rows_done, 1)

            def step(s):
                v_par, hi = 1 - s.par, s.hi
                for k, (kind, a) in enumerate(s.plan):
                    if s.has_v and (kind, a) in SCORES:
                        softmax_shift(s.u + 1, v_par, s.pair + s.par, SCORES[kind, a])
                    if kind == OUT:
                        residual(s, a, k)
                    else:
                        hi = hi + 1
                        lo_half(kind, a, k, hi)
                    if s.has_w and (kind, a) == (TURN, 5):
                        norm_shift(s.u + 2)
                    if s.has_v and (kind, a) in SUM:
                        softmax_sum(s.u + 1, v_par, SUM[kind, a])
                    if s.has_w and (kind, a) in STATS:
                        group_stats(s.u + 2, s.par, s.pair + 2, STATS[kind, a])
                    if s.has_w and (kind, a) == (TURN, 3):
                        norm_mean(s.u + 2)
                    if final and kind == OUT and a > 0:
                        last_stats(s, a - 1)
                if s.has_v:
                    softmax_sum(s.u + 1, v_par, SUB - 1)
                if final:
                    last_stats(s, SUB - 1)
                    last_mean(s)

            steps(dve, opening, step)
            if final:
                for i in range(SUB):
                    last_output(i)

        @block.tensor
        def _(pe):
            pe.wait_ge(made, 2)

            def turn_x(par, k, at):
                for i in range(SUB):
                    mm = pe.transpose(bank[at % 4][:, i * P:(i + 1) * P], x[:, par, i, k * P:(k + 1) * P], ident[:, :])
                return mm

            def query(m, at):
                for k in range(KC):
                    mm = product3(pe, bank[at % 4][:, :], [wq_hl[:, h, k, m * P:(m + 1) * P] for h in range(2)],
                                  [xt[:, h, k] for h in range(2)], k == 0, k == KC - 1)
                return mm

            def scores(v, par, i, after_first):
                if after_first:
                    pe.wait_ge(score_free, SUB * v + i - 1)
                if i == 0 and par == 0:
                    pe.wait_ge(k_loaded, 32 * v + 64)
                for g in range(KC):
                    mm = product3(pe, score_bank[i % 2][:, g * 4 * KEYS:(g + 1) * 4 * KEYS],
                                  [qt[:, h, g, i * P:(i + 1) * P] for h in range(2)],
                                  [kbd[:, h, g] for h in range(2)], True, True)
                mm.then_inc(score_full, 1)

            def opening():
                for k, (kind, a) in enumerate(OPENING):
                    t = int(k >= 8)
                    if (kind, a) == (XT, 0):
                        pe.wait_ge(normed_x, SUB * (t + 1))
                    if (kind, a) == (QT, 0):
                        pe.wait_ge(w_ready, 1)
                        pe.wait_ge(free, 4)
                    elif k >= 4:
                        pe.wait_ge(free, k - 3)
                    mm = turn_x(t, a, k) if kind == XT else query(a, k)
                    mm.then_inc(full, 1)
                pe.wait_ge(free, 8)
                for i in range(SUB):
                    scores(0, 0, i, i >= 2)

            def step(s):
                for k, (kind, a) in enumerate(s.plan):
                    if (kind, a) == (QT, 0):
                        pe.wait_ge(free, N_OPEN if isinstance(s.u, int) and s.u == 0 else s.use - 4)
                    before = PRODUCED if final and s.has_w else SCORES
                    if s.has_v and (kind, a) in before:
                        if before[kind, a] == 0:
                            pe.wait_ge(free, s.after((QT, 3)))
                        scores(s.u + 1, 1 - s.par, before[kind, a], True)
                    if (kind, a) == (TURN, 0):
                        pe.wait_ge(prob_ready, SUB * (s.u + 1))
                        if s.par == 0:
                            pe.wait_ge(v_loaded, 32 * s.u + 64)
                    pe.wait_ge(free, s.use + k - 3)
                    if kind == TURN:
                        for i in range(SUB):
                            mm = pe.transpose(bank[k % 4][:, i * P:(i + 1) * P],
                                              prob[:, s.par, i, 2 * a:2 * a + 2, :].rearrange("p h s -> p (h s)"),
                                              ident[:, :])
                    elif kind == PV:
                        pe.wait_ge(free, s.after((TURN, 2 * a + 1)))
                        for j in range(2):
                            mm = product3(pe, bank[k % 4][:, :], [vbd[:, h, a, j] for h in range(2)],
                                          [prob_t[:, (2 * a + j) % 4, h] for h in range(2)], j == 0, j == 1)
                    elif kind == XT:
                        if a == 0:
                            pe.wait_ge(normed_x, SUB * (s.u + 3))
                        mm = turn_x(s.par, a, k)
                    elif kind == OUT:
                        if isinstance(s.u, int) and (s.u, a) == (0, 0):
                            pe.wait_ge(w_ready, 2)
                        if a == 0:
                            pe.wait_ge(free, s.after((PV, 3)))
                        for g in range(KC):
                            mm = product3(pe, bank[k % 4][:, :],
                                          [heads_t[:, h, g, a * P:(a + 1) * P] for h in range(2)],
                                          [wo_hl[:, h, g] for h in range(2)], g == 0, g == KC - 1)
                    else:
                        mm = query(a, k)
                    mm.then_inc(full, 1)

            steps(pe, opening, step)


def mlp(nc, routed, x_in, res_in, x_out, w_all, gates, gate_w, bias_rows, order, experts, starts, fallback):
    tiles = NT + 1 if routed else NT
    xv = x_in[0:TOK, :].rearrange("(t s p) d -> t p s d", s=SUB, p=P)
    rv = res_in[0:TOK, :].rearrange("(t s p) d -> t p s d", s=SUB, p=P)
    ov = x_out[0:TOK, :].rearrange("(t s p) d -> t p s d", s=SUB, p=P)
    with ExitStack() as ctx:
        sb, ps, sem = allocators(nc, ctx, "mr_" if routed else "ms_")
        RING = 4 if routed else 2
        stage = sb("stage", [P, RING, WCOL])
        w_hl = sb("w", [P, 2, CH, 2 * D], F32R)
        b1 = sb("b1", [P, CH])
        x = sb("x", [P, SUB, D])
        xt = sb("xt", [P, 2, KC, TILE], F32R)
        hidden = sb("hidden", [P, 2, TILE])
        h_hl = sb("h", [P, 2, 2, TILE], F32R)
        res = sb("res", [P, SUB, D])
        ident = sb("ident", [P, P])
        minus_half, eps, zero = (sb(n, [P, SUB]) for n in ("minus_half", "eps", "zero"))
        gate_in = sb("gate_in", [P, 4])
        gate = sb("gate", [P, 4])
        stats = sb("stats", [P, SUB, 6])
        waited = sb("waited", [P, 1])
        mean_var = sb("mean_var", [P, SUB, 2])
        rstd = sb("rstd", [P, SUB])
        shift = sb("shift", [P, SUB])
        if routed:
            x_list = sb("x_list", [P, SUB], I32)
            res_list = sb("res_list", [P, SUB], I32)
            fall = sb("fall", [P, D])
            carrier = sb("carrier", [P, 2 + 3 * SUB])
        else:
            gate_rows = sb("gate_rows", [P, 2, D])
            product = sb("product", [P, D])
            score = sb("score", [P, SUB, 2])
            is_second = sb("is_second", [P, GROUPS])
            other = sb("other", [P, 4, D + 1])
            relu_b1 = sb("relu_b1", [P, 4])
            fall_sum = sb("fall_sum", [P, 2, D])
            bias3 = sb("bias3", [3, D])
            upto = sb("upto", [P, P])
            ones = sb("ones", [P, P])
            totals, before, rank, token_f, spot, zeros = (
                sb(n, [P, GROUPS]) for n in ("totals", "before", "rank", "token_f", "spot", "zeros"))
            token, place = sb("token", [P, GROUPS], I32), sb("place", [P, GROUPS], I32)
            first_half = sb("first_half", [1, NT], I32)
            expert_i, start_i = (sb(n, [1, NT + 1], I32) for n in ("expert_i", "start_i"))
            first_f, middle, expert_f, start_f, seconds = (
                sb(n, [1, k]) for n, k in (("first_f", NT), ("middle", NT), ("expert_f", NT + 1),
                                           ("start_f", NT + 1), ("seconds", 1)))
            (order_made, counted, chain, scattered, facts_out, first_scored, fall_w_in, fall_relu,
             fall_terms, fall_full, fall_row) = (
                sem(n) for n in ("order_made", "counted", "chain", "scattered", "facts_out",
                                 "first_scored", "fall_w_in", "fall_relu",
                                 "fall_terms", "fall_full", "fall_row"))
            PLACED, PLANNED = 10, 20
        hid_bank = [ps(f"hid{i}") for i in range(2)]
        turn_bank = [ps(f"turn{i}") for i in range(2)]
        out_bank = [ps(f"out{i}") for i in range(SUB)]
        (small_in, made, gate_done, x_loaded, res_loaded, stored, norm_chain, rstd_done, norm_ready,
         normed_x, turn_full, turn_hi, turn_free, w_split, w_ready, hid_full, hid_hi, hid_ready, piece_done,
         out_ready, fall_in, fall_added, x_list_in, res_list_in, scored, chosen) = (
            sem(n) for n in (
                "small_in", "made", "gate_done", "x_loaded", "res_loaded", "stored", "norm_chain",
                "rstd_done", "norm_ready", "normed_x", "turn_full", "turn_hi", "turn_free", "w_split",
                "w_ready", "hid_full", "hid_hi", "hid_ready", "piece_done", "out_ready",
                "fall_in", "fall_added", "x_list_in", "res_list_in", "scored", "chosen"))
        w_in = [sem(f"w_in{r}") for r in range(RING)]
        AHEAD = 3
        LOADS = 64 if routed else 16
        block = ctx.enter_context(nc.Block())

        def tiles_loop(eng, body):
            end = NT - 1
            body(0, True)
            with eng.Fori(1, end) as s:
                body(s, True)
            for s in range(end, tiles):
                body(s, s + 1 < tiles)

        def loads_until(t):
            return LOADS * t + LOADS * groups(t) // SUB

        def groups(t):
            return HALF // P if isinstance(t, int) and t == NT else SUB

        def tile_start(sp, t):
            return sp.value_load(starts[0:1, bass.ds(t, 1)], min_val=0, max_val=(LIST - groups(t) * P) // HALF)

        def list_rows(start, t):
            return order[bass.ds(start * HALF, groups(t) * P), :].rearrange("(p g) o -> p (g o)", p=P)

        @block.sync
        def _(sp):
            if not routed:
                sp.dma_start(x[:], xv[0]).then_inc(x_loaded, 16)
                for e in range(2):
                    sp.dma_start(gate_rows[:, e, :], gate_w[e:e + 1, :].to_broadcast([P, D])).then_inc(small_in, 16)
            else:
                start = tile_start(sp, 0)
                sp.dma_start(x_list[:, :], list_rows(start, 0)).then_inc(x_list_in, 16)
            sp.dma_start(gate_in[:, :], gates.to_broadcast([P, 4])).then_inc(small_in, 16)

            def weights(s, which, lists=None):
                for j in range(CH):
                    if not (isinstance(s, int) and CH * s + j < RING):
                        sp.wait_ge(w_ready, CH * s + j - RING + 1)
                    sp.dma_start(stage[:, j % RING, :], which[j]).then_inc(w_in[j % RING], 16)
                    if routed and isinstance(s, int) and (s, j) == (0, 0):
                        sp.wait_ge(x_loaded, 64)
                    if lists and j == 2 * RING:
                        lists()

            if routed:
                def body(s, more):
                    e = sp.value_load(experts[0:1, bass.ds(s, 1)], min_val=0, max_val=1)
                    rows = list_rows(tile_start(sp, s), s)
                    if more:
                        next_rows = list_rows(tile_start(sp, s + 1), s + 1)

                    def lists():
                        if not (isinstance(s, int) and s == 0):
                            sp.wait_ge(stored, 64 * s)
                        sp.dma_start(res_list[:, 0:groups(s)], rows).then_inc(res_list_in, 16)
                        sp.dma_start(fall[:, :], fallback[e]).then_inc(fall_in, 16)
                        if more:
                            sp.wait_ge(x_loaded, 64 * (s + 1))
                            sp.dma_start(x_list[:, 0:groups(s + 1)], next_rows).then_inc(x_list_in, 16)
                    weights(s, w_all[e + 1], lists)
                tiles_loop(sp, body)
            else:
                sp.dma_start(bias3[:, :], bias_rows).then_inc(small_in, 16)

                def loads(s, more):
                    if not (isinstance(s, int) and s == 0):
                        sp.wait_ge(stored, 16 * s)
                    sp.dma_start(res[:], rv[s]).then_inc(res_loaded, 16)
                    if not (isinstance(s, int) and s == 0):
                        sp.wait_ge(fall_terms, 4 * s)
                    for n in range(4):
                        sp.dma_start(other[:, n, :], w_pieces[n % 2][s, n // 2]).then_inc(fall_w_in, 16)
                    if more:
                        sp.wait_ge(turn_full, KC * (s + 1))
                        sp.wait_ge(scored, SUB * (s + 1))
                        sp.dma_start(x[:], xv[s + 1]).then_inc(x_loaded, 16)
                w_pieces = [w_all[1 + e].rearrange("(s n) p c -> s n p c", n=2)[:, :, :, D:WCOL] for e in range(2)]

                def body(s, more):
                    if isinstance(s, int) and s == 0:
                        weights(0, w_all[0], lambda: loads(0, True))
                    else:
                        loads(s, more)
                    if not more:
                        sp.wait_ge(chain, PLANNED)
                        sp.dma_start(experts, expert_i[:, :]).then_inc(facts_out, 16)
                        sp.dma_start(starts, start_i[:, :]).then_inc(facts_out, 16)
                        for e in range(2):
                            sp.wait_ge(fall_row, e + 1)
                            sp.dma_start(fallback[e], fall_sum[:, e, :]).then_inc(facts_out, 16)
                    sp.wait_ge(out_ready, SUB * (s + 1))
                    sp.dma_start(ov[s], res[:]).then_inc(stored, 16)
                tiles_loop(sp, body)
                sp.wait_ge(stored, 16 * tiles)
                sp.wait_ge(scattered, 16 * GROUPS)
                sp.wait_ge(facts_out, 64)

        @block.gpsimd
        def _(pool):
            diagonal(pool, ident, made)
            for m, value in ((minus_half, -0.5), (eps, EPS), (zero, 0.0)):
                pool.memset(m[:, :], value).then_inc(made, 1)
            pool.wait_ge(made, 5)

            def gather(dst, lists, lists_in, table, loaded, s):
                pool.wait_ge(lists_in, 16 * (s + 1))
                at = 0 if dst is x else 1
                pool.tensor_tensor(carrier[:, at:at + 1], zero[:, 0:1], zero[:, 0:1], ALU.add)
                for g in range(groups(s)):
                    pool.indirect_dma_start(
                        out=dst[:, g, :], out_offset=None, in_=table,
                        in_offset=bass.IndirectOffsetOnAxis(ap=lists[:, g:g + 1], axis=0)).then_inc(loaded, 16)

            def scatter(s, g, at):
                pool.wait_ge(out_ready, SUB * s + g + 1)
                pool.tensor_tensor(carrier[:, at:at + 1], zero[:, 0:1], zero[:, 0:1], ALU.add)
                pool.indirect_dma_start(
                    out=x_out, out_offset=bass.IndirectOffsetOnAxis(ap=res_list[:, g:g + 1], axis=0),
                    in_=res[:, g, :], in_offset=None).then_inc(stored, 16)

            def norm_rstd(t):
                pool.wait_ge(norm_chain, 2 * t + 2)
                pool.tensor_tensor(rstd[:, :], mean_var[:, :, 1], eps[:, :], ALU.add).then_inc(rstd_done, 1)
                pool.wait_ge(rstd_done, 2 * t + 1)
                pool.tensor_tensor(rstd[:, :], rstd[:, :], minus_half[:, :], ALU.pow).then_inc(rstd_done, 1)

            def split(s, j):
                pool.wait_ge(w_split, CH * s + j + 1)
                pool.tensor_tensor(b1[:, j:j + 1], stage[:, j % RING, 2 * D:WCOL], zero[:, 0:1], ALU.add)
                pool.tensor_tensor(w_hl[:, 1, j], stage[:, j % RING, 0:2 * D], w_hl[:, 0, j].bitcast(F32),
                                   ALU.subtract).then_inc(w_ready, 1)

            if routed:
                gather(x, x_list, x_list_in, x_in, x_loaded, 0)
            else:
                pool.memset(fall_sum[:], 0.0).then_inc(order_made, 1)
                pool.memset(upto[:, :], 1.0).then_inc(order_made, 1)
                pool.memset(ones[:, :], 1.0).then_inc(order_made, 1)
                pool.memset(zeros[:, :], 0.0).then_inc(order_made, 1)
                pool.iota(token[:, :], pattern=[[P, GROUPS]], base=0, channel_multiplier=1).then_inc(order_made, 1)
                pool.iota(first_half[:, :], pattern=[[TILE // HALF, NT]], base=0,
                          channel_multiplier=0).then_inc(order_made, 1)
                pool.wait_ge(order_made, 2)
                pool.affine_select(out=upto[:, :], in_=upto[:, :], compare_op=ALU.is_ge, fill=0.0,
                                   base=0, pattern=[[1, P]], channel_multiplier=-1).then_inc(order_made, 1)
            norm_rstd(0)
            for j in range(AHEAD):
                split(0, j)

            def body(s, more):
                first = isinstance(s, int) and s == 0
                for j in range(CH):
                    if j + AHEAD < CH:
                        if routed or first:
                            split(s, j + AHEAD)
                    elif routed and more:
                        split(s + 1, j + AHEAD - CH)
                    if routed and j < SUB and not first:
                        scatter(s - 1, j, (2 if more else 2 + SUB) + j)
                    if routed and j == 5 and more:
                        pool.wait_ge(turn_full, KC * (s + 1))
                        gather(x, x_list, x_list_in, x_in, x_loaded, s + 1)
                    if routed and j == 6:
                        if not first:
                            pool.wait_ge(stored, 64 * s)
                        gather(res, res_list, res_list_in, res_in, res_loaded, s)
                    if more and j == 9:
                        norm_rstd(s + 1)
                if not routed and not more:
                    pool.wait_ge(chain, PLACED)
                    for g in range(GROUPS):
                        pool.indirect_dma_start(
                            out=order, out_offset=bass.IndirectOffsetOnAxis(ap=place[:, g:g + 1], axis=0),
                            in_=token[:, g:g + 1], in_offset=None).then_inc(scattered, 16)
            tiles_loop(pool, body)
            if routed:
                for g in range(groups(tiles - 1)):
                    scatter(tiles - 1, g, 2 + 2 * SUB + g)
                pool.wait_ge(stored, 16 * (LIST // P))

        @block.scalar
        def _(act):
            def norm(t):
                act.wait_ge(norm_ready, t + 1)
                for i in range(groups(t)):
                    act.activation(x[:, i], x[:, i], ACT.Identity, bias=shift[:, i:i + 1],
                                   scale=rstd[:, i:i + 1]).then_inc(normed_x, 1)

            def turn_halves(t):
                for k in range(KC):
                    act.wait_ge(turn_full, KC * t + k + 1)
                    n = groups(t) * P
                    act.activation(xt[:, 0, k, 0:n], turn_bank[k % 2][:, 0:n], ACT.Copy).then_inc(turn_hi, 1)

            def split(s, j):
                act.wait_ge(w_in[j % RING], 16 * (CH // RING * s + j // RING + 1))
                if not (isinstance(s, int) and s == 0):
                    act.wait_ge(piece_done, CH * s + j - CH + 1)
                act.activation(w_hl[:, 0, j], stage[:, j % RING, 0:2 * D], ACT.Copy).then_inc(w_split, 1)

            def split_ahead(s, j, more):
                if j + AHEAD < CH:
                    if routed or (isinstance(s, int) and s == 0):
                        split(s, j + AHEAD)
                elif routed and more:
                    split(s + 1, j + AHEAD - CH)

            split(0, 0)
            norm(0)
            act.wait_ge(small_in, 16 if routed else 64)
            act.activation(gate[:, :], gate_in[:, :], ACT.Tanh).then_inc(gate_done, 1)
            split(0, 1)
            turn_halves(0)
            split(0, 2)

            def body(s, more):
                n = groups(s) * P
                for j in range(CH):
                    split_ahead(s, j, more)
                    if j == 11 and more:
                        norm(s + 1)
                    act.wait_ge(hid_full, CH * s + j + 1)
                    if not (isinstance(s, int) and CH * s + j < 2):
                        act.wait_ge(piece_done, CH * s + j - 1)
                    for dst in (hidden[:, j % 2, 0:n], h_hl[:, j % 2, 0, 0:n]):
                        last = act.activation(dst, hid_bank[j % 2][:, 0:n], ACT.Relu, bias=b1[:, j:j + 1])
                    last.then_inc(hid_hi, 1)
                if more:
                    turn_halves(s + 1)
            tiles_loop(act, body)

        @block.vector
        def _(dve):
            def norm_stats(t):
                dve.wait_ge(x_loaded, loads_until(t))
                if not (isinstance(t, int) and t == 0):
                    dve.wait_ge(normed_x, SUB * t)
                for i in range(groups(t)):
                    last = dve.bn_stats(stats[:, i, :], x[:, i, :])
                last.then_inc(norm_chain, 1)
                dve.wait_ge(norm_chain, 2 * t + 1)
                dve.tensor_copy(waited[:, :], stats[:, 0, 0:1])
                for i in range(groups(t)):
                    last = dve.bn_aggr(mean_var[:, i, :], stats[:, i, :])
                last.then_inc(norm_chain, 1)

            def norm_shift(t):
                dve.wait_ge(rstd_done, 2 * t + 2)
                dve.scalar_tensor_tensor(out=shift[:, :], in0=mean_var[:, :, 0], scalar=-1.0,
                                         in1=rstd[:, :], op0=ALU.mult, op1=ALU.mult).then_inc(norm_ready, 1)

            def gate_scores(t):
                dve.wait_ge(normed_x, SUB * (t + 1))
                for i in range(SUB):
                    for e in range(2):
                        done = (first_scored, scored)[e]
                        dve.tensor_tensor_reduce(product[:, :], x[:, i, :], gate_rows[:, e, :], 1.0, 0.0,
                                                 ALU.mult, ALU.add, score[:, i, e:e + 1]).then_inc(done, 1)
                        dve.wait_ge(done, SUB * t + i + 1)
                dve.tensor_tensor(is_second[:, bass.ds(t * SUB, SUB)], score[:, :, 1], score[:, :, 0],
                                  ALU.is_gt).then_inc(chosen, 1)

            def turn_los(t):
                for k in range(KC):
                    dve.wait_ge(turn_hi, KC * t + k + 1)
                    n = groups(t) * P
                    dve.tensor_tensor(xt[:, 1, k, 0:n], turn_bank[k % 2][:, 0:n], xt[:, 0, k, 0:n].bitcast(F32),
                                      ALU.subtract).then_inc(turn_free, 1)

            def fall_term(s, n):
                if n == 0:
                    dve.wait_ge(fall_w_in, 64 * (s + 1))
                    if not (isinstance(s, int) and s == 0):
                        dve.wait_ge(fall_terms, 4 * s)
                    dve.tensor_scalar(relu_b1[:, :], other[:, :, D], 0.0, None, ALU.max).then_inc(fall_relu, 1)
                    dve.wait_ge(fall_relu, s + 1)
                if not (isinstance(s, int) and s == 0 and n < 2):
                    dve.wait_ge(fall_terms, 4 * s + n - 1)
                at = fall_sum[:, n % 2, :]
                dve.scalar_tensor_tensor(out=at, in0=other[:, n, 0:D], scalar=relu_b1[:, n:n + 1], in1=at,
                                         op0=ALU.mult, op1=ALU.add).then_inc(fall_terms, 1)

            def fall_rows():
                for e in range(2):
                    dve.wait_ge(fall_full, e + 1)
                    dve.tensor_scalar(fall_sum[:, e, :], turn_bank[e][:, :], gate[:, 2:3], None,
                                      ALU.mult).then_inc(fall_row, 1)

            def places():
                done = [0]

                def link(ins):
                    done[0] += 1
                    ins.then_inc(chain, 1)
                    dve.wait_ge(chain, done[0])
                dve.wait_ge(counted, 2)
                link(dve.tensor_copy(totals[:, :], turn_bank[1][:, 0:GROUPS]))
                link(dve.tensor_tensor_scan(before[:, :], totals[:, :], zeros[:, :], 0.0, ALU.add, ALU.add))
                link(dve.tensor_tensor(rank[:, :], before[:, :], totals[:, :], ALU.subtract))
                link(dve.tensor_tensor(rank[:, :], turn_bank[0][:, 0:GROUPS], rank[:, :], ALU.add))
                link(dve.tensor_copy(token_f[:, :], token[:, :]))
                link(dve.tensor_scalar(spot[:, :], token_f[:, :], -1.0, float(LIST), ALU.mult, ALU.add))
                link(dve.tensor_tensor(spot[:, :], spot[:, :], is_second[:, :], ALU.mult))
                link(dve.tensor_tensor(spot[:, :], spot[:, :], token_f[:, :], ALU.add))
                link(dve.tensor_tensor(spot[:, :], spot[:, :], rank[:, :], ALU.subtract))
                link(dve.tensor_copy(place[:, :], spot[:, :]))
                of_second = before[0:1, GROUPS - 1:GROUPS]
                link(dve.tensor_copy(first_f[:, :], first_half[:, :]))
                link(dve.tensor_scalar(middle[:, :], first_f[:, :], float(HALF), float(HALF), ALU.mult, ALU.add))
                link(dve.tensor_scalar(expert_f[:, 0:NT], middle[:, :], of_second, float(TOK), ALU.add, ALU.is_ge))
                link(dve.tensor_tensor(start_f[:, 0:NT], expert_f[:, 0:NT], first_f[:, :], ALU.add))
                link(dve.tensor_reduce(seconds[:, :], expert_f[:, 0:NT], AX.X, ALU.add))
                link(dve.tensor_scalar(start_f[:, NT:NT + 1], seconds[:, :], -2.0, 2.0 * NT, ALU.mult, ALU.add))
                link(dve.tensor_scalar(middle[:, 0:1], start_f[:, NT:NT + 1], float(HALF), None, ALU.mult))
                link(dve.tensor_scalar(expert_f[:, NT:NT + 1], middle[:, 0:1], of_second, float(TOK),
                                       ALU.add, ALU.is_ge))
                link(dve.tensor_copy(start_i[:, :], start_f[:, :]))
                link(dve.tensor_copy(expert_i[:, :], expert_f[:, :]))

            norm_stats(0)
            norm_shift(0)
            dve.wait_ge(gate_done, 1)
            turn_los(0)
            if not routed:
                gate_scores(0)
                dve.wait_ge(order_made, 7)

            def body(s, more):
                n = groups(s) * P
                for j in range(CH):
                    if more and j == 8:
                        norm_stats(s + 1)
                    if more and j == 10:
                        norm_shift(s + 1)
                    if more and j == 13 and not routed:
                        gate_scores(s + 1)
                    dve.wait_ge(hid_hi, CH * s + j + 1)
                    dve.tensor_tensor(h_hl[:, j % 2, 1, 0:n], hidden[:, j % 2, 0:n],
                                      h_hl[:, j % 2, 0, 0:n].bitcast(F32), ALU.subtract).then_inc(hid_ready, 1)
                    if not routed and j in (4, 5, 6, 7):
                        fall_term(s, j - 4)
                    if not routed and not more and j == 2:
                        places()
                    if not routed and not more and j == 10:
                        fall_rows()
                    if routed and j == 10:
                        dve.wait_ge(fall_in, 16 * (s + 1))
                        dve.wait_ge(res_loaded, loads_until(s))
                        rows = res[:, 0:groups(s)]
                        dve.tensor_tensor(rows, rows, fall[:, :].unsqueeze(1).to_broadcast([P, groups(s), D]),
                                          ALU.add).then_inc(fall_added, 1)
                if more:
                    turn_los(s + 1)
                if routed:
                    dve.wait_ge(fall_added, s + 1)
                else:
                    dve.wait_ge(res_loaded, LOADS * (s + 1))
                dve.wait_ge(piece_done, CH * (s + 1))
                for i in range(groups(s)):
                    dve.scalar_tensor_tensor(out=res[:, i], in0=out_bank[i][:, :], scalar=gate[:, 2:3],
                                             in1=res[:, i], op0=ALU.mult, op1=ALU.add).then_inc(out_ready, 1)
            tiles_loop(dve, body)

        @block.tensor
        def _(pe):
            pe.wait_ge(made, 2)
            if not routed:
                pe.wait_ge(order_made, 7)

            def turn(t, ks=range(KC)):
                if ks[0] == 0:
                    pe.wait_ge(normed_x, SUB * t + groups(t))
                for k in ks:
                    if not (isinstance(t, int) and KC * t + k < 2):
                        pe.wait_ge(turn_free, KC * t + k - 1)
                    for i in range(groups(t)):
                        mm = pe.transpose(turn_bank[k % 2][:, i * P:(i + 1) * P], x[:, i, k * P:(k + 1) * P],
                                          ident[:, :])
                    mm.then_inc(turn_full, 1)

            def up(s, j):
                pe.wait_ge(w_ready, CH * s + j + 1 if routed else j + 1)
                if not (isinstance(s, int) and CH * s + j < 2):
                    pe.wait_ge(hid_ready, CH * s + j - 1)
                if j == 0:
                    pe.wait_ge(turn_free, KC * (s + 1))
                for k in range(KC):
                    n = groups(s) * P
                    mm = product3(pe, hid_bank[j % 2][:, 0:n], [w_hl[:, h, j, k * P:(k + 1) * P] for h in range(2)],
                                  [xt[:, h, k, 0:n] for h in range(2)], k == 0, k == KC - 1)
                mm.then_inc(hid_full, 1)

            def down(s, j):
                pe.wait_ge(hid_ready, CH * s + j + 1)
                if j == 0 and not (isinstance(s, int) and s == 0):
                    pe.wait_ge(out_ready, SUB * s)
                for i in range(groups(s)):
                    mm = product3(pe, out_bank[i][:, :], [h_hl[:, j % 2, h, i * P:(i + 1) * P] for h in range(2)],
                                  [w_hl[:, h, j, D:2 * D] for h in range(2)], j == 0, j == CH - 1)
                mm.then_inc(piece_done, 1)

            turn(0)

            def body(s, more):
                up(s, 0)
                for j in range(CH):
                    if j + 1 < CH:
                        up(s, j + 1)
                    if j == CH - 2 and more:
                        turn(s + 1, (0, 1))
                    if j == CH - 1 and more:
                        turn(s + 1, (2, 3))
                    if not routed and not more and j == 1:
                        pe.wait_ge(chosen, NT)
                        pe.wait_ge(turn_free, KC * NT)
                        for b, m in enumerate((upto, ones)):
                            pe.matmul(turn_bank[b][:, 0:GROUPS], m[:, :], is_second[:, :],
                                      start=True, stop=True).then_inc(counted, 1)
                    if not routed and not more and j == 9:
                        pe.wait_ge(fall_terms, 4 * NT)
                        pe.wait_ge(chain, PLACED)
                        for e in range(2):
                            pe.matmul(turn_bank[e][:, :], ones[:, :], fall_sum[:, 1 - e, :], start=True, stop=False)
                            mm = pe.matmul(turn_bank[e][:, :], ones[0:3, :], bias3[:, :], start=False, stop=True)
                        mm.then_inc(fall_full, 2)
                    down(s, j)
            tiles_loop(pe, body)


def program(nc, x, ctx_t, gates, wq, wk, wv, wo, bq, bk, bv, rows1, gate_w, w_all, mlp_rows, out):
    def dram(name, shape, dt=F32):
        return nc.dram_tensor(name, shape, dt, kind="Internal").ap()
    k_dram = dram("k_dram", (2, P, 2, KC, BATCH * KEYS))
    v_dram = dram("v_dram", (2, 2, P, 2, D))
    x1 = dram("x1", (LIST, D))
    x1s = dram("x1s", (LIST, D))
    x2 = dram("x2", (LIST, D))
    order = dram("order", (LIST, 1), I32)
    experts = dram("experts", (1, NT + 1), I32)
    starts = dram("starts", (1, NT + 1), I32)
    fallback = dram("fallback", (2, P, D))
    context(nc, ctx_t, wk, wv, bk, bv, k_dram, v_dram, order, [x1[TOK:LIST, :], x1s[TOK:LIST, :]])
    attention(nc, 0, x, x1, wq[0], wo[0], bq[0], gates, k_dram[0], v_dram[0], None)
    mlp(nc, False, x1, x1, x1s, w_all, gates, gate_w, mlp_rows, order, experts, starts, fallback)
    mlp(nc, True, x1, x1s, x2, w_all, gates, None, None, order, experts, starts, fallback)
    attention(nc, 1, x2, out, wq[1], wo[1], bq[1], gates, k_dram[1], v_dram[1], rows1)


def kernel(**inputs):
    import numpy as np
    import concourse.bacc as bacc
    from concourse.bass_utils import run_bass_kernel_spmd

    def merged(w):
        return w.transpose(1, 0, 2).reshape(D, D)

    def columns(b):
        return b.reshape(KC, P).T
    i = {k: np.asarray(v) for k, v in inputs.items()}
    none = np.zeros(D, np.float32)
    w1 = np.stack([i["L0_ffn_sw1"], *i["L0_ffn_w1"]])
    w2 = np.stack([i["L0_ffn_sw2"], *i["L0_ffn_w2"]])
    b1 = np.stack([i["L0_ffn_sb1"], *i["L0_ffn_b1"]])
    w_all = np.concatenate([
        w1.reshape(3, KC, P, CH, P).transpose(0, 3, 2, 1, 4).reshape(3, CH, P, D),
        w2.reshape(3, CH, P, D), b1.reshape(3, CH, P, 1)], axis=3)
    arrays = {
        "x": i["x"].reshape(TOK, D),
        "ctx_t": i["ctx_1024"].transpose(2, 0, 1).reshape(D, BATCH * KEYS),
        "gates": np.concatenate([i["g_xattn"], i["g_ffn"]]).reshape(1, 4),
        "wq": np.stack([i["L0_xattn_Wq"].T, merged(i["L1_xattn_Wq"])]),
        "wk": np.stack([i["L0_xattn_Wk"].T, merged(i["L1_xattn_Wk"])]),
        "wv": np.stack([i["L0_xattn_Wv"].T, merged(i["L1_xattn_Wv"])]),
        "wo": np.stack([i["L0_xattn_Wo"].T, i["L1_xattn_Wo"]]),
        "bq": np.stack([columns(none), columns(i["L1_xattn_bq"].reshape(D))]),
        "bk": np.stack([columns(none), columns(i["L1_xattn_bk"].reshape(D))]),
        "bv": np.stack([none, i["L1_xattn_bv"].reshape(D)]).reshape(2, 1, D),
        "rows1": np.stack([i["L1_xattn_bo"], i["L1_ffn_ln_g"], i["L1_ffn_ln_b"]]),
        "gate_w": i["L0_ffn_gate_w"],
        "w_all": w_all,
        "mlp_rows": np.stack([i["L0_ffn_sb2"], *i["L0_ffn_b2"]]),
    }
    arrays = {k: np.ascontiguousarray(v) for k, v in arrays.items()}
    nc = bacc.Bacc("TRN2", target_bir_lowering=False, num_devices=1)
    args = {k: nc.dram_tensor(k, v.shape, mybir.dt.from_np(v.dtype), kind="ExternalInput").ap()
            for k, v in arrays.items()}
    out = nc.dram_tensor("out", (TOK, D), F32, kind="ExternalOutput").ap()
    program(nc, **args, out=out)
    r = run_bass_kernel_spmd(nc, [arrays], core_ids=[0])
    return r.results[0]["out"].reshape(BATCH, SEQ, D)
```
